# Optimizing a Trainium2 kernel written in Bass

```python
import numpy as np
import jax
import jax.numpy as jnp

def _softmax(x, axis=-1):
    return jax.nn.softmax(x, axis=axis)

def _gelu(x):
    return jax.nn.gelu(x, approximate=True)

def _silu(x):
    return jax.nn.silu(x)

def _sigmoid(x):
    return jax.nn.sigmoid(x)

def _layernorm(x, axis=-1, eps=1e-05):
    m = jnp.mean(x, axis=axis, keepdims=True)
    v = jnp.var(x, axis=axis, keepdims=True)
    return (x - m) / jnp.sqrt(v + eps)

def _scatter_add(tgt, idx, src, axis=0):
    return tgt.at[idx].add(src)

def _segment_sum(src, seg, n):
    return jax.ops.segment_sum(src, seg, n)
kernel_name = 'mk_adaln_d1_jaxref_r4_b65933'

def setup_inputs(seed: int=0):
    np.random.seed(seed)
    _w = jnp.asarray

    def _L0_attn_setup():
        import jax, jax.numpy as jnp
        import numpy as np
        import math
        B, T, C = (2, 512, 512)
        N_HEAD = 16
        N_KV = 4
        GROUP = N_HEAD // N_KV
        HS = C // N_HEAD
        WINDOW = 256
        SINK = 4

        def _sliding_window_sink_mask(t):
            i = jnp.arange(t)[:, None]
            j = jnp.arange(t)[None, :]
            causal = j <= i
            band = j >= i - (WINDOW - 1)
            mask = causal & band
            mask = mask | (j < SINK)
            mask = mask & ((i >= SINK) | causal)
            return mask
        key = jax.random.key(seed)
        ks = jax.random.split(key, 5)
        s = 1.0 / math.sqrt(C)
        return {'x': jax.random.normal(ks[0], (B, T, C), dtype=jnp.float32), 'Wq': jax.random.normal(ks[1], (C, C), dtype=jnp.float32) * s, 'Wk': jax.random.normal(ks[2], (N_KV * HS, C), dtype=jnp.float32) * s, 'Wv': jax.random.normal(ks[3], (N_KV * HS, C), dtype=jnp.float32) * s, 'Wo': jax.random.normal(ks[4], (C, C), dtype=jnp.float32) * s}
    _L0_attn_in = _L0_attn_setup()

    def _L0_ffn_setup():
        import jax, jax.numpy as jnp
        import numpy as np
        B, T, D = (2, 256, 512)
        E, F, K = (64, 128, 4)
        S, HS = (2, 128 * 4)
        key = jax.random.key(seed)
        ks = jax.random.split(key, 9)
        s = 0.02
        f32 = jnp.float32
        return {'x': jax.random.normal(ks[0], (B, T, D), f32), 'router_w': jax.random.normal(ks[1], (D, E), f32) * s, 'router_bias': jnp.zeros((E,), f32), 'wg': jax.random.normal(ks[2], (E, D, F), f32) * s, 'wu': jax.random.normal(ks[3], (E, D, F), f32) * s, 'wd': jax.random.normal(ks[4], (E, F, D), f32) * s, 'swg': jax.random.normal(ks[5], (S, D, HS), f32) * s, 'swu': jax.random.normal(ks[6], (S, D, HS), f32) * s, 'swd': jax.random.normal(ks[7], (S, HS, D), f32) * s}
    _L0_ffn_in = _L0_ffn_setup()
    _L0_c = _w((lambda *s: np.random.randn(*s).astype(np.float32) * 0.05)(1, 512))
    _L0_wmod = _w((lambda *s: np.random.randn(*s).astype(np.float32) * 0.05)(512, 6 * 512) * 512 ** (-0.5))
    _d = {'L0_attn_x': _L0_attn_in['x'], 'L0_attn_Wq': _L0_attn_in['Wq'], 'L0_attn_Wk': _L0_attn_in['Wk'], 'L0_attn_Wv': _L0_attn_in['Wv'], 'L0_attn_Wo': _L0_attn_in['Wo'], 'L0_ffn_router_w': _L0_ffn_in['router_w'], 'L0_ffn_router_bias': _L0_ffn_in['router_bias'], 'L0_ffn_wg': _L0_ffn_in['wg'], 'L0_ffn_wu': _L0_ffn_in['wu'], 'L0_ffn_wd': _L0_ffn_in['wd'], 'L0_ffn_swg': _L0_ffn_in['swg'], 'L0_ffn_swu': _L0_ffn_in['swu'], 'L0_ffn_swd': _L0_ffn_in['swd'], 'L0_c': _L0_c, 'L0_wmod': _L0_wmod}
    _x0 = _d['L0_attn_x']
    _d['L0_attn_x'] = jax.random.normal(jax.random.fold_in(jax.random.key(seed), 1), (1, 2048, 512), dtype=_x0.dtype)
    del _x0
    return _d

def reference(L0_attn_x, L0_attn_Wq, L0_attn_Wk, L0_attn_Wv, L0_attn_Wo, L0_ffn_router_w, L0_ffn_router_bias, L0_ffn_wg, L0_ffn_wu, L0_ffn_wd, L0_ffn_swg, L0_ffn_swu, L0_ffn_swd, L0_c, L0_wmod):

    def _L0_attn_ref(x, Wq, Wk, Wv, Wo):
        import jax, jax.numpy as jnp
        import numpy as np
        import math
        B, T, C = (2, 512, 512)
        N_HEAD = 16
        N_KV = 4
        GROUP = N_HEAD // N_KV
        HS = C // N_HEAD
        WINDOW = 256
        SINK = 4

        def _sliding_window_sink_mask(t):
            i = jnp.arange(t)[:, None]
            j = jnp.arange(t)[None, :]
            causal = j <= i
            band = j >= i - (WINDOW - 1)
            mask = causal & band
            mask = mask | (j < SINK)
            mask = mask & ((i >= SINK) | causal)
            return mask
        b, t, c = x.shape
        q = (x @ Wq.T).reshape(b, t, N_HEAD, HS).transpose(0, 2, 1, 3)
        q = q.reshape(b, N_KV, GROUP, t, HS)
        k = (x @ Wk.T).reshape(b, t, N_KV, HS).transpose(0, 2, 1, 3)
        v = (x @ Wv.T).reshape(b, t, N_KV, HS).transpose(0, 2, 1, 3)
        scale = 1.0 / math.sqrt(HS)
        att = jnp.einsum('bkgqd,bkjd->bkgqj', q, k) * scale
        mask = _sliding_window_sink_mask(t)
        att = jnp.where(mask[None, None, None, :, :], att, -jnp.inf)
        att = jax.nn.softmax(att, axis=-1)
        y = jnp.einsum('bkgqj,bkjd->bkgqd', att, v)
        y = y.reshape(b, N_HEAD, t, HS).transpose(0, 2, 1, 3).reshape(b, t, c)
        return y @ Wo.T

    def _L0_ffn_ref(x, router_w, router_bias, wg, wu, wd, swg, swu, swd):
        import jax, jax.numpy as jnp
        import numpy as np
        B, T, D = (2, 256, 512)
        E, F, K = (64, 128, 4)
        S, HS = (2, 128 * 4)
        b, t, d = x.shape
        flat = x.reshape(b * t, d)
        n = flat.shape[0]
        logits = flat @ router_w
        scores = jax.nn.softmax(logits, axis=-1)
        _, topk_idx = jax.lax.top_k(logits + router_bias, K)
        topk_scores = jnp.take_along_axis(scores, topk_idx, axis=-1)
        topk_scores = topk_scores / topk_scores.sum(axis=-1, keepdims=True)
        comb = jnp.zeros((n, E), dtype=flat.dtype).at[jnp.arange(n)[:, None], topk_idx].set(topk_scores)
        g = jax.nn.silu(jnp.einsum('nd,edf->nef', flat, wg))
        u = jnp.einsum('nd,edf->nef', flat, wu)
        routed = jnp.einsum('ne,nef,efd->nd', comb, g * u, wd)
        sg = jax.nn.silu(jnp.einsum('nd,sdh->nsh', flat, swg))
        su = jnp.einsum('nd,sdh->nsh', flat, swu)
        shared = jnp.einsum('nsh,shd->nd', sg * su, swd)
        return (routed + shared).reshape(b, t, d)
    x = L0_attn_x
    mod = (_silu(L0_c) @ L0_wmod).reshape(L0_c.shape[0], 6, 1, -1)
    sa, ca, ga, sb, cb, gb = (mod[:, 0], mod[:, 1], mod[:, 2], mod[:, 3], mod[:, 4], mod[:, 5])
    ga = (2 * (ga >= 0) - 1) * jnp.maximum(jnp.abs(ga), 0.25)
    gb = (2 * (gb >= 0) - 1) * jnp.maximum(jnp.abs(gb), 0.25)
    h = _layernorm(x, axis=-1) * (1 + ca) + sa
    x = x + ga * _L0_attn_ref(h, L0_attn_Wq, L0_attn_Wk, L0_attn_Wv, L0_attn_Wo)
    h = _layernorm(x, axis=-1) * (1 + cb) + sb
    x = x + gb * _L0_ffn_ref(h, L0_ffn_router_w, L0_ffn_router_bias, L0_ffn_wg, L0_ffn_wu, L0_ffn_wd, L0_ffn_swg, L0_ffn_swu, L0_ffn_swd)
    return x

_drawn_inputs = setup_inputs


def setup_inputs(seed=0):
    import zlib

    import numpy as np

    out = dict(_drawn_inputs(seed))
    spreads = {'L0_ffn_router_bias': (0.0, 0.8)}
    factors = {'L0_ffn_router_w': 8.0,
     'L0_ffn_wg': 8.0,
     'L0_ffn_wu': 8.0,
     'L0_ffn_wd': 8.0,
     'L0_ffn_swg': 3.323,
     'L0_ffn_swu': 3.259,
     'L0_ffn_swd': 3.254}
    for name, (base, spread) in spreads.items():
        noise = np.random.default_rng([zlib.crc32(name.encode()), seed]).standard_normal(out[name].shape)
        drawn = base * np.exp(spread * noise) if base else spread * noise
        out[name] = jnp.asarray(drawn.astype(out[name].dtype))
    for name, factor in factors.items():
        out[name] = (out[name] * factor).astype(out[name].dtype)
    return out
```

```python
from contextlib import ExitStack

import concourse.bass as bass
from concourse import mybir

F32 = mybir.dt.float32
BF16 = mybir.dt.bfloat16
I32 = mybir.dt.int32
U32 = mybir.dt.uint32
ALU = mybir.AluOpType
ACT = mybir.ActivationFunctionType
AX = mybir.AxisListType

P = 128
T, C = 2048, 512
NT = T // P
KC = C // P
HS, NH, NKV = 32, 16, 4
HPG = NH // NKV
SINK = 4
WT = 3
E, F, TOPK = 64, 128, 4
SH, HC = 2, 4
MAXT = 128
SLOTS = MAXT * P
EPS = 1e-5
NEG = -1e30
SCALE = HS ** -0.5
KW = WT * P
SW = KW + SINK


class Chain:

    def __init__(self, eng, sem, base=0):
        self.eng, self.sem, self.base, self.n = eng, sem, base, 0

    def step(self, ins):
        ins.then_inc(self.sem, 1)
        self.n += 1

    def last(self):
        self.eng.wait_ge(self.sem, self.base + self.n)


def hold(eng, g):
    eng.sem_inc(g["s_held"][eng.engine.name], 1)


def rsqrt(dve, ch, out, var, tmp):
    v, t = tmp
    ch.step(dve.tensor_scalar(v, var, EPS, None, ALU.add))
    ch.last()
    ch.step(dve.tensor_scalar(t.bitcast(I32), v.bitcast(I32), 1, None, ALU.arith_shift_right))
    ch.last()
    ch.step(dve.tensor_scalar(out.bitcast(I32), t.bitcast(I32), -1.0, float(0x5F3759DF), ALU.mult, ALU.add))
    for _ in range(3):
        ch.last()
        ch.step(dve.tensor_tensor(t, out, out, ALU.mult))
        ch.last()
        ch.step(dve.tensor_tensor(t, t, v, ALU.mult))
        ch.last()
        ch.step(dve.tensor_scalar(t, t, -0.5, 1.5, ALU.mult, ALU.add))
        ch.last()
        ch.step(dve.tensor_tensor(out, out, t, ALU.mult))
    ch.last()


RSQRT_STEPS = 15


def build_kernel(nc, x, Wq, Wk, Wv, Wo, router_w, router_bias, wg, wu, wd, swg, swu, swd, cvec, wmod, out):
    stack = ExitStack()
    with stack:
        def sb(name, shape, dt=F32, ctx=stack):
            return ctx.enter_context(nc.sbuf_tensor(name, shape, dt))

        def ps(name, shape, dt=F32, ctx=stack):
            return ctx.enter_context(nc.psum_tensor(name, shape, dt))

        def sem(name):
            return stack.enter_context(nc.semaphore(name))

        x_t = x.rearrange("b (t p) c -> p (b t) c", p=P)
        out_t = out.rearrange("b (t p) c -> p (b t) c", p=P)
        h2_rows = nc.dram_tensor("h2_rows", [NT, P, C], F32, kind="Internal").ap()
        h2t_cols = nc.dram_tensor("h2t_cols", [NT, P, KC, P], F32, kind="Internal").ap()
        slot_x = nc.dram_tensor("slot_x", [SLOTS, C], F32, kind="Internal").ap()
        slot_y = nc.dram_tensor("slot_y", [SLOTS, C], F32, kind="Internal").ap()

        X = sb("X", [P, NT, C])
        ident = sb("ident", [P, P])
        ones = sb("ones", [P, P])
        ga_row = sb("ga_row", [P, C])
        gb_row = sb("gb_row", [P, C])
        cb1_row = sb("cb1_row", [P, C])
        sb_row = sb("sb_row", [P, C])
        LG = sb("LG", [P, NT, E])
        EIDX = sb("EIDX", [P, NT, 8])
        GATE = sb("GATE", [P, NT, TOPK])
        POSI = sb("POSI", [P, NT, TOPK], I32)

        tile_expert = nc.dram_tensor("tile_expert", [1, P], I32, kind="Internal").ap()
        eid_row = sb("eid_row", [1, P], I32)
        s_tile_expert = sem("s_tile_expert")
        s_held = {"DVE": sem("s_held_dve"), "Pool": sem("s_held_pool")}
        s_ident = sem("s_ident")
        s_in = [sem(f"s_in{i}") for i in range(10)]
        s_zero = sem("s_zero")
        s_slots_zeroed = sem("s_slots_zeroed")

        attn = ExitStack()
        with attn:
            A = lambda name, shape, dt=F32: sb(name, shape, dt, attn)
            WoT = A("WoT", [P, KC, C])
            V = A("V", [P, NT, P])
            Q4 = A("Q4", [P, NH, T], BF16)
            K4 = A("K4", [P, NKV, T], BF16)
            rw = A("rw", [P, KC, E])
            rbias = A("rbias", [P, E])

            with ExitStack() as pro:
                prologue(nc, pro, sb, ps, sem, locals())
            with ExitStack() as mid:
                attention(nc, mid, sb, ps, sem, locals())
        with ExitStack() as tail:
            dispatch(nc, tail, sb, ps, sem, locals())
        with ExitStack() as tail:
            shared_experts(nc, tail, sb, ps, sem, locals())
        with ExitStack() as tail:
            routed_experts(nc, tail, sb, ps, sem, locals())
        with ExitStack() as tail:
            combine(nc, tail, sb, ps, sem, locals())


def prologue(nc, ctx, sb, ps, sem, g):
    X, V, Q4, K4, WoT = (g[k] for k in ("X", "V", "Q4", "K4", "WoT"))
    ident, ones = g["ident"], g["ones"]
    s_in = g["s_in"]
    B = lambda name, shape, dt=F32: sb(name, shape, dt, ctx)
    QT = B("QT", [P, 2, NKV, T], BF16)
    KT = B("KT", [P, 2, T], BF16)
    room = Q4[:].rearrange("p h t -> p (h t)").bitcast(F32)
    WqT = room[:, 11264:13312].rearrange("p (k o) -> p k o", k=KC)
    WkvT = room[:, 13312:14336].rearrange("p (s k o) -> p s k o", s=2, k=KC)
    cT = B("cT", [P, KC])
    sc = B("sc", [P, KC])
    scb = room[:, 14336:14848].rearrange("p (k m) -> p k m", k=KC)
    sa_col = B("sa_col", [P, KC])
    ca1_col = B("ca1_col", [P, KC])
    gtmp = room[:, 14848:15872].rearrange("p (s c) -> p s c", s=2)
    stats = B("stats", [P, NT, 6])
    mv = B("mv", [P, NT, 2])
    rstd = B("rstd", [P, NT])
    rt = B("rt", [P, 2, NT])
    xh = room[:, 0:1024].rearrange("p (s c) -> p s c", s=2)
    hT = room[:, 1024:2048].rearrange("p (s k n) -> p s k n", s=2, k=KC)
    s_c, s_sc, s_scb, s_mod, s_modc, s_wt, s_wtc, s_dve = (
        sem(n) for n in ("s_c", "s_sc", "s_scb", "s_mod", "s_modc", "s_wt", "s_wtc", "s_pdve"))
    wmod_v = g["wmod"].rearrange("(p k) n -> p k n", k=KC)
    SECT = 6
    with ExitStack() as w:
        wm = room[:, 0:4096].rearrange("p (k s n) -> p k s n", k=KC, s=2)
        Wqo = room[:, 4096:8192].rearrange("p (s o c) -> p s o c", s=2, o=KC)
        Wkv = room[:, 8192:9216].rearrange("p (s c) -> p s c", s=2)
        zeros = room[:, 9216:11264]
        psW = [ps(f"psW{i}", [P, C], F32, w) for i in range(8)]
        s_wm = [sem(f"s_wm{i}") for i in range(3)]
        with nc.Block() as block:
            @block.sync
            def _(sp):
                sp.dma_start(cT[:], g["cvec"].rearrange("b (p k) -> (b p) k", k=KC)).then_inc(s_c, 16)
                sp.dma_start(wm, wmod_v[:, :, 0:2 * C].rearrange("p k (s n) -> p k s n", s=2)).then_inc(s_wm[0], 16)
                sp.dma_start(Wqo[:, 0], g["Wq"].rearrange("(o p) c -> p o c", p=P)).then_inc(s_in[0], 16)
                sp.dma_start(Wkv[:, 0], g["Wk"]).then_inc(s_in[1], 16)
                sp.dma_start(Wkv[:, 1], g["Wv"]).then_inc(s_in[2], 16)
                for i in range(4):
                    sp.dma_start(X[:, 4 * i:4 * i + 4], g["x_t"][:, 4 * i:4 * i + 4]).then_inc(s_in[3 + i], 16)
                sp.dma_start(Wqo[:, 1], g["Wo"].rearrange("(o p) c -> p o c", p=P)).then_inc(s_in[7], 16)
                sp.dma_start(g["rw"][:], g["router_w"].rearrange("(p k) e -> p k e", k=KC)).then_inc(s_in[8], 16)
                sp.dma_start(g["rbias"][:], g["router_bias"].rearrange("(a e) -> a e", a=1).broadcast_to([P, E])).then_inc(s_in[9], 16)
                for r in range(1, 3):
                    sp.wait_ge(s_mod, 2 * r)
                    sp.dma_start(wm, wmod_v[:, :, 2 * r * C:(2 * r + 2) * C].rearrange("p k (s n) -> p k s n", s=2)).then_inc(s_wm[r], 16)

            @block.gpsimd
            def _(pool):
                pool.memset(ident[:], 0.0).then_inc(g["s_ident"], 1)
                pool.memset(ones[:], 1.0).then_inc(g["s_ident"], 1)
                pool.wait_ge(g["s_ident"], 2)
                pool.affine_select(out=ident[:], in_=ident[:], compare_op=ALU.not_equal, fill=1.0, base=0,
                                   pattern=[[-1, P]], channel_multiplier=1).then_inc(g["s_ident"], 1)
                pool.memset(zeros, 0.0).then_inc(g["s_zero"], 1)
                pool.wait_ge(g["s_zero"], 1)
                slots = g["slot_x"].rearrange("(n p r) c -> n p (r c)", p=P, r=4)
                for n in range(SLOTS // (4 * P)):
                    pool.dma_start(slots[n], zeros).then_inc(g["s_slots_zeroed"], 16)
                pool.wait_ge(g["s_slots_zeroed"], 16 * (SLOTS // (4 * P)))

            @block.scalar
            def _(act):
                act.wait_ge(s_c, 16)
                act.activation(sc[:], cT[:], ACT.Silu).then_inc(s_sc, 1)
                for n in range(10):
                    act.wait_ge(s_wt, n + 1)
                    if n < 4:
                        dst = WqT[:, n]
                    elif n < 6:
                        dst = WkvT[:, n - 4].rearrange("p k o -> p (k o)")
                    else:
                        dst = WoT[:, n - 6]
                    act.activation(dst, psW[n % 4][:], ACT.Copy).then_inc(s_wtc, 1)

            @block.vector
            def _(dve):
                ch = Chain(dve, s_dve)
                dve.wait_ge(s_sc, 1)
                for k in range(KC):
                    dve.tensor_copy(scb[:, k, :], sc[:, k:k + 1].broadcast_to([P, P])).then_inc(s_scb, 1)
                dve.wait_ge(s_mod, 1)
                dve.tensor_copy(sa_col[:], psW[4][:, 0:KC]).then_inc(s_modc, 1)
                dve.wait_ge(s_mod, 2)
                dve.tensor_scalar(ca1_col[:], psW[5][:, 0:KC], 1.0, None, ALU.add).then_inc(s_modc, 1)

                def floored(dst, src, sem_value):
                    dve.wait_ge(s_mod, sem_value)
                    ch.step(dve.tensor_scalar(gtmp[:, 0], src, -1.0, 0.25, ALU.mult, ALU.max))
                    ch.last()
                    ch.step(dve.scalar_tensor_tensor(out=gtmp[:, 0], in0=src, scalar=0.25, in1=gtmp[:, 0],
                                                     op0=ALU.max, op1=ALU.max))
                    ch.step(dve.tensor_scalar(gtmp[:, 1], src, 0.0, 2.0, ALU.is_ge, ALU.mult))
                    ch.last()
                    dve.scalar_tensor_tensor(out=dst, in0=gtmp[:, 1], scalar=-1.0, in1=gtmp[:, 0],
                                             op0=ALU.add, op1=ALU.mult).then_inc(s_modc, 1)
                floored(g["ga_row"][:], psW[6][:], 3)
                dve.wait_ge(s_mod, 4)
                dve.tensor_copy(g["sb_row"][:], psW[7][:]).then_inc(s_modc, 1)
                dve.wait_ge(s_mod, 5)
                dve.tensor_scalar(g["cb1_row"][:], psW[4][:], 1.0, None, ALU.add).then_inc(s_modc, 1)
                dve.wait_ge(s_modc, 3)
                floored(g["gb_row"][:], psW[5][:], 6)

            @block.tensor
            def _(pe):
                def columns(s, bank):
                    for c in range(KC):
                        for k in range(KC):
                            ins = pe.matmul(bank[:, c:c + 1], wm[:, k, s, c::KC], sc[:, k:k + 1],
                                            start=(k == 0), stop=(k == KC - 1))
                    ins.then_inc(s_mod, 1)

                def rows(s, bank):
                    for k in range(KC):
                        ins = pe.matmul(bank[:], scb[:, k, :], wm[:, k, s, :], start=(k == 0), stop=(k == KC - 1))
                    ins.then_inc(s_mod, 1)

                def turn(n, blocks):
                    if n >= 4:
                        pe.wait_ge(s_wtc, n - 3)
                    for j, b in enumerate(blocks):
                        ins = pe.transpose(psW[n % 4][:, j * P:(j + 1) * P], b, ident[:])
                    ins.then_inc(s_wt, 1)

                pe.wait_ge(s_sc, 1)
                pe.wait_ge(s_wm[0], 16)
                columns(0, psW[4])
                columns(1, psW[5])
                pe.wait_ge(g["s_ident"], 3)
                pe.wait_ge(s_in[0], 16)
                for k in range(KC):
                    turn(k, [Wqo[:, 0, o, k::KC] for o in range(KC)])
                pe.wait_ge(s_in[1], 16)
                turn(4, [Wkv[:, 0, k::KC] for k in range(KC)])
                pe.wait_ge(s_in[2], 16)
                turn(5, [Wkv[:, 1, k::KC] for k in range(KC)])
                pe.wait_ge(s_in[7], 16)
                for k in range(KC):
                    turn(6 + k, [Wqo[:, 1, o, k * P:(k + 1) * P] for o in range(KC)])
                pe.wait_ge(s_scb, KC)
                pe.wait_ge(s_wm[1], 16)
                rows(0, psW[6])
                rows(1, psW[7])
                pe.wait_ge(s_wm[2], 16)
                pe.wait_ge(s_modc, 2)
                rows(0, psW[4])
                rows(1, psW[5])

    with ExitStack() as w:
        psT = [ps(f"psT{i}", [P, KC, P], F32, w) for i in range(2)]
        psQ = [ps(f"psQ{i}", [P, KC, P], F32, w) for i in range(2)]
        psK = [ps(f"psK{i}", [P, C], F32, w) for i in range(2)]
        psV = [ps(f"psV{i}", [P, C], F32, w) for i in range(2)]
        s_xh, s_tr, s_hT, s_q, s_k, s_v, s_hi, s_lo, s_vc, s_ln, s_rep = (
            sem(n) for n in ("s_xh", "s_tr", "s_hT", "s_q", "s_k", "s_v", "s_hi", "s_lo", "s_vc", "s_ln", "s_rep"))
        with nc.Block() as block:
            @block.vector
            def _(dve):
                def norm(i, b):
                    dve.tensor_scalar(xh[:, b], X[:, bass.ds(i, 1)].rearrange("p a c -> p (a c)"),
                                      mv[:, bass.ds(i, 1), 0:1].rearrange("p a b -> p (a b)"), rstd[:, bass.ds(i, 1)],
                                      ALU.subtract, ALU.mult).then_inc(s_xh, 1)

                def low_parts(i, b):
                    tok = bass.ds(i * P, P)
                    dve.wait_ge(s_hi, 2 * i + 1)
                    dve.scalar_tensor_tensor(out=QT[:, 1, :, tok], in0=psQ[b][:], scalar=SCALE, in1=QT[:, 0, :, tok],
                                             op0=ALU.mult, op1=ALU.subtract).then_inc(s_lo, 1)
                    dve.wait_ge(s_hi, 2 * i + 2)
                    dve.scalar_tensor_tensor(out=KT[:, 1, tok], in0=psK[b][:, 0:P], scalar=1.0, in1=KT[:, 0, tok],
                                             op0=ALU.mult, op1=ALU.subtract).then_inc(s_lo, 1)

                for i in range(4):
                    dve.wait_ge(s_in[3 + i], 16)
                ch = Chain(dve, s_ln)
                for i in range(NT):
                    ch.step(dve.bn_stats(stats[:, i], X[:, i]))
                ch.last()
                for i in range(NT):
                    ch.step(dve.bn_aggr(mv[:, i], stats[:, i]))
                ch.last()
                rsqrt(dve, ch, rstd[:], mv[:, :, 1:2].rearrange("p t a -> p (t a)"), (rt[:, 0], rt[:, 1]))
                with dve.Fori(0, NT // 2) as h:
                    for b in range(2):
                        i = h * 2 + b
                        dve.wait_ge(s_tr, (i + 0))
                        norm(i, b)
                        low_parts(i, b)

            @block.tensor
            def _(pe):
                with pe.Fori(0, NT // 2) as h:
                    for b in range(2):
                        i = h * 2 + b
                        pe.wait_ge(s_xh, i + 1)
                        for k in range(KC):
                            ins = pe.transpose(psT[b][:, k, :], xh[:, b, k::KC], ident[:])
                        ins.then_inc(s_tr, 1)
                        pe.wait_ge(s_hT, i + 1)
                        pe.wait_ge(s_lo, i * 2)
                        for o in range(KC):
                            for k in range(KC):
                                ins = pe.matmul(psQ[b][:, o, :], WqT[:, k, o * P:(o + 1) * P], hT[:, b, k, :],
                                                start=(k == 0), stop=(k == KC - 1))
                        ins.then_inc(s_q, 1)
                        for k in range(KC):
                            ins = pe.matmul(psK[b][:, 0:P], WkvT[:, 0, k, :], hT[:, b, k, :],
                                            start=(k == 0), stop=(k == KC - 1))
                        ins.then_inc(s_k, 1)
                        pe.wait_ge(s_vc, i + 0)
                        for k in range(KC):
                            ins = pe.matmul(psV[b][:, 0:P], hT[:, b, k, :], WkvT[:, 1, k, :],
                                            start=(k == 0), stop=(k == KC - 1))
                        ins.then_inc(s_v, 1)

            @block.scalar
            def _(act):
                with act.Fori(0, NT // 2) as h:
                    for b in range(2):
                        i = h * 2 + b
                        tok = bass.ds(i * P, P)
                        act.wait_ge(s_tr, i + 1)
                        act.wait_ge(s_v, i + 0)
                        for k in range(KC):
                            ins = act.activation(hT[:, b, k, :], psT[b][:, k, :], ACT.Identity,
                                                 bias=sa_col[:, k:k + 1], scale=ca1_col[:, k:k + 1])
                        ins.then_inc(s_hT, 1)
                        act.wait_ge(s_q, i + 1)
                        act.activation(QT[:, 0, :, tok], psQ[b][:], ACT.Copy, scale=SCALE).then_inc(s_hi, 1)
                        act.wait_ge(s_k, i + 1)
                        act.activation(KT[:, 0, tok], psK[b][:, 0:P], ACT.Copy).then_inc(s_hi, 1)
                        act.wait_ge(s_v, i + 1)
                        act.activation(V[:, bass.ds(i, 1)].rearrange("p a c -> p (a c)"), psV[b][:, 0:P],
                                       ACT.Copy).then_inc(s_vc, 1)

            @block.sync
            def _(sp):
                sp.wait_ge(s_lo, 2 * NT)
                sp.wait_ge(s_v, NT)
                n = 0
                for j in range(HPG):
                    for r in range(4):
                        sp.dma_start(Q4[r * HS:(r + 1) * HS, j::HPG, :], QT[j * HS:(j + 1) * HS, r // 2, :, :]).then_inc(s_rep, 16)
                        sp.dma_start(K4[r * HS:(r + 1) * HS, j, :], KT[j * HS:(j + 1) * HS, r % 2, :]).then_inc(s_rep, 16)
                        n += 32
                sp.wait_ge(s_rep, n)


def attention(nc, ctx, sb, ps, sem, g):
    X, V, Q4, K4, WoT = (g[k] for k in ("X", "V", "Q4", "K4", "WoT"))
    ident, LG = g["ident"], g["LG"]
    B = lambda name, shape, dt=F32: sb(name, shape, dt, ctx)
    mask = B("mask", [P, 4, SW], BF16)
    S = B("S", [P, 2, HPG, SW])
    PT = B("PT", [P, 2, HPG, KW])
    skP = B("skP", [P, 2, HPG * SINK])
    skT = B("skT", [HPG * SINK, P])
    s_skn = sem("a_skn")
    Vs = B("Vs", [HPG * SINK, NKV, P])
    Vc = B("Vc", [P, WT, P])
    yT = B("yT", [P, NKV, P])
    mx = B("mx", [P, 2, HPG])
    nm = B("nm", [P, 2, HPG])
    den = B("den", [P, 2, HPG])
    rden = B("rden", [P, 2, HPG])
    xh = B("xh2", [P, C])
    t1 = B("t1", [P, C])
    stats = B("stats2", [P, 6])
    mv = B("mv2", [P, 2])
    rstd = B("rstd2", [P, 1])
    rt = B("rt2", [P, 2])
    v8 = B("v8", [P, 8])
    i8 = B("i8", [P, 8], U32)
    lgb = B("lgb", [P, E])
    h2t = B("h2t", [P, KC, P])
    s_rproj = sem("a_rproj")
    psS = ps("psS", [P, HPG, C], F32, ctx)
    psT = [ps(f"psTa{i}", [P, C], F32, ctx) for i in range(2)]
    psO = ps("psO", [P, C], F32, ctx)
    psA = ps("psA", [P, C], F32, ctx)
    (s_mask, s_vs, s_vcur, s_scores, s_masked, s_nm, s_exp, s_rden, s_norm, s_pt, s_pta, s_ptd, s_sk, s_skc, s_pv,
     s_y, s_proj, s_x1, s_xh, s_t1, s_h2, s_h2t, s_h2c, s_rl, s_dve) = (sem("a_" + n) for n in (
         "mask", "vs", "vcur", "scores", "masked", "nm", "exp", "rden", "norm", "pt", "pta", "ptd", "sk", "skc",
         "pv", "y", "proj", "x1", "xh", "t1", "h2", "h2t", "h2c", "rl", "dve"))
    s_h2w = sem("a_h2w")
    s_h2tw = sem("a_h2tw")
    U = NKV
    DVE_STEPS = 4 * U + 8

    def shape_of(qt):
        if isinstance(qt, int) and qt < WT:
            return (qt + 1) * P, 0, qt, qt == WT - 1
        return KW, (qt - (WT - 1)) * P, WT, True

    with nc.Block() as block:
        @block.sync
        def _(sp):
            sp.wait_ge(s_vs, 1)
            for j in range(HPG):
                sp.dma_start(Vs[j * SINK:(j + 1) * SINK, :, j * HS:(j + 1) * HS],
                             V[0:SINK, 0, :].rearrange("p (g d) -> p g d", g=NKV)).then_inc(s_vs, 16)

            with sp.Fori(0, NT) as i:
                sp.wait_ge(s_h2, i + 1)
                sp.dma_start(g["h2_rows"][bass.ds(i, 1)].rearrange("a p c -> p (a c)"), t1[:]).then_inc(s_h2w, 16)
                sp.wait_ge(s_h2c, i + 1)
                sp.dma_start(g["h2t_cols"][bass.ds(i, 1)].rearrange("a p k n -> p (a k) n"), h2t[:]).then_inc(s_h2tw, 16)
            sp.wait_ge(s_h2w, 16 * NT)
            sp.wait_ge(s_h2tw, 16 * NT)

        @block.gpsimd
        def _(pool):
            pool.memset(Vs[:], 0.0).then_inc(s_vs, 1)
            pool.memset(mask[:], 0.0).then_inc(s_mask, 1)
            pool.wait_ge(s_mask, 1)

            def keep(m, lo, n, base, step, mult):
                pool.affine_select(out=mask[:, m, lo:lo + n], in_=mask[:, m, lo:lo + n], compare_op=ALU.is_ge,
                                   fill=NEG, base=base, pattern=[[step, n]], channel_multiplier=mult).then_inc(s_mask, 1)
            keep(0, 0, P, 0, -1, 1)
            keep(1, P, P, 0, -1, 1)
            keep(2, 2 * P, P, 0, -1, 1)
            keep(3, 2 * P, P, 0, -1, 1)
            keep(2, 0, P, -1, 1, -1)
            keep(3, 0, P, -1, 1, -1)
            pool.wait_ge(s_mask, 7)
            keep(2, 0, P, -SINK, 1, 0)

            def tile(qt):
                first = isinstance(qt, int) and qt == 0
                W, k0, m, sinks = shape_of(qt)
                n = W // P
                if not first:
                    pool.wait_ge(s_pv, U * qt)
                pool.tensor_copy(Vc[:, 0:n], V[:, bass.ds(qt - (n - 1), n)]).then_inc(s_vcur, 1)
                for u in range(U):
                    pool.wait_ge(s_rden, qt * U + u + 1)
                    if not (isinstance(qt, int) and (qt < WT - 1 or (qt == WT - 1 and u < 2))):
                        pool.wait_ge(s_sk, qt * U + u - 1 - (WT - 1) * U)
                    hold(pool, g)
                    for j in range(HPG):
                        pool.tensor_scalar(S[:, u % 2, j, 0:W], S[:, u % 2, j, 0:W],
                                           rden[:, u % 2, j:j + 1], None, ALU.mult).then_inc(s_norm, 1)
                    if sinks:
                        pool.tensor_tensor(skP[:, u % 2].rearrange("p (j s) -> p j s", j=HPG), S[:, u % 2, :, KW:SW],
                                           rden[:, u % 2].unsqueeze(2).broadcast_to([P, HPG, SINK]), ALU.mult).then_inc(s_skn, 1)
                pool.wait_ge(s_xh, qt + 1)
                if not first:
                    pool.wait_ge(s_h2w, 16 * qt)
                    pool.wait_ge(s_h2t, qt)
                pool.tensor_tensor(xh[:], xh[:], g["cb1_row"][:], ALU.mult).then_inc(s_t1, 1)
                pool.wait_ge(s_t1, qt + 1)
                pool.tensor_tensor(t1[:], xh[:], g["sb_row"][:], ALU.add).then_inc(s_h2, 1)

            for qt in range(WT):
                tile(qt)
            with pool.Fori(WT, NT) as qt:
                tile(qt)

        @block.tensor
        def _(pe):
            def scores(qt, u):
                W, k0, m, sinks = shape_of(qt)
                for j in range(HPG):
                    if not (isinstance(qt, int) and qt == 0 and u == 0):
                        pe.wait_ge(s_masked, (qt * U + u) * HPG + j - (HPG - 1))
                    q = Q4[:, u * HPG + j, bass.ds(qt * P, P)]
                    ins = pe.matmul(psS[:, j, 0:W], q, K4[:, u, bass.ds(k0, W)], start=True, stop=True)
                    if sinks:
                        ins = pe.matmul(psS[:, j, KW:SW], q, K4[:, u, 0:SINK], start=True, stop=True)
                    ins.then_inc(s_scores, 1)

            def values(qt, u):
                W, k0, m, sinks = shape_of(qt)
                n = W // P
                b = u % 2
                first = isinstance(qt, int) and qt == 0
                for j in range(HPG):
                    pe.wait_ge(s_norm, (qt * U + u) * HPG + j + 1)
                    if not (first and u == 0 and j < 2):
                        pe.wait_ge((s_pta, s_ptd)[j % 2], (qt * U + u) * 2 + (1 if j >= 2 else 0))
                    for k in range(n):
                        ins = pe.transpose(psT[j % 2][:, k * P:(k + 1) * P], S[:, b, j, k * P:(k + 1) * P], ident[:])
                    ins.then_inc(s_pt, 1)
                if not (first and u == 0):
                    pe.wait_ge(s_y, qt * U + u)
                if sinks:
                    base = (WT - 1) * U
                    pe.wait_ge(s_skn, qt * U + u + 1 - base)
                    pe.transpose(psO[0:HPG * SINK, P:2 * P], skP[:, b], ident[:]).then_inc(s_sk, 1)
                    pe.wait_ge(s_skc, qt * U + u + 1 - base)
                if u == 0:
                    pe.wait_ge(s_vcur, qt + 1)
                pe.wait_ge(s_pta, (qt * U + u + 1) * 2)
                pe.wait_ge(s_ptd, (qt * U + u + 1) * 2)
                if sinks:
                    if isinstance(qt, int):
                        pe.wait_ge(s_vs, 1 + 16 * HPG)
                    pe.matmul(psO[:, 0:P], Vs[:, u, :], skT[:], start=True, stop=False, skip_group_check=True)
                for k in range(n):
                    for j in range(HPG):
                        ins = pe.matmul(psO[j * HS:(j + 1) * HS, 0:P], Vc[:, k, u * HS:(u + 1) * HS],
                                        PT[:, b, j, k * P:(k + 1) * P], start=(k == 0 and not sinks),
                                        stop=(k == n - 1), skip_group_check=True)
                ins.then_inc(s_pv, 1)

            def tile(qt):
                for u in range(U):
                    scores(qt, u)
                    if u >= 1:
                        values(qt, u - 1)
                values(qt, U - 1)
                pe.wait_ge(s_y, (qt + 1) * U)
                if not (isinstance(qt, int) and qt == 0):
                    pe.wait_ge(s_rl, qt)
                for k in range(NKV):
                    ins = pe.matmul(psA[:], yT[:, k, :], WoT[:, k, :], start=(k == 0), stop=(k == NKV - 1))
                ins.then_inc(s_proj, 1)
                pe.wait_ge(s_h2, qt + 1)
                for k in range(KC):
                    ins = pe.transpose(psA[:, k * P:(k + 1) * P], t1[:, k::KC], ident[:])
                ins.then_inc(s_h2t, 1)
                pe.wait_ge(s_h2c, qt + 1)
                for k in range(KC):
                    ins = pe.matmul(psA[:, 0:E], t2_of(k), g["rw"][:, k, :], start=(k == 0), stop=(k == KC - 1))
                ins.then_inc(s_rproj, 1)

            def t2_of(k):
                return h2t[:, k, :]

            for qt in range(WT):
                tile(qt)
            with pe.Fori(WT, NT) as qt:
                tile(qt)

        @block.scalar
        def _(act):
            def exps(qt, u):
                W, k0, m, sinks = shape_of(qt)
                act.wait_ge(s_nm, qt * U + u + 1)
                w = SW if sinks else W
                for j in range(HPG):
                    act.activation(S[:, u % 2, j, 0:w], S[:, u % 2, j, 0:w], ACT.Exp, bias=nm[:, u % 2, j:j + 1],
                                   accum_out=den[:, u % 2, j:j + 1]).then_inc(s_exp, 1)

            def copies(qt, u):
                W, k0, m, sinks = shape_of(qt)
                first = isinstance(qt, int) and qt == 0
                for j in (0, 2):
                    act.wait_ge(s_pt, (qt * U + u) * HPG + j + 1)
                    if not (first and u < 2):
                        act.wait_ge(s_pv, qt * U + u - 1)
                    act.activation(PT[:, u % 2, j, 0:W], psT[0][:, 0:W], ACT.Copy).then_inc(s_pta, 1)
                act.wait_ge(s_pv, qt * U + u + 1)
                if u == 0 and not first:
                    act.wait_ge(s_proj, qt)
                act.activation(yT[:, u, :], psO[:, 0:P], ACT.Copy).then_inc(s_y, 1)

            def tile(qt):
                for u in range(U):
                    exps(qt, u)
                    if u >= 1:
                        copies(qt, u - 1)
                copies(qt, U - 1)
                act.wait_ge(s_h2t, qt + 1)
                if not (isinstance(qt, int) and qt == 0):
                    act.wait_ge(s_rproj, qt)
                    act.wait_ge(s_h2tw, 16 * qt)
                act.activation(h2t[:], psA[:].rearrange("p (k n) -> p k n", k=KC), ACT.Copy).then_inc(s_h2c, 1)

            for qt in range(WT):
                tile(qt)
            with act.Fori(WT, NT) as qt:
                tile(qt)

        @block.vector
        def _(dve):
            def maxes(ch, qt, u):
                W, k0, m, sinks = shape_of(qt)
                first = isinstance(qt, int) and qt == 0
                w = SW if sinks else W
                b = u % 2
                for j in range(HPG):
                    dve.wait_ge(s_scores, (qt * U + u) * HPG + j + 1)
                    if not (first and u < 2):
                        dve.wait_ge(s_pt, (qt * U + u - 1) * HPG)
                        if j == 0 and not (isinstance(qt, int) and (qt < WT - 1 or (qt == WT - 1 and u < 2))):
                            dve.wait_ge(s_skn, qt * U + u - 1 - (WT - 1) * U)
                    hold(dve, g)
                    dve.tensor_tensor_reduce(S[:, b, j, 0:w], psS[:, j, 0:w], mask[:, m, 0:w], 1.0, -3e38,
                                             ALU.add, ALU.max, mx[:, b, j:j + 1]).then_inc(s_masked, 1)
                dve.wait_ge(s_masked, (qt * U + u + 1) * HPG)
                dve.tensor_scalar(nm[:, b], mx[:, b], -1.0, None, ALU.mult).then_inc(s_nm, 1)

            def rest(ch, qt, u):
                W, k0, m, sinks = shape_of(qt)
                first = isinstance(qt, int) and qt == 0
                b = u % 2
                dve.wait_ge(s_exp, (qt * U + u + 1) * HPG)
                dve.reciprocal(rden[:, b], den[:, b]).then_inc(s_rden, 1)
                for j in (1, 3):
                    dve.wait_ge(s_pt, (qt * U + u) * HPG + j + 1)
                    if not (first and u < 2):
                        dve.wait_ge(s_pv, qt * U + u - 1)
                    dve.tensor_copy(PT[:, b, j, 0:W], psT[1][:, 0:W]).then_inc(s_ptd, 1)
                if sinks:
                    dve.wait_ge(s_sk, qt * U + u + 1 - (WT - 1) * U)
                    if not (first and u == 0):
                        dve.wait_ge(s_pv, qt * U + u)
                    dve.tensor_copy(skT[:], psO[0:HPG * SINK, P:2 * P]).then_inc(s_skc, 1)

            def tile(qt):
                ch = Chain(dve, s_dve, qt * (7 + RSQRT_STEPS))
                for u in range(U):
                    maxes(ch, qt, u)
                    if u >= 1:
                        rest(ch, qt, u - 1)
                rest(ch, qt, U - 1)
                Xq = X[:, bass.ds(qt, 1)].rearrange("p a c -> p (a c)")
                first = isinstance(qt, int) and qt == 0
                dve.wait_ge(s_proj, qt + 1)
                if not first:
                    dve.wait_ge(s_h2, qt)
                ch.step(dve.tensor_tensor(xh[:], psA[:], g["ga_row"][:], ALU.mult))
                ch.last()
                ch.step(dve.tensor_tensor(Xq, Xq, xh[:], ALU.add))
                ch.last()
                hold(dve, g)
                ch.step(dve.bn_stats(stats[:], Xq))
                ch.last()
                hold(dve, g)
                ch.step(dve.bn_aggr(mv[:], stats[:]))
                ch.last()
                rsqrt(dve, ch, rstd[:], mv[:, 1:2], (rt[:, 0:1], rt[:, 1:2]))
                dve.tensor_scalar(xh[:], Xq, mv[:, 0:1], rstd[:], ALU.subtract, ALU.mult).then_inc(s_xh, 1)
                dve.wait_ge(s_rproj, qt + 1)
                lg = LG[:, bass.ds(qt, 1)].rearrange("p a c -> p (a c)")
                dve.tensor_copy(lg, psA[:, 0:E]).then_inc(s_rl, 1)
                dve.wait_ge(s_rl, qt + 1)
                ch.step(dve.tensor_tensor(lgb[:], lg, g["rbias"][:], ALU.add))
                ch.last()
                hold(dve, g)
                ch.step(dve.max(v8[:], lgb[:]))
                ch.last()
                hold(dve, g)
                ch.step(dve.max_index(i8[:], v8[:], lgb[:]))
                ch.last()
                dve.tensor_copy(g["EIDX"][:, bass.ds(qt, 1)].rearrange("p a c -> p (a c)"), i8[:])

            dve.wait_ge(s_mask, 8)
            dve.wait_ge(g["s_in"][9], 16)
            for qt in range(WT):
                tile(qt)
            with dve.Fori(WT, NT) as qt:
                tile(qt)


def dispatch(nc, ctx, sb, ps, sem, g):
    LG, EIDX, GATE, POSI = (g[k] for k in ("LG", "EIDX", "GATE", "POSI"))
    B = lambda name, shape, dt=F32: sb(name, shape, dt, ctx)
    iota_i = B("iota_i", [P, E], I32)
    iota_e = B("iota_e", [P, E])
    iota_pi = B("iota_pi", [P, 1], I32)
    iota_p = B("iota_p", [P, 1])
    before = B("before", [P, P])
    OH = B("OH", [P, NT, TOPK, E])
    PR = B("PR", [P, NT, TOPK, E])
    M = B("M", [P, NT, E])
    MP = B("MP", [P, NT + 1, E])
    R = B("R", [P, NT, E])
    cnt_i = B("cnt_i", [P, E], I32)
    tiles = B("tiles", [P, E])
    incl = B("incl", [P, E])
    base = B("base", [P, E])
    lk = B("lk", [P, NT, TOPK])
    mxk = B("mxk", [P, NT])
    sumk = B("sumk", [P, NT])
    posf = B("posf", [P, NT, TOPK])
    eid_f = B("eid_f", [P, 1])
    eid_i = B("eid_i", [P, 1], I32)
    cmp_e = B("cmp_e", [P, E])
    HR = B("HR", [P, 2, C])
    psR = [ps(f"psR{i}", [P, NT // 2, E], F32, ctx) for i in range(2)]
    psC = ps("psC", [P, E], F32, ctx)
    s_iota, s_bef, s_cnt, s_rank, s_d, s_lk, s_ek, s_eid, s_slots = (
        sem("d_" + n) for n in ("iota", "bef", "cnt", "rank", "d", "lk", "ek", "eid", "slots"))
    s_row = [sem(f"d_row{i}") for i in range(2)]
    s_sent = [sem(f"d_sent{i}") for i in range(2)]
    with nc.Block() as block:
        @block.gpsimd
        def _(pool):
            pool.iota(iota_i[:], pattern=[[1, E]], base=0, channel_multiplier=0).then_inc(s_iota, 1)
            pool.iota(iota_pi[:], pattern=[[0, 1]], base=0, channel_multiplier=1).then_inc(s_iota, 1)
            pool.memset(before[:], 1.0).then_inc(s_bef, 1)
            pool.wait_ge(s_bef, 1)
            pool.affine_select(out=before[:], in_=before[:], compare_op=ALU.is_ge, fill=0.0, base=-1,
                               pattern=[[1, P]], channel_multiplier=-1).then_inc(s_bef, 1)
            pool.wait_ge(s_slots, 1)
            for t in range(NT):
                b = t % 2
                pool.wait_ge(s_row[b], 16 * (t // 2 + 1))
                for k in range(TOPK):
                    pool.indirect_dma_start(out=g["slot_x"], out_offset=bass.IndirectOffsetOnAxis(ap=POSI[:, t, k:k + 1], axis=0),
                                            in_=HR[:, b, :], in_offset=None).then_inc(s_sent[b], 16)
            for b in range(2):
                pool.wait_ge(s_sent[b], 16 * TOPK * (NT // 2))

        @block.sync
        def _(sp):
            for t in range(NT):
                b = t % 2
                if t >= 2:
                    sp.wait_ge(s_sent[b], 16 * TOPK * (t // 2))
                sp.dma_start(HR[:, b, :], g["h2_rows"][t]).then_inc(s_row[b], 16)

        @block.scalar
        def _(act):
            act.wait_ge(s_lk, 1)
            act.activation(lk[:], lk[:], ACT.Exp).then_inc(s_ek, 1)
            act.wait_ge(s_eid, 1)
            act.dma_start(g["tile_expert"].rearrange("a p -> p a"), eid_i[:]).then_inc(g["s_tile_expert"], 16)
            act.wait_ge(g["s_tile_expert"], 16)
            act.dma_start(g["eid_row"][:], g["tile_expert"]).then_inc(g["s_tile_expert"], 16)
            act.wait_ge(g["s_tile_expert"], 32)

        @block.tensor
        def _(pe):
            pe.wait_ge(s_cnt, 1)
            pe.wait_ge(s_bef, 2)
            pe.matmul(psC[:], g["ones"][:], MP[:, NT, :], start=True, stop=True).then_inc(s_rank, 1)
            for h in range(2):
                t = slice(h * NT // 2, (h + 1) * NT // 2)
                pe.matmul(psR[h][:], before[:], M[:, t, :], start=True, stop=False)
                pe.matmul(psR[h][:], g["ones"][:], MP[:, t, :], start=False, stop=True).then_inc(s_rank, 1)

        @block.vector
        def _(dve):
            ch = Chain(dve, s_d)
            dve.wait_ge(s_iota, 2)
            ch.step(dve.tensor_copy(iota_e[:], iota_i[:]))
            ch.step(dve.tensor_copy(iota_p[:], iota_pi[:]))
            ch.step(dve.memset(MP[:, 0, :], 0.0))
            ch.last()
            for k in range(TOPK):
                ch.step(dve.tensor_tensor(OH[:, :, k, :], iota_e[:].unsqueeze(1).broadcast_to([P, NT, E]),
                                          EIDX[:, :, k:k + 1].broadcast_to([P, NT, E]), ALU.is_equal))
            ch.last()
            ch.step(dve.tensor_tensor(M[:], OH[:, :, 0, :], OH[:, :, 1, :], ALU.add))
            for k in range(2, TOPK):
                ch.last()
                ch.step(dve.tensor_tensor(M[:], M[:], OH[:, :, k, :], ALU.add))
            for t in range(NT):
                ch.last()
                ins = dve.tensor_tensor(MP[:, t + 1, :], MP[:, t, :], M[:, t, :], ALU.add)
                if t < NT - 1:
                    ch.step(ins)
            ins.then_inc(s_cnt, 1)
            for k in range(TOPK):
                ch.step(dve.tensor_tensor(PR[:, :, k, :], OH[:, :, k, :], LG[:], ALU.mult))
            ch.last()
            ch.step(dve.tensor_reduce(lk[:], PR[:], AX.X, ALU.add))
            ch.last()
            ch.step(dve.tensor_reduce(mxk[:], lk[:], AX.X, ALU.max))
            ch.last()
            dve.tensor_tensor(lk[:], lk[:], mxk[:].unsqueeze(2).broadcast_to([P, NT, TOPK]), ALU.subtract).then_inc(s_lk, 1)
            dve.wait_ge(s_ek, 1)
            ch.step(dve.tensor_reduce(sumk[:], lk[:], AX.X, ALU.add))
            ch.last()
            ch.step(dve.reciprocal(sumk[:], sumk[:]))
            ch.last()
            ch.step(dve.tensor_tensor(GATE[:], lk[:], sumk[:].unsqueeze(2).broadcast_to([P, NT, TOPK]), ALU.mult))
            dve.wait_ge(s_rank, 1)
            ch.step(dve.tensor_scalar(cnt_i[:], psC[:], float(P - 1), None, ALU.add))
            ch.last()
            ch.step(dve.tensor_scalar(cnt_i[:], cnt_i[:], 7, None, ALU.arith_shift_right))
            ch.last()
            ch.step(dve.tensor_copy(tiles[:], cnt_i[:]))
            ch.step(dve.memset(base[:], 1.0))
            ch.last()
            ch.step(dve.tensor_tensor_scan(incl[:], base[:], tiles[:], 0.0, ALU.mult, ALU.add))
            ch.last()
            ch.step(dve.tensor_tensor(base[:], incl[:], tiles[:], ALU.subtract))
            ch.step(dve.tensor_scalar(cmp_e[:], incl[:], iota_p[:], None, ALU.is_le))
            ch.last()
            ch.step(dve.tensor_reduce(eid_f[:], cmp_e[:], AX.X, ALU.add))
            ch.step(dve.tensor_scalar(base[:], base[:], float(P), None, ALU.mult))
            ch.last()
            dve.tensor_scalar(eid_i[:], eid_f[:], float(E - 1), None, ALU.min).then_inc(s_eid, 1)
            for h in range(2):
                dve.wait_ge(s_rank, 2 + h)
                t = slice(h * NT // 2, (h + 1) * NT // 2)
                ch.step(dve.tensor_tensor(R[:, t, :], psR[h][:], base[:].unsqueeze(1).broadcast_to([P, NT // 2, E]), ALU.add))
            ch.last()
            for k in range(TOPK):
                ch.step(dve.tensor_tensor(PR[:, :, k, :], OH[:, :, k, :], R[:], ALU.mult))
            ch.last()
            ch.step(dve.tensor_reduce(posf[:], PR[:], AX.X, ALU.add))
            ch.last()
            dve.tensor_copy(POSI[:], posf[:]).then_inc(s_slots, 1)


def shared_experts(nc, ctx, sb, ps, sem, g):
    X = g["X"]
    B = lambda name, shape, dt=F32: sb(name, shape, dt, ctx)
    GT = 4
    NG = NT // GT
    WG = B("WG", [P, 2, KC, SH * HC * P // 2])
    WU = B("WU", [P, 2, KC, SH * HC * P // 2])
    WD = B("WD", [P, SH, HC, C])
    HT = B("HT", [P, 2, GT, KC, P])
    sg = B("sg", [P, 2, C])
    hid = B("hid", [P, SH * HC, C])
    tmp = B("tmp", [P, 2, C])
    psG = [ps(f"psG{i}", [P, C], F32, ctx) for i in range(2)]
    psU = [ps(f"psU{i}", [P, C], F32, ctx) for i in range(2)]
    psY = [ps(f"psY{i}", [P, C], F32, ctx) for i in range(2)]
    s_w = [sem(f"h_w{i}") for i in range(3)]
    s_ht = [sem(f"h_ht{i}") for i in range(2)]
    s_gate, s_up, s_silu, s_hid, s_down, s_add, s_t = (sem("h_" + n) for n in ("gate", "up", "silu", "hid", "down", "add", "t"))
    NCH = SH * HC
    with nc.Block() as block:
        @block.sync
        def _(sp):
            sp.dma_start(WG[:], g["swg"].rearrange("s (p k) h -> p s k h", k=KC)).then_inc(s_w[0], 16)
            sp.dma_start(WU[:], g["swu"].rearrange("s (p k) h -> p s k h", k=KC)).then_inc(s_w[1], 16)
            sp.dma_start(WD[:], g["swd"].rearrange("s (c p) n -> p s c n", p=P)).then_inc(s_w[2], 16)
            for n in range(NG):
                if n >= 2:
                    sp.wait_ge(s_up, NCH * (n - 1))
                for t in range(GT):
                    sp.dma_start(HT[:, n % 2, t], g["h2t_cols"][n * GT + t]).then_inc(s_ht[n % 2], 16)

        @block.tensor
        def _(pe):
            pe.wait_ge(s_w[0], 16)
            pe.wait_ge(s_w[1], 16)
            pe.wait_ge(s_w[2], 16)

            def up(n, c):
                i = n * NCH + c
                for w, bank, done in ((WG, psG, s_gate), (WU, psU, s_up)):
                    if i >= 2:
                        pe.wait_ge(s_hid, i - 1)
                    for k in range(KC):
                        ins = pe.matmul(bank[i % 2][:].rearrange("p (t n) -> p t n", t=GT),
                                        w[:, c // HC, k, (c % HC) * P:(c % HC + 1) * P],
                                        HT[:, n % 2, :, k, :], start=(k == 0), stop=(k == KC - 1))
                    ins.then_inc(done, 1)

            for n in range(NG):
                pe.wait_ge(s_ht[n % 2], 16 * GT * (n // 2 + 1))
                for c in range(NCH):
                    up(n, c)
                pe.wait_ge(s_hid, NCH * (n + 1))
                for t in range(GT):
                    i = n * GT + t
                    if i >= 2:
                        pe.wait_ge(s_add, i - 1)
                    for c in range(NCH):
                        ins = pe.matmul(psY[i % 2][:], hid[:, c, t * P:(t + 1) * P], WD[:, c // HC, c % HC, :],
                                        start=(c == 0), stop=(c == NCH - 1))
                    ins.then_inc(s_down, 1)

        @block.scalar
        def _(act):
            for i in range(NG * NCH):
                act.wait_ge(s_gate, i + 1)
                if i >= 2:
                    act.wait_ge(s_hid, i - 1)
                act.activation(sg[:, i % 2], psG[i % 2][:], ACT.Silu).then_inc(s_silu, 1)

        @block.vector
        def _(dve):
            for n in range(NG):
                if n:
                    dve.wait_ge(s_down, GT * n)
                for c in range(NCH):
                    i = n * NCH + c
                    dve.wait_ge(s_silu, i + 1)
                    dve.wait_ge(s_up, i + 1)
                    dve.tensor_tensor(hid[:, c], sg[:, i % 2], psU[i % 2][:], ALU.mult).then_inc(s_hid, 1)
                for t in range(GT):
                    i = n * GT + t
                    dve.wait_ge(s_down, i + 1)
                    if i >= 2:
                        dve.wait_ge(s_t, i - 1)
                    dve.tensor_tensor(tmp[:, i % 2], psY[i % 2][:], g["gb_row"][:], ALU.mult).then_inc(s_add, 1)

        @block.gpsimd
        def _(pool):
            for i in range(NT):
                pool.wait_ge(s_add, i + 1)
                pool.tensor_tensor(X[:, i], X[:, i], tmp[:, i % 2], ALU.add).then_inc(s_t, 1)


def routed_experts(nc, ctx, sb, ps, sem, g):
    B = lambda name, shape, dt=F32: sb(name, shape, dt, ctx)
    NB = 2
    ident = g["ident"]
    WG = B("rWG", [P, NB, KC, F])
    WU = B("rWU", [P, NB, KC, F])
    WD = B("rWD", [P, NB, C])
    XT = B("rX", [P, NB, C])
    xT = B("rxT", [P, NB, KC, P])
    sg = B("rsg", [P, NB, P])
    hT = B("rhT", [P, NB, P])
    Y = B("rY", [P, NB, C])
    psX = [ps(f"rpX{i}", [P, KC, P], F32, ctx) for i in range(2)]
    psG = [ps(f"rpG{i}", [P, P], F32, ctx) for i in range(2)]
    psU = [ps(f"rpU{i}", [P, P], F32, ctx) for i in range(2)]
    psY = [ps(f"rpY{i}", [P, C], F32, ctx) for i in range(2)]
    s_w = [sem(f"r_w{i}") for i in range(NB)]
    s_x = [sem(f"r_x{i}") for i in range(NB)]
    s_yo = [sem(f"r_yo{i}") for i in range(NB)]
    s_tr, s_xt, s_gate, s_up, s_silu, s_h, s_down, s_y = (
        sem("r_" + n) for n in ("tr", "xt", "gate", "up", "silu", "h", "down", "y"))
    wg_v = g["wg"].rearrange("e (p k) f -> e p k f", k=KC)
    wu_v = g["wu"].rearrange("e (p k) f -> e p k f", k=KC)
    with nc.Block() as block:
        @block.scalar
        def _(act):
            def load(t, b, head):
                e = act.value_load(g["eid_row"][0:1, bass.ds(t, 1)], min_val=0, max_val=E - 1)
                if not head:
                    act.wait_ge(s_up, t - NB + 1)
                act.dma_start(WG[:, b], wg_v[bass.ds(e, 1)].rearrange("a p k f -> p (a k) f")).then_inc(s_w[b], 16)
                act.dma_start(WU[:, b], wu_v[bass.ds(e, 1)].rearrange("a p k f -> p (a k) f")).then_inc(s_w[b], 16)
                if not head:
                    act.wait_ge(s_down, t - NB + 1)
                act.dma_start(WD[:, b], g["wd"][bass.ds(e, 1)].rearrange("a p n -> (a p) n")).then_inc(s_w[b], 16)

            def compute(t, b, head):
                act.wait_ge(s_tr, t + 1)
                if not head:
                    act.wait_ge(s_up, t - NB + 1)
                act.activation(xT[:, b], psX[b][:], ACT.Copy).then_inc(s_xt, 1)
                act.wait_ge(s_gate, t + 1)
                if not head:
                    act.wait_ge(s_h, t - NB + 1)
                act.activation(sg[:, b], psG[b][:], ACT.Silu).then_inc(s_silu, 1)

            for b in range(NB):
                load(b, b, True)
            for b in range(NB):
                compute(b, b, True)
                load(b + NB, b, False)
            with act.Fori(1, MAXT // NB - 1) as h:
                for b in range(NB):
                    compute(h * NB + b, b, False)
                    load(h * NB + b + NB, b, False)
            for b in range(NB):
                compute(MAXT - NB + b, b, False)

        @block.sync
        def _(sp):
            def load(t, b, head):
                if not head:
                    sp.wait_ge(s_tr, t - NB + 1)
                sp.dma_start(XT[:, b], g["slot_x"][bass.ds(t * P, P), :]).then_inc(s_x[b], 16)

            def store(t, b):
                sp.wait_ge(s_y, t + 1)
                sp.dma_start(g["slot_y"][bass.ds(t * P, P), :], Y[:, b]).then_inc(s_yo[b], 16)
            for b in range(NB):
                load(b, b, True)
            with sp.Fori(0, MAXT // NB - 1) as h:
                for b in range(NB):
                    load(h * NB + b + NB, b, False)
                    store(h * NB + b, b)
            for b in range(NB):
                store(MAXT - NB + b, b)
            for b in range(NB):
                sp.wait_ge(s_yo[b], 16 * MAXT // NB)

        @block.tensor
        def _(pe):
            def tile(h, b, head):
                t = h * NB + b
                pe.wait_ge(s_x[b], 16 * h + 16)
                if not head:
                    pe.wait_ge(s_xt, t - NB + 1)
                for k in range(KC):
                    ins = pe.transpose(psX[b][:, k, :], XT[:, b, k::KC], ident[:])
                ins.then_inc(s_tr, 1)
                pe.wait_ge(s_w[b], 48 * h + 48)
                pe.wait_ge(s_xt, t + 1)
                if not head:
                    pe.wait_ge(s_h, t - NB + 1)
                for w, bank, done in ((WG, psG, s_gate), (WU, psU, s_up)):
                    for k in range(KC):
                        ins = pe.matmul(bank[b][:], w[:, b, k, :], xT[:, b, k, :], start=(k == 0), stop=(k == KC - 1))
                    ins.then_inc(done, 1)
                pe.wait_ge(s_h, t + 1)
                if not head:
                    pe.wait_ge(s_y, t - NB + 1)
                pe.matmul(psY[b][:], hT[:, b], WD[:, b], start=True, stop=True).then_inc(s_down, 1)
            for b in range(NB):
                tile(0, b, True)
            with pe.Fori(1, MAXT // NB) as h:
                for b in range(NB):
                    tile(h, b, False)

        @block.vector
        def _(dve):
            def tile(h, b, head):
                t = h * NB + b
                dve.wait_ge(s_silu, t + 1)
                dve.wait_ge(s_up, t + 1)
                if not head:
                    dve.wait_ge(s_down, t - NB + 1)
                dve.tensor_tensor(hT[:, b], sg[:, b], psU[b][:], ALU.mult).then_inc(s_h, 1)
                dve.wait_ge(s_down, t + 1)
                if not head:
                    dve.wait_ge(s_yo[b], 16 * h)
                dve.tensor_copy(Y[:, b], psY[b][:]).then_inc(s_y, 1)
            for b in range(NB):
                tile(0, b, True)
            with dve.Fori(1, MAXT // NB) as h:
                for b in range(NB):
                    tile(h, b, False)


def combine(nc, ctx, sb, ps, sem, g):
    X, GATE, POSI = (g[k] for k in ("X", "GATE", "POSI"))
    B = lambda name, shape, dt=F32: sb(name, shape, dt, ctx)
    NB = 3
    YR = B("YR", [P, NB, TOPK, C])
    acc = B("acc", [P, 2, C])
    s_rows = [sem(f"c_rows{i}") for i in range(NB)]
    s_c, s_sum, s_out = (sem("c_" + n) for n in ("c", "sum", "out"))
    with nc.Block() as block:
        @block.gpsimd
        def _(pool):
            for t in range(NT):
                b = t % NB
                if t >= NB:
                    pool.wait_ge(s_sum, t - NB + 1)
                for k in range(TOPK):
                    pool.indirect_dma_start(out=YR[:, b, k, :], out_offset=None, in_=g["slot_y"],
                                            in_offset=bass.IndirectOffsetOnAxis(ap=POSI[:, t, k:k + 1], axis=0)).then_inc(s_rows[b], 16)

        @block.vector
        def _(dve):
            ch = Chain(dve, s_c)
            for t in range(NT):
                b = t % NB
                dve.wait_ge(s_rows[b], 16 * TOPK * (t // NB + 1))
                a = acc[:, t % 2]
                ch.step(dve.tensor_scalar(a, YR[:, b, 0, :], GATE[:, t, 0:1], None, ALU.mult))
                for k in range(1, TOPK):
                    ch.last()
                    ins = dve.scalar_tensor_tensor(out=a, in0=YR[:, b, k, :], scalar=GATE[:, t, k:k + 1], in1=a,
                                                   op0=ALU.mult, op1=ALU.add)
                    ch.step(ins)
                ch.last()
                ch.step(dve.tensor_tensor(a, a, g["gb_row"][:], ALU.mult))
                ch.last()
                dve.tensor_tensor(X[:, t], X[:, t], a, ALU.add).then_inc(s_sum, 1)

        @block.sync
        def _(sp):
            for t in range(NT):
                sp.wait_ge(s_sum, t + 1)
                sp.dma_start(g["out_t"][:, t], X[:, t]).then_inc(s_out, 16)
            sp.wait_ge(s_out, 16 * NT)


_INS = ["L0_attn_x", "L0_attn_Wq", "L0_attn_Wk", "L0_attn_Wv", "L0_attn_Wo", "L0_ffn_router_w", "L0_ffn_router_bias",
        "L0_ffn_wg", "L0_ffn_wu", "L0_ffn_wd", "L0_ffn_swg", "L0_ffn_swu", "L0_ffn_swd", "L0_c", "L0_wmod"]
_OUTS = [((1, T, C), "float32")]


def kernel(**inputs):
    import numpy as _np
    import concourse.bacc as _bacc
    from concourse import mybir as _mybir
    from concourse.bass_utils import run_bass_kernel_spmd as _run

    nc = _bacc.Bacc("TRN2", target_bir_lowering=False, num_devices=1)
    arrays, args = {}, []
    for name in _INS:
        a = _np.ascontiguousarray(inputs[name])
        arrays[f"in_{name}_dram"] = a
        args.append(nc.dram_tensor(f"in_{name}_dram", a.shape, _mybir.dt.from_np(a.dtype), kind="ExternalInput").ap())
    for i, (shape, dtype) in enumerate(_OUTS):
        dt = _mybir.dt.from_np(_np.dtype(dtype))
        args.append(nc.dram_tensor(f"out_{i}_dram", shape, dt, kind="ExternalOutput").ap())
    build_kernel(nc, *args)
    r = _run(nc, [arrays], core_ids=[0])
    got = tuple(r.results[0][f"out_{i}_dram"] for i in range(len(_OUTS)))
    return got[0]
```

```python
from contextlib import ExitStack

import concourse.bass as bass
from concourse import mybir

F32 = mybir.dt.float32
BF16 = mybir.dt.bfloat16
I32 = mybir.dt.int32
U32 = mybir.dt.uint32
ALU = mybir.AluOpType
ACT = mybir.ActivationFunctionType
AX = mybir.AxisListType

P = 128
T, C = 2048, 512
NT = T // P
KC = C // P
HS, NH, NKV = 32, 16, 4
HPG = NH // NKV
SINK = 4
WT = 3
E, F, TOPK = 64, 128, 4
SH, HC = 2, 4
MAXT = 128
SLOTS = MAXT * P
AHEAD_TILES = 2
EPS = 1e-5
NEG = -1e30
GROUPS = 4
GT = T // GROUPS
SCALE = HS ** -0.5
KW = WT * P
SW = KW + SINK


class Chain:

    def __init__(self, eng, sem, base=0):
        self.eng, self.sem, self.base, self.n = eng, sem, base, 0

    def step(self, ins):
        ins.then_inc(self.sem, 1)
        self.n += 1

    def last(self):
        self.eng.wait_ge(self.sem, self.base + self.n)


def wait(eng, sem, value):
    if not (isinstance(value, int) and value <= 0):
        eng.wait_ge(sem, value)


def hold(eng, g):
    eng.sem_inc(g["s_held"][eng.engine.name], 1)


def rsqrt(dve, ch, out, var, tmp):
    v, t = tmp
    ch.step(dve.tensor_scalar(v, var, EPS, None, ALU.add))
    ch.last()
    ch.step(dve.tensor_scalar(t.bitcast(I32), v.bitcast(I32), 1, None, ALU.arith_shift_right))
    ch.last()
    ch.step(dve.tensor_scalar(out.bitcast(I32), t.bitcast(I32), -1.0, float(0x5F3759DF), ALU.mult, ALU.add))
    for _ in range(3):
        ch.last()
        ch.step(dve.tensor_tensor(t, out, out, ALU.mult))
        ch.last()
        ch.step(dve.tensor_tensor(t, t, v, ALU.mult))
        ch.last()
        ch.step(dve.tensor_scalar(t, t, -0.5, 1.5, ALU.mult, ALU.add))
        ch.last()
        ch.step(dve.tensor_tensor(out, out, t, ALU.mult))
    ch.last()


RSQRT_STEPS = 15


def build_kernel(nc, x, Wq, Wk, Wv, Wo, router_w, router_bias, wg, wu, wd, swg, swu, swd, cvec, wmod, out):
    stack = ExitStack()
    with stack:
        def sb(name, shape, dt=F32, ctx=stack):
            return ctx.enter_context(nc.sbuf_tensor(name, shape, dt))

        def ps(name, shape, dt=F32, ctx=stack):
            return ctx.enter_context(nc.psum_tensor(name, shape, dt))

        def sem(name):
            return stack.enter_context(nc.semaphore(name))

        x_t = x.rearrange("b (t p) c -> p (b t) c", p=P)
        out_t = out.rearrange("b (t p) c -> p (b t) c", p=P)
        h2_rows = nc.dram_tensor("h2_rows", [NT, P, C], F32, kind="Internal").ap()
        h2t_cols = nc.dram_tensor("h2t_cols", [NT, P, KC, P], F32, kind="Internal").ap()
        slot_y = nc.dram_tensor("slot_y", [SLOTS, C], F32, kind="Internal").ap()

        X = sb("X", [P, NT, C])
        ident = sb("ident", [P, P])
        ones = sb("ones", [P, P])
        ga_row = sb("ga_row", [P, C])
        gb_row = sb("gb_row", [P, C])
        cb1_row = sb("cb1_row", [P, C])
        sb_row = sb("sb_row", [P, C])
        LG = sb("LG", [P, NT, E])
        EIDX = sb("EIDX", [P, NT, 8])
        GATE = sb("GATE", [P, NT, TOPK])
        POSI = sb("POSI", [P, NT, TOPK], I32)
        TOKI = sb("TOKI", [P, MAXT + AHEAD_TILES], I32)

        tile_expert = nc.dram_tensor("tile_expert", [1, P], I32, kind="Internal").ap()
        eid_row = sb("eid_row", [1, P], I32)
        end_row = sb("end_row", [1, E], I32)
        pairs = sb("pairs", [1, 1], I32)
        s_tile_expert = sem("s_tile_expert")
        s_held = {name: sem("s_held_" + name) for name in ("DVE", "Pool", "SP", "Activation")}
        s_ident = sem("s_ident")
        s_in = [sem(f"s_in{i}") for i in range(10)]
        s_stacked = [sem(f"s_stacked{i}") for i in range(GROUPS)]

        attn = ExitStack()
        with attn:
            A = lambda name, shape, dt=F32: sb(name, shape, dt, attn)
            WoT = A("WoT", [P, KC, C])
            V = A("V", [P, NT, P])
            Q4 = A("Q4", [P, NH, T], BF16)
            K4 = A("K4", [P, NKV, T], BF16)
            rw = A("rw", [P, KC, E])
            rbias = A("rbias", [P, E])

            QT = A("QT", [P, GROUPS, 2, NKV, GT], BF16)
            KT = A("KT", [P, GROUPS, 2, GT], BF16)
            with ExitStack() as pro:
                prologue(nc, pro, sb, ps, sem, locals())
            with ExitStack() as mid:
                attention(nc, mid, sb, ps, sem, locals())
        with ExitStack() as tail:
            shared_experts(nc, tail, sb, ps, sem, locals())
        with ExitStack() as tail:
            routed_experts(nc, tail, sb, ps, sem, locals())
        with ExitStack() as tail:
            combine(nc, tail, sb, ps, sem, locals())


def prologue(nc, ctx, sb, ps, sem, g):
    X, V, Q4, K4, WoT = (g[k] for k in ("X", "V", "Q4", "K4", "WoT"))
    QT, KT = g["QT"], g["KT"]
    ident, ones = g["ident"], g["ones"]
    s_in = g["s_in"]
    B = lambda name, shape, dt=F32: sb(name, shape, dt, ctx)
    WqT = B("WqT", [P, KC, C])
    WkvT = B("WkvT", [P, 2, KC, P])
    xh = B("xh", [P, 2, C])
    hT = B("hT", [P, 2, KC, P])
    cT = B("cT", [P, KC])
    sc = B("sc", [P, KC])
    sa_col = B("sa_col", [P, KC])
    ca1_col = B("ca1_col", [P, KC])
    stats = B("stats", [P, NT, 6])
    mv = B("mv", [P, NT, 2])
    rstd = B("rstd", [P, NT])
    rt = B("rt", [P, 2, NT])
    room = Q4[:].rearrange("p h t -> p (h t)").bitcast(F32)
    wm = room[:, 0:6 * KC * C].rearrange("p (r k s n) -> p r k s n", r=3, k=KC, s=2)
    Wqo = room[:, 6 * KC * C:8 * KC * C].rearrange("p (s o c) -> p s o c", s=2, o=KC)
    room = K4[:].rearrange("p h t -> p (h t)").bitcast(F32)
    Wkv = room[:, 0:2 * C].rearrange("p (s c) -> p s c", s=2)
    scb = room[:, 2 * C:3 * C].rearrange("p (k m) -> p k m", k=KC)
    gtmp = room[:, 3 * C:5 * C].rearrange("p (s c) -> p s c", s=2)
    s_c, s_sc, s_scb, s_mod, s_modc, s_wt, s_wtc, s_dve, s_xh, s_tr, s_hT, s_q, s_k, s_v, s_hi, s_lo, s_vc, s_ln = (
        sem("p_" + n) for n in ("c", "sc", "scb", "mod", "modc", "wt", "wtc", "dve", "xh", "tr", "hT", "q", "k", "v",
                                "hi", "lo", "vc", "ln"))
    s_wm = [sem(f"p_wm{i}") for i in range(3)]
    psT = [ps(f"psT{i}", [P, KC, P], F32, ctx) for i in range(2)]
    psQ = [ps(f"psQ{i}", [P, KC, P], F32, ctx) for i in range(2)]
    psK = [ps(f"psK{i}", [P, C], F32, ctx) for i in range(2)]
    psV = [ps(f"psV{i}", [P, C], F32, ctx) for i in range(2)]
    psW = psT + psQ
    wmod_v = g["wmod"].rearrange("(p k) n -> p k n", k=KC)
    TURNS, MODS = 2 * KC + 2, 6
    XQ = NT // 4

    def parts(dst, h, b, part):
        tok = bass.ds(h % (XQ // 2) * (2 * P) + b * P, P)
        if dst is KT:
            return dst[:, bass.ds(h // (XQ // 2), 1), part, tok].rearrange("p a n -> p (a n)")
        return dst[:, bass.ds(h // (XQ // 2), 1), part, :, tok].rearrange("p a g n -> p (a g) n")

    def sweep(eng, tile):
        for i in range(2):
            tile(0, i, i)
        with eng.Fori(1, NT // 2 - 1) as h:
            for b in range(2):
                tile(h, h * 2 + b, b)
        for i in range(NT - 2, NT):
            tile(NT // 2 - 1, i, i % 2)

    with nc.Block() as block:
        @block.sync
        def _(sp):
            def mod_sections(r):
                sp.dma_start(wm[:, r], wmod_v[:, :, 2 * r * C:(2 * r + 2) * C].rearrange("p k (s n) -> p k s n", s=2)).then_inc(s_wm[r], 16)

            sp.dma_start(cT[:], g["cvec"].rearrange("b (p k) -> (b p) k", k=KC)).then_inc(s_c, 16)
            sp.dma_start(Wqo[:, 0], g["Wq"].rearrange("(o p) c -> p o c", p=P)).then_inc(s_in[0], 16)
            sp.dma_start(Wkv[:, 0], g["Wk"]).then_inc(s_in[1], 16)
            sp.dma_start(Wkv[:, 1], g["Wv"]).then_inc(s_in[2], 16)
            for i in range(4):
                sp.dma_start(X[:, XQ * i:XQ * (i + 1)], g["x_t"][:, XQ * i:XQ * (i + 1)]).then_inc(s_in[3 + i], 16)
                if i == 0:
                    mod_sections(0)
            mod_sections(1)
            mod_sections(2)
            sp.dma_start(Wqo[:, 1], g["Wo"].rearrange("(o p) c -> p o c", p=P)).then_inc(s_in[7], 16)
            sp.dma_start(g["rw"][:], g["router_w"].rearrange("(p k) e -> p k e", k=KC)).then_inc(s_in[8], 16)
            sp.dma_start(g["rbias"][:], g["router_bias"].rearrange("(a e) -> a e", a=1).broadcast_to([P, E])).then_inc(s_in[9], 16)
            sp.wait_ge(s_wtc, TURNS)
            sp.wait_ge(s_modc, MODS)
            for q in range(GROUPS - 1):
                sp.wait_ge(s_lo, 2 * XQ * (q + 1))
                stack_group(sp, g, q)
            for q in range(GROUPS - 1):
                sp.wait_ge(g["s_stacked"][q], 16 * 2 * 4 * HPG)

        @block.gpsimd
        def _(pool):
            pool.memset(ident[:], 0.0).then_inc(g["s_ident"], 1)
            pool.memset(ones[:], 1.0).then_inc(g["s_ident"], 1)
            pool.wait_ge(g["s_ident"], 2)
            pool.affine_select(out=ident[:], in_=ident[:], compare_op=ALU.not_equal, fill=1.0, base=0,
                               pattern=[[-1, P]], channel_multiplier=1).then_inc(g["s_ident"], 1)

        @block.scalar
        def _(act):
            act.wait_ge(s_c, 16)
            act.activation(sc[:], cT[:], ACT.Silu).then_inc(s_sc, 1)
            for n in range(TURNS):
                act.wait_ge(s_wt, n + 1)
                if n < KC:
                    dst = WqT[:, n]
                elif n < KC + 2:
                    dst = WkvT[:, n - KC].rearrange("p k o -> p (k o)")
                else:
                    dst = WoT[:, n - KC - 2]
                act.activation(dst, psW[n % 4][:].rearrange("p k n -> p (k n)"), ACT.Copy).then_inc(s_wtc, 1)

            def modulated(i, b):
                act.wait_ge(s_tr, i + 1)
                wait(act, s_v, i - 1)
                if isinstance(i, int) and i == 0:
                    act.wait_ge(s_modc, 2)
                for k in range(KC):
                    ins = act.activation(hT[:, b, k, :], psT[b][:, k, :], ACT.Identity,
                                         bias=sa_col[:, k:k + 1], scale=ca1_col[:, k:k + 1])
                ins.then_inc(s_hT, 1)

            def tile(h, i, b):
                q_hi, k_hi = parts(QT, h, b, 0), parts(KT, h, b, 0)
                if not isinstance(i, int) or i + 1 < NT:
                    modulated(i + 1, 1 - b)
                act.wait_ge(s_q, i + 1)
                act.activation(q_hi, psQ[b][:], ACT.Copy, scale=-SCALE).then_inc(s_hi, 1)
                act.wait_ge(s_k, i + 1)
                act.activation(k_hi, psK[b][:, 0:P], ACT.Copy).then_inc(s_hi, 1)
                act.wait_ge(s_v, i + 1)
                act.activation(V[:, bass.ds(i, 1)].rearrange("p a c -> p (a c)"), psV[b][:, 0:P],
                               ACT.Copy).then_inc(s_vc, 1)
            modulated(0, 0)
            sweep(act, tile)

        @block.vector
        def _(dve):
            ch = Chain(dve, s_dve)
            dve.wait_ge(s_sc, 1)
            for k in range(KC):
                dve.tensor_copy(scb[:, k, :], sc[:, k:k + 1].broadcast_to([P, P])).then_inc(s_scb, 1)
            ln = Chain(dve, s_ln)
            for i in range(NT):
                if i % XQ == 0:
                    dve.wait_ge(s_in[3 + i // XQ], 16)
                ln.step(dve.bn_stats(stats[:, i], X[:, i]))
                if i == XQ - 1:
                    dve.wait_ge(s_mod, 1)
                    dve.tensor_copy(sa_col[:], psK[0][:, 0:KC]).then_inc(s_modc, 1)
                    dve.wait_ge(s_mod, 2)
                    dve.tensor_scalar(ca1_col[:], psK[1][:, 0:KC], 1.0, None, ALU.add).then_inc(s_modc, 1)
            ln.last()
            for i in range(NT):
                ln.step(dve.bn_aggr(mv[:, i], stats[:, i]))
            ln.last()
            rsqrt(dve, ln, rstd[:], mv[:, :, 1:2].rearrange("p t a -> p (t a)"), (rt[:, 0], rt[:, 1]))

            def norm(i, b):
                wait(dve, s_tr, i - 1)
                dve.tensor_scalar(xh[:, b], X[:, bass.ds(i, 1)].rearrange("p a c -> p (a c)"),
                                  mv[:, bass.ds(i, 1), 0:1].rearrange("p a b -> p (a b)"), rstd[:, bass.ds(i, 1)],
                                  ALU.subtract, ALU.mult).then_inc(s_xh, 1)

            def tile(h, i, b):
                if not isinstance(i, int) or i + 2 < NT:
                    norm(i + 2, b)
                dve.wait_ge(s_hi, 2 * i + 1)
                dve.scalar_tensor_tensor(out=parts(QT, h, b, 1), in0=psQ[b][:], scalar=-SCALE, in1=parts(QT, h, b, 0),
                                         op0=ALU.mult, op1=ALU.subtract).then_inc(s_lo, 1)
                dve.wait_ge(s_hi, 2 * i + 2)
                dve.scalar_tensor_tensor(out=parts(KT, h, b, 1), in0=psK[b][:, 0:P], scalar=1.0, in1=parts(KT, h, b, 0),
                                         op0=ALU.mult, op1=ALU.subtract).then_inc(s_lo, 1)

            def floored(dst, src, sem_value):
                dve.wait_ge(s_mod, sem_value)
                ch.step(dve.tensor_scalar(gtmp[:, 0], src, -1.0, 0.25, ALU.mult, ALU.max))
                ch.last()
                ch.step(dve.scalar_tensor_tensor(out=gtmp[:, 0], in0=src, scalar=0.25, in1=gtmp[:, 0],
                                                 op0=ALU.max, op1=ALU.max))
                ch.step(dve.tensor_scalar(gtmp[:, 1], src, 0.0, 2.0, ALU.is_ge, ALU.mult))
                ch.last()
                dve.scalar_tensor_tensor(out=dst, in0=gtmp[:, 1], scalar=-1.0, in1=gtmp[:, 0],
                                         op0=ALU.add, op1=ALU.mult).then_inc(s_modc, 1)
            norm(0, 0)
            norm(1, 1)
            floored(g["ga_row"][:], psV[0][:], 3)
            dve.wait_ge(s_mod, 4)
            dve.tensor_copy(g["sb_row"][:], psV[1][:]).then_inc(s_modc, 1)
            dve.wait_ge(s_mod, 5)
            dve.tensor_scalar(g["cb1_row"][:], psK[0][:], 1.0, None, ALU.add).then_inc(s_modc, 1)
            dve.wait_ge(s_modc, 3)
            floored(g["gb_row"][:], psK[1][:], 6)
            sweep(dve, tile)

        @block.tensor
        def _(pe):
            def columns(s, bank):
                for c in range(KC):
                    for k in range(KC):
                        ins = pe.matmul(bank[:, c:c + 1], wm[:, 0, k, s, c::KC], sc[:, k:k + 1],
                                        start=(k == 0), stop=(k == KC - 1))
                ins.then_inc(s_mod, 1)

            def rows(r, s, bank):
                for k in range(KC):
                    ins = pe.matmul(bank[:], scb[:, k, :], wm[:, r, k, s, :], start=(k == 0), stop=(k == KC - 1))
                ins.then_inc(s_mod, 1)

            def turn(n, blocks):
                if n >= 4:
                    pe.wait_ge(s_wtc, n - 3)
                for j, b in enumerate(blocks):
                    ins = pe.transpose(psW[n % 4][:, j, :], b, ident[:])
                ins.then_inc(s_wt, 1)

            pe.wait_ge(g["s_ident"], 3)
            pe.wait_ge(s_in[0], 16)
            for k in range(KC):
                turn(k, [Wqo[:, 0, o, k::KC] for o in range(KC)])
            pe.wait_ge(s_in[1], 16)
            turn(KC, [Wkv[:, 0, k::KC] for k in range(KC)])
            pe.wait_ge(s_in[2], 16)
            turn(KC + 1, [Wkv[:, 1, k::KC] for k in range(KC)])
            pe.wait_ge(s_sc, 1)
            pe.wait_ge(s_wm[0], 16)
            columns(0, psK[0])
            columns(1, psK[1])
            pe.wait_ge(s_scb, KC)
            pe.wait_ge(s_wm[1], 16)
            rows(1, 0, psV[0])
            rows(1, 1, psV[1])
            pe.wait_ge(s_wm[2], 16)
            pe.wait_ge(s_modc, 2)
            rows(2, 0, psK[0])
            rows(2, 1, psK[1])
            pe.wait_ge(s_in[7], 16)
            for k in range(KC):
                turn(KC + 2 + k, [Wqo[:, 1, o, k * P:(k + 1) * P] for o in range(KC)])

            def turned(i, b):
                pe.wait_ge(s_xh, i + 1)
                wait(pe, s_hT, i - 1)
                for k in range(KC):
                    ins = pe.transpose(psT[b][:, k, :], xh[:, b, k::KC], ident[:])
                ins.then_inc(s_tr, 1)

            def tile(h, i, b):
                if not isinstance(i, int) or i + 1 < NT:
                    turned(i + 1, 1 - b)
                pe.wait_ge(s_hT, i + 1)
                wait(pe, s_lo, (i - 1) * 2)
                for o in range(KC):
                    for k in range(KC):
                        ins = pe.matmul(psQ[b][:, o, :], WqT[:, k, o * P:(o + 1) * P], hT[:, b, k, :],
                                        start=(k == 0), stop=(k == KC - 1))
                ins.then_inc(s_q, 1)
                if isinstance(i, int) and i == 0:
                    pe.wait_ge(s_modc, MODS)
                for k in range(KC):
                    ins = pe.matmul(psK[b][:, 0:P], WkvT[:, 0, k, :], hT[:, b, k, :],
                                    start=(k == 0), stop=(k == KC - 1))
                ins.then_inc(s_k, 1)
                wait(pe, s_vc, i - 1)
                for k in range(KC):
                    ins = pe.matmul(psV[b][:, 0:P], hT[:, b, k, :], WkvT[:, 1, k, :],
                                    start=(k == 0), stop=(k == KC - 1))
                ins.then_inc(s_v, 1)

            pe.wait_ge(s_wtc, TURNS)
            turned(0, 0)
            sweep(pe, tile)


def stack_group(sp, g, q):
    tok = slice(q * T // GROUPS, (q + 1) * T // GROUPS)
    for j in range(HPG):
        for r in range(4):
            rows, dst = slice(j * HS, (j + 1) * HS), slice(r * HS, (r + 1) * HS)
            sp.dma_start(g["Q4"][dst, j::HPG, tok], g["QT"][rows, q, r // 2]).then_inc(g["s_stacked"][q], 16)
            sp.dma_start(g["K4"][dst, j, tok], g["KT"][rows, q, r % 2]).then_inc(g["s_stacked"][q], 16)


def attention(nc, ctx, sb, ps, sem, g):
    X, V, Q4, K4, WoT = (g[k] for k in ("X", "V", "Q4", "K4", "WoT"))
    ident, LG = g["ident"], g["LG"]
    B = lambda name, shape, dt=F32: sb(name, shape, dt, ctx)
    S_AHEAD, M_AHEAD, E_AHEAD = 3, 2, 1
    U = NKV
    GROUP_DMAS = 2 * 4 * HPG
    mask = B("mask", [P, 4, SW], BF16)
    room = g["QT"][:].rearrange("p q r h n -> p (q r h n)").bitcast(F32)
    S = B("S", [P, 8, SW])
    den = B("den", [P, 8])
    nm = B("nm", [P, 8])
    PT = room[:, 0:2 * HPG * KW].rearrange("p (s j n) -> p s j n", s=2, j=HPG)
    yT, t1, xh, h2, h2t = (room[:, 2 * HPG * KW + i * C:2 * HPG * KW + (i + 1) * C] for i in range(5))
    yT, h2t = yT.rearrange("p (u n) -> p u n", u=NKV), h2t.rearrange("p (k n) -> p k n", k=KC)
    skP = B("skP", [P, 2, HPG * SINK])
    skT = B("skT", [HPG * SINK, P])
    Vs = B("Vs", [HPG * SINK, NKV, P])
    Vc = B("Vc", [P, WT, P])
    RB = B("RB", [P, 2, HPG, HS])
    rden = B("rden", [P, 2, HPG])
    s_rden = sem("a_rden")
    yU = B("yU", [P, 2, P])
    stats = B("stats2", [P, 6])
    mv = B("mv2", [P, 2])
    rstd = B("rstd2", [P, 1])
    rt = B("rt2", [P, 2])
    v8 = B("v8", [P, 8])
    i8 = B("i8", [P, 8], U32)
    lgb = B("lgb", [P, E])
    psS = [ps(f"psS{i}", [P, C], F32, ctx) for i in range(2)]
    psT = [ps(f"psTa{i}", [P, C], F32, ctx) for i in range(2)]
    psO = ps("psO", [P, C], F32, ctx)
    psA = ps("psA", [P, C], F32, ctx)
    psX = ps("psX", [P, C], F32, ctx)
    psL = ps("psL", [P, E], F32, ctx)
    (s_mask, s_vs, s_vcur, s_scores, s_masked, s_exp, s_turned, s_copied_a, s_copied_d, s_sinkw, s_sinkt, s_sinkc,
     s_rb, s_pv, s_yu, s_y, s_part, s_proj, s_res, s_x1, s_st, s_xh, s_scaled, s_h2, s_h2w, s_h2t, s_h2c, s_h2tw,
     s_logit, s_lgread, s_top) = (sem("a_" + n) for n in (
         "mask", "vs", "vcur", "scores", "masked", "exp", "turned", "copied_a", "copied_d", "sinkw", "sinkt",
         "sinkc", "rb", "pv", "yu", "y", "part", "proj", "res", "x1", "st", "xh", "scaled", "h2", "h2w", "h2t",
         "h2c", "h2tw", "logit", "lgread", "top"))
    SINK_FROM = WT - 1

    def shape_of(qt):
        if isinstance(qt, int) and qt < WT:
            return (qt + 1) * P, 0, qt, qt >= SINK_FROM
        return KW, (qt - (WT - 1)) * P, WT, True

    def ahead(qt, n, by):
        qt, n = qt + (n + by) // NH, (n + by) % NH
        return None if isinstance(qt, int) and qt >= NT else (qt, n)

    def sweep(eng, slot):
        for qt in range(WT):
            for n in range(NH):
                slot(qt, n)
        with eng.Fori(WT, NT - 1) as qt:
            for n in range(NH):
                slot(qt, n)
        for qt in range(NT - 1, NT + 2):
            for n in range(NH):
                slot(qt, n)

    def tile_in(qt, back):
        return not isinstance(qt, int) or 0 <= qt - back < NT

    with nc.Block() as block:
        @block.sync
        def _(sp):
            stack_group(sp, g, GROUPS - 1)
            sp.wait_ge(s_vs, 1)
            for j in range(HPG):
                sp.dma_start(Vs[j * SINK:(j + 1) * SINK, :, j * HS:(j + 1) * HS],
                             V[0:SINK, 0, :].rearrange("p (g d) -> p g d", g=NKV)).then_inc(s_vs, 16)
            with sp.Fori(0, NT) as i:
                sp.wait_ge(s_h2, i + 1)
                sp.dma_start(g["h2_rows"][bass.ds(i, 1)].rearrange("a p c -> p (a c)"), h2[:]).then_inc(s_h2w, 16)
                sp.wait_ge(s_h2c, i + 1)
                sp.dma_start(g["h2t_cols"][bass.ds(i, 1)].rearrange("a p k n -> p (a k) n"), h2t[:]).then_inc(s_h2tw, 16)
            sp.wait_ge(s_h2w, 16 * NT)
            sp.wait_ge(s_h2tw, 16 * NT)

        @block.gpsimd
        def _(pool):
            pool.memset(Vs[:], 0.0).then_inc(s_vs, 1)
            pool.memset(mask[:], 0.0).then_inc(s_mask, 1)
            pool.wait_ge(s_mask, 1)

            def keep(m, lo, n, base, step, mult):
                pool.affine_select(out=mask[:, m, lo:lo + n], in_=mask[:, m, lo:lo + n], compare_op=ALU.is_ge,
                                   fill=-NEG, base=base, pattern=[[step, n]], channel_multiplier=mult).then_inc(s_mask, 1)
            keep(0, 0, P, 0, -1, 1)
            keep(1, P, P, 0, -1, 1)
            keep(2, 2 * P, P, 0, -1, 1)
            keep(3, 2 * P, P, 0, -1, 1)
            keep(2, 0, P, -1, 1, -1)
            keep(3, 0, P, -1, 1, -1)
            pool.wait_ge(s_mask, 7)
            keep(2, 0, P, -SINK, 1, 0)

            def slot(qt, n):
                j, u = n % HPG, n // HPG
                if n == 2 and tile_in(qt, 0):
                    w = shape_of(qt)[0] // P
                    wait(pool, s_pv, U * qt)
                    hold(pool, g)
                    pool.tensor_copy(Vc[:, 0:w], V[:, bass.ds(qt - (w - 1), w)]).then_inc(s_vcur, 1)
                if j == 3 and tile_in(qt, 0) and shape_of(qt)[3]:
                    G, i = qt * U + u, (qt - SINK_FROM) * U + u
                    wait(pool, s_exp, (G + 1) * HPG)
                    wait(pool, s_sinkt, i - 1)
                    b = (u % 2) * HPG
                    hold(pool, g)
                    pool.tensor_copy(skP[:, u % 2].rearrange("p (j s) -> p j s", j=HPG),
                                     S[:, b:b + HPG, KW:SW]).then_inc(s_sinkw, 1)
                if n == 8 and tile_in(qt, 1):
                    Xr = X[:, bass.ds(qt - 1, 1)].rearrange("p a c -> p (a c)")
                    wait(pool, s_res, qt)
                    pool.tensor_tensor(Xr, Xr, t1[:], ALU.add).then_inc(s_x1, 1)
                if n == 15 and tile_in(qt, 1):
                    wait(pool, s_xh, qt)
                    pool.tensor_tensor(xh[:], xh[:], g["cb1_row"][:], ALU.mult).then_inc(s_scaled, 1)
                    wait(pool, s_scaled, qt)
                    wait(pool, s_h2w, 16 * (qt - 1))
                    wait(pool, s_h2t, qt - 1)
                    pool.tensor_tensor(h2[:], xh[:], g["sb_row"][:], ALU.add).then_inc(s_h2, 1)
            sweep(pool, slot)

        @block.tensor
        def _(pe):
            def scores(qt, n):
                W, k0, m, sinks = shape_of(qt)
                u = n // HPG
                wait(pe, s_masked, qt * NH + n - 1)
                q = Q4[:, n, bass.ds(qt * P, P)]
                ins = pe.matmul(psS[n % 2][:, 0:W], q, K4[:, u, bass.ds(k0, W)], start=True, stop=True)
                if sinks:
                    ins = pe.matmul(psS[n % 2][:, KW:SW], q, K4[:, u, 0:SINK], start=True, stop=True)
                ins.then_inc(s_scores, 1)

            def turn(qt, n):
                wait(pe, s_exp, qt * NH + n + 1)
                wait(pe, (s_copied_a, s_copied_d)[n % 2], qt * (NH // 2) + n // 2)
                for k in range(shape_of(qt)[0] // P):
                    ins = pe.transpose(psT[n % 2][:, k * P:(k + 1) * P], S[:, n % 8, k * P:(k + 1) * P], ident[:])
                ins.then_inc(s_turned, 1)

            def sinks_turn(qt, u):
                if shape_of(qt)[3]:
                    wait(pe, s_sinkw, (qt - SINK_FROM) * U + u + 1)
                    wait(pe, s_y, qt * U + u)
                    pe.transpose(psO[0:HPG * SINK, 2 * P:3 * P], skP[:, u % 2], ident[:]).then_inc(s_sinkt, 1)

            def products(qt, u):
                W, k0, m, sinks = shape_of(qt)
                G = qt * U + u
                wait(pe, s_y, G)
                wait(pe, s_rb, G + 1)
                if sinks:
                    wait(pe, s_sinkc, (qt - SINK_FROM) * U + u + 1)
                pe.matmul(psO[:, P:2 * P], RB[:, u % 2].rearrange("p j d -> p (j d)"), ident[:], start=True, stop=True)
                wait(pe, s_copied_a, 2 * (G + 1))
                wait(pe, s_copied_d, 2 * (G + 1))
                if u == 0:
                    wait(pe, s_vcur, qt + 1)
                if sinks:
                    if isinstance(qt, int) and qt == SINK_FROM and u == 0:
                        wait(pe, s_vs, 1 + 16 * HPG)
                    pe.matmul(psO[:, 0:P], Vs[:, u, :], skT[:], start=True, stop=False, skip_group_check=True)
                for k in range(W // P):
                    for j in range(HPG):
                        ins = pe.matmul(psO[j * HS:(j + 1) * HS, 0:P], Vc[:, k, u * HS:(u + 1) * HS],
                                        PT[:, u % 2, j, k * P:(k + 1) * P], start=(k == 0 and not sinks),
                                        stop=(k == W // P - 1), skip_group_check=True)
                ins.then_inc(s_pv, 1)

            def project(qt, u):
                wait(pe, s_y, qt * U + u + 1)
                if u == 0:
                    wait(pe, s_res, qt)
                ins = pe.matmul(psA[:], yT[:, u, :], WoT[:, u, :], start=(u == 0), stop=(u == U - 1))
                ins.then_inc(s_part, 1)

            def slot(qt, n):
                j, u = n % HPG, n // HPG
                if tile_in(qt, 0):
                    turn(qt, n)
                if isinstance(qt, int) and qt == 1 and n == 0:
                    for q in range(1, GROUPS):
                        pe.wait_ge(g["s_stacked"][q], GROUP_DMAS * 16)
                if h := ahead(qt, n, S_AHEAD):
                    scores(*h)
                back, v = (0, u - 1) if u else (1, U - 1)
                if j == 0 and tile_in(qt, back):
                    sinks_turn(qt - back, v)
                if j == 1 and tile_in(qt, back):
                    products(qt - back, v)
                back, v = (0, u - 2) if u >= 2 else (1, u + U - 2)
                if j == 0 and tile_in(qt, back):
                    project(qt - back, v)
                if n == 2 and tile_in(qt, 2):
                    wait(pe, s_h2, qt - 1)
                    wait(pe, s_h2c, qt - 2)
                    for k in range(KC):
                        ins = pe.transpose(psX[:, k * P:(k + 1) * P], h2[:, k::KC], ident[:])
                    ins.then_inc(s_h2t, 1)
                if n == 7 and tile_in(qt, 2):
                    wait(pe, s_h2c, qt - 1)
                    wait(pe, s_lgread, qt - 2)
                    for k in range(KC):
                        ins = pe.matmul(psL[:], h2t[:, k, :], g["rw"][:, k, :], start=(k == 0), stop=(k == KC - 1))
                    ins.then_inc(s_logit, 1)

            pe.wait_ge(g["s_stacked"][0], GROUP_DMAS * 16)
            pe.wait_ge(g["s_in"][8], 16)
            for n in range(S_AHEAD):
                scores(0, n)
            sweep(pe, slot)

        @block.scalar
        def _(act):
            def exps(qt, n):
                W, k0, m, sinks = shape_of(qt)
                wait(act, s_masked, qt * NH + n + 1)
                wait(act, s_rb, qt * U + n // HPG - 1)
                w = SW if sinks else W
                act.activation(S[:, n % 8, 0:w], S[:, n % 8, 0:w], ACT.Exp, bias=nm[:, n % 8:n % 8 + 1], scale=-1.0,
                               accum_out=den[:, n % 8:n % 8 + 1]).then_inc(s_exp, 1)

            def copy(qt, n):
                W = shape_of(qt)[0]
                wait(act, s_turned, qt * NH + n + 1)
                wait(act, s_pv, qt * U + n // HPG - 1)
                act.activation(PT[:, (n // HPG) % 2, n % HPG, 0:W], psT[0][:, 0:W], ACT.Copy).then_inc(s_copied_a, 1)

            def slot(qt, n):
                j, u = n % HPG, n // HPG
                if h := ahead(qt, n, E_AHEAD):
                    exps(*h)
                if n % 2 == 1 and tile_in(qt, 0):
                    copy(qt, n - 1)
                back, v = (0, u - 1) if u else (1, U - 1)
                if j == 2 and tile_in(qt, back):
                    G = (qt - back) * U + v
                    wait(act, s_pv, G + 1)
                    wait(act, s_y, G - 1)
                    act.activation(yU[:, v % 2, :], psO[:, 0:P], ACT.Copy).then_inc(s_yu, 1)
                if n == 4 and tile_in(qt, 2):
                    wait(act, s_h2t, qt - 1)
                    wait(act, s_logit, qt - 2)
                    wait(act, s_h2tw, 16 * (qt - 2))
                    act.activation(h2t[:].rearrange("p k n -> p (k n)"), psX[:], ACT.Copy).then_inc(s_h2c, 1)

            for n in range(E_AHEAD):
                exps(0, n)
            sweep(act, slot)

        @block.vector
        def _(dve):
            def masked(qt, n):
                W, k0, m, sinks = shape_of(qt)
                w = SW if sinks else W
                N = qt * NH + n
                wait(dve, s_scores, N + 1)
                wait(dve, s_turned, N - 7)
                if n % HPG == 0 and not (isinstance(qt, int) and qt <= SINK_FROM and n < 8):
                    wait(dve, s_sinkw, (qt - SINK_FROM) * U + n // HPG - 1)
                hold(dve, g)
                dve.tensor_tensor_reduce(S[:, n % 8, 0:w], psS[n % 2][:, 0:w], mask[:, m, 0:w], 1.0, 3e38,
                                         ALU.add, ALU.min, nm[:, n % 8:n % 8 + 1]).then_inc(s_masked, 1)

            def copy(qt, n):
                W = shape_of(qt)[0]
                wait(dve, s_turned, qt * NH + n + 1)
                wait(dve, s_pv, qt * U + n // HPG - 1)
                dve.tensor_copy(PT[:, (n // HPG) % 2, n % HPG, 0:W], psT[1][:, 0:W]).then_inc(s_copied_d, 1)

            STEPS = 14

            def step(ins):
                ins.then_inc(s_st, 1)

            def since(qt, k):
                wait(dve, s_st, (qt - 1) * STEPS + k)

            def norm_steps(qt, n):
                v, t, y = rt[:, 0:1], rt[:, 1:2], rstd[:]
                if n == 9:
                    wait(dve, s_x1, qt)
                    hold(dve, g)
                    step(dve.bn_stats(stats[:], X[:, bass.ds(qt - 1, 1)].rearrange("p a c -> p (a c)")))
                    since(qt, 1)
                    hold(dve, g)
                    step(dve.bn_aggr(mv[:], stats[:]))
                    since(qt, 2)
                    step(dve.tensor_scalar(v, mv[:, 1:2], EPS, None, ALU.add))
                if n == 10:
                    since(qt, 3)
                    step(dve.tensor_scalar(t.bitcast(I32), v.bitcast(I32), 1, None, ALU.arith_shift_right))
                    since(qt, 4)
                    step(dve.tensor_scalar(y.bitcast(I32), t.bitcast(I32), -1.0, float(0x5F3759DF), ALU.mult, ALU.add))
                if 11 <= n <= 13:
                    k = 5 + 3 * (n - 11)
                    since(qt, k)
                    step(dve.scalar_tensor_tensor(out=t, in0=y, scalar=v, in1=y, op0=ALU.mult, op1=ALU.mult))
                    since(qt, k + 1)
                    step(dve.tensor_scalar(t, t, -0.5, 1.5, ALU.mult, ALU.add))
                    since(qt, k + 2)
                    step(dve.tensor_tensor(y, y, t, ALU.mult))
                if n == 14:
                    since(qt, 14)
                    wait(dve, s_h2, qt - 1)
                    dve.tensor_scalar(xh[:], X[:, bass.ds(qt - 1, 1)].rearrange("p a c -> p (a c)"), mv[:, 0:1], y,
                                      ALU.subtract, ALU.mult).then_inc(s_xh, 1)

            def top_steps(qt, n):
                lg = LG[:, bass.ds(qt - 2, 1)].rearrange("p a c -> p (a c)")

                def since_top(k):
                    wait(dve, s_top, (qt - 2) * 3 + k)
                if n == 9:
                    wait(dve, s_logit, qt - 1)
                    dve.tensor_copy(lg, psL[:]).then_inc(s_lgread, 1)
                if n == 10:
                    wait(dve, s_lgread, qt - 1)
                    dve.tensor_tensor(lgb[:], lg, g["rbias"][:], ALU.add).then_inc(s_top, 1)
                if n == 11:
                    since_top(1)
                    hold(dve, g)
                    dve.max(v8[:], lgb[:]).then_inc(s_top, 1)
                if n == 12:
                    since_top(2)
                    hold(dve, g)
                    dve.max_index(i8[:], v8[:], lgb[:]).then_inc(s_top, 1)
                if n == 13:
                    since_top(3)
                    dve.tensor_copy(g["EIDX"][:, bass.ds(qt - 2, 1)].rearrange("p a c -> p (a c)"), i8[:])

            def slot(qt, n):
                j, u = n % HPG, n // HPG
                if h := ahead(qt, n, M_AHEAD):
                    masked(*h)
                back, v = (0, u - 1) if u else (1, U - 1)
                if j == 0 and tile_in(qt, back):
                    G = (qt - back) * U + v
                    wait(dve, s_exp, (G + 1) * HPG)
                    wait(dve, s_pv, G - 1)
                    b = (v % 2) * HPG
                    dve.reciprocal(rden[:, v % 2], den[:, b:b + HPG]).then_inc(s_rden, 1)
                if n % 2 == 0 and n and tile_in(qt, 0):
                    copy(qt, n - 1)
                if n == 0 and tile_in(qt, 1):
                    copy(qt - 1, NH - 1)
                if j == 0 and tile_in(qt, back):
                    wait(dve, s_rden, G + 1)
                    dve.tensor_copy(RB[:, v % 2], rden[:, v % 2].unsqueeze(2).broadcast_to([P, HPG, HS])).then_inc(s_rb, 1)
                if j == 0 and tile_in(qt, back) and shape_of(qt - back)[3]:
                    G, i = (qt - back) * U + v, (qt - back - SINK_FROM) * U + v
                    wait(dve, s_sinkt, i + 1)
                    wait(dve, s_pv, G)
                    dve.tensor_copy(skT[:], psO[0:HPG * SINK, 2 * P:3 * P]).then_inc(s_sinkc, 1)
                if j == 3 and tile_in(qt, back):
                    G = (qt - back) * U + v
                    wait(dve, s_yu, G + 1)
                    wait(dve, s_part, G - 3)
                    dve.tensor_tensor(yT[:, v, :], yU[:, v % 2, :], psO[:, P:2 * P], ALU.mult).then_inc(s_y, 1)
                if n == 6 and tile_in(qt, 1):
                    wait(dve, s_part, qt * U)
                    wait(dve, s_x1, qt - 1)
                    dve.tensor_tensor(t1[:], psA[:], g["ga_row"][:], ALU.mult).then_inc(s_res, 1)
                if tile_in(qt, 1):
                    norm_steps(qt, n)
                if tile_in(qt, 2):
                    top_steps(qt, n)

            dve.wait_ge(s_mask, 8)
            dve.wait_ge(g["s_in"][9], 16)
            for n in range(M_AHEAD):
                masked(0, n)
            sweep(dve, slot)


def shared_experts(nc, ctx, sb, ps, sem, g):
    X, LG, EIDX, GATE, POSI = (g[k] for k in ("X", "LG", "EIDX", "GATE", "POSI"))
    B = lambda name, shape, dt=F32: sb(name, shape, dt, ctx)
    GT = 4
    NG = NT // GT
    NCH = SH * HC
    STEPS = NG * NCH
    WG = B("WG", [P, SH, KC, HC * P])
    WU = B("WU", [P, SH, KC, HC * P])
    WD = B("WD", [P, SH, HC, C])
    HT = B("HT", [P, 2, GT, KC, P])
    sg = B("sg", [P, 2, C])
    hid = B("hid", [P, NCH, C])
    tmp = B("tmp", [P, 2, C])
    psG = [ps(f"psG{i}", [P, C], F32, ctx) for i in range(2)]
    psU = [ps(f"psU{i}", [P, C], F32, ctx) for i in range(2)]
    psY = [ps(f"psY{i}", [P, C], F32, ctx) for i in range(2)]
    s_w = [sem(f"h_w{i}") for i in range(3)]
    s_ht = [sem(f"h_ht{i}") for i in range(2)]
    s_gate, s_up, s_silu, s_hid, s_down, s_add, s_t = (sem("h_" + n) for n in ("gate", "up", "silu", "hid", "down", "add", "t"))

    iota_i = B("iota_i", [P, P], I32)
    iota_e = B("iota_e", [P, P])
    iota_pi = B("iota_pi", [P, 1], I32)
    iota_p = B("iota_p", [P, 1])
    before = B("before", [P, P])
    OH = B("OH", [P, NT, TOPK, E])
    PR = B("PR", [P, NT, TOPK, E])
    M = B("M", [P, NT, E])
    MP = B("MP", [P, NT + 1, E])
    R = B("R", [P, NT, E])
    cnt_i = B("cnt_i", [P, E], I32)
    tiles = B("tiles", [P, E])
    incl = B("incl", [P, E])
    base = B("base", [P, E])
    lk = B("lk", [P, NT, TOPK])
    mxk = B("mxk", [P, NT])
    sumk = B("sumk", [P, NT])
    posf = B("posf", [P, NT, TOPK])
    eid_f = B("eid_f", [P, 1])
    eid_i = B("eid_i", [P, 1], I32)
    cmp_e = B("cmp_e", [P, E])
    slot_i = B("slot_i", [P, 2, NT, TOPK], I32)
    slot_f = B("slot_f", [P, 2, NT, TOPK])
    place = B("place", [P, 2, TOPK, P], BF16)
    where = B("where", [P, 2, TOPK, P])
    token = B("token", [P, 2, 2, TOPK, P], BF16)
    psR = [ps(f"psR{i}", [P, C], F32, ctx) for i in range(2)]
    s_iota, s_bef, s_cnt, s_rank, s_d, s_lk, s_ek, s_eid, s_seen, s_place, s_table, s_toks = (
        sem("d_" + n) for n in ("iota", "bef", "cnt", "rank", "d", "lk", "ek", "eid", "seen", "place", "table", "toks"))
    COUNT_AT, RANK_AT, TABLE_AT = 5, 8, 16

    with nc.Block() as block:
        @block.sync
        def _(sp):
            sp.dma_start(WG[:], g["swg"].rearrange("s (p k) h -> p s k h", k=KC)).then_inc(s_w[0], 16)
            sp.dma_start(WU[:], g["swu"].rearrange("s (p k) h -> p s k h", k=KC)).then_inc(s_w[1], 16)
            for n in range(NG):
                if n >= 2:
                    sp.wait_ge(s_up, NCH * (n - 1))
                for t in range(GT):
                    sp.dma_start(HT[:, n % 2, t], g["h2t_cols"][n * GT + t]).then_inc(s_ht[n % 2], 16)
                if n == 0:
                    sp.dma_start(WD[:], g["swd"].rearrange("s (c p) n -> p s c n", p=P)).then_inc(s_w[2], 16)
            sp.wait_ge(s_eid, 1)
            sp.dma_start(g["tile_expert"].rearrange("a p -> p a"), eid_i[:]).then_inc(g["s_tile_expert"], 16)
            sp.wait_ge(g["s_tile_expert"], 16)
            sp.dma_start(g["eid_row"][:], g["tile_expert"]).then_inc(g["s_tile_expert"], 16)
            sp.wait_ge(g["s_tile_expert"], 32)

        @block.tensor
        def _(pe):
            pe.wait_ge(s_w[0], 16)
            pe.wait_ge(s_w[1], 16)

            def up(n, c):
                i = n * NCH + c
                for w, bank, done in ((WG, psG, s_gate), (WU, psU, s_up)):
                    if i >= 2:
                        pe.wait_ge(s_hid, i - 1)
                    for k in range(KC):
                        ins = pe.matmul(bank[i % 2][:].rearrange("p (t n) -> p t n", t=GT),
                                        w[:, c // HC, k, (c % HC) * P:(c % HC + 1) * P],
                                        HT[:, n % 2, :, k, :], start=(k == 0), stop=(k == KC - 1))
                    ins.then_inc(done, 1)

            def dispatch_step(m):
                if m == COUNT_AT:
                    pe.wait_ge(s_cnt, 1)
                    pe.wait_ge(s_bef, 2)
                    pe.matmul(psR[0][:, 0:E], g["ones"][:], MP[:, NT, :], start=True, stop=True).then_inc(s_rank, 1)
                if m == RANK_AT:
                    for h in (1, 0):
                        if h == 0:
                            pe.wait_ge(s_seen, 1)
                        t = slice(h * NT // 2, (h + 1) * NT // 2)
                        bank = psR[h][:].rearrange("p (t e) -> p t e", e=E)
                        pe.matmul(bank, before[:], M[:, t, :], start=True, stop=False)
                        pe.matmul(bank, g["ones"][:], MP[:, t, :], start=False, stop=True).then_inc(s_rank, 1)
                if m > TABLE_AT:
                    t = m - TABLE_AT - 1
                    if t == 0:
                        pe.wait_ge(s_seen, 2)
                    pe.wait_ge(s_place, t + 1)
                    for k in range(TOPK):
                        for half in range(2):
                            ins = pe.matmul(psR[1][:, 0:P], place[:, t % 2, k], token[:, t % 2, half, k],
                                            start=(t + k + half == 0), stop=(t == NT - 1 and k == TOPK - 1 and half == 1))
                    ins.then_inc(s_table, 1)

            for n in range(NG):
                pe.wait_ge(s_ht[n % 2], 16 * GT * (n // 2 + 1))
                for c in range(NCH):
                    up(n, c)
                    dispatch_step(n * NCH + c)
                if n == NG - 1:
                    dispatch_step(STEPS)
                if n == 0:
                    pe.wait_ge(s_w[2], 16)
                pe.wait_ge(s_hid, NCH * (n + 1))
                for t in range(GT):
                    i = n * GT + t
                    if i >= 2:
                        pe.wait_ge(s_add, i - 1)
                    for c in range(NCH):
                        ins = pe.matmul(psY[i % 2][:], hid[:, c, t * P:(t + 1) * P], WD[:, c // HC, c % HC, :],
                                        start=(c == 0), stop=(c == NCH - 1))
                    ins.then_inc(s_down, 1)

        @block.scalar
        def _(act):
            for i in range(STEPS):
                act.wait_ge(s_gate, i + 1)
                if i >= 2:
                    act.wait_ge(s_hid, i - 1)
                act.activation(sg[:, i % 2], psG[i % 2][:], ACT.Silu).then_inc(s_silu, 1)
                if i == RANK_AT:
                    act.wait_ge(s_lk, 1)
                    act.activation(lk[:], lk[:], ACT.Exp).then_inc(s_ek, 1)

        @block.vector
        def _(dve):
            ch = Chain(dve, s_d)

            def dispatch_step(m):
                if m == 0:
                    dve.wait_ge(s_iota, 2)
                    ch.step(dve.tensor_copy(iota_e[:], iota_i[:]))
                    ch.step(dve.tensor_copy(iota_p[:], iota_pi[:]))
                    ch.step(dve.memset(MP[:, 0, :], 0.0))
                    ch.last()
                if m < 2:
                    for k in (2 * m, 2 * m + 1):
                        ch.step(dve.tensor_tensor(OH[:, :, k, :], iota_e[:, 0:E].unsqueeze(1).broadcast_to([P, NT, E]),
                                                  EIDX[:, :, k:k + 1].broadcast_to([P, NT, E]), ALU.is_equal))
                if m == 2:
                    ch.last()
                    ch.step(dve.tensor_tensor(M[:], OH[:, :, 0, :], OH[:, :, 1, :], ALU.add))
                    for k in range(2, TOPK):
                        ch.last()
                        ch.step(dve.tensor_tensor(M[:], M[:], OH[:, :, k, :], ALU.add))
                if m == 3:
                    for t in range(NT):
                        ch.last()
                        ins = dve.tensor_tensor(MP[:, t + 1, :], MP[:, t, :], M[:, t, :], ALU.add)
                        if t < NT - 1:
                            ch.step(ins)
                    ins.then_inc(s_cnt, 1)
                if 4 <= m < 6:
                    for k in (2 * (m - 4), 2 * (m - 4) + 1):
                        ch.step(dve.tensor_tensor(PR[:, :, k, :], OH[:, :, k, :], LG[:], ALU.mult))
                if m == 6:
                    ch.last()
                    ch.step(dve.tensor_reduce(lk[:], PR[:], AX.X, ALU.add))
                if m == 7:
                    ch.last()
                    ch.step(dve.tensor_reduce(mxk[:], lk[:], AX.X, ALU.max))
                    ch.last()
                    dve.tensor_tensor(lk[:], lk[:], mxk[:].unsqueeze(2).broadcast_to([P, NT, TOPK]), ALU.subtract).then_inc(s_lk, 1)
                if m == 9:
                    dve.wait_ge(s_ek, 1)
                    ch.step(dve.tensor_reduce(sumk[:], lk[:], AX.X, ALU.add))
                    ch.last()
                    ch.step(dve.reciprocal(sumk[:], sumk[:]))
                    ch.last()
                    ch.step(dve.tensor_tensor(GATE[:], lk[:], sumk[:].unsqueeze(2).broadcast_to([P, NT, TOPK]), ALU.mult))
                if m == 8:
                    dve.wait_ge(s_rank, 1)
                    dve.tensor_scalar(cnt_i[:], psR[0][:, 0:E], 1.0, float(P - 1), ALU.max, ALU.add).then_inc(s_seen, 1)
                    dve.wait_ge(s_seen, 1)
                    ch.step(dve.tensor_scalar(cnt_i[:], cnt_i[:], 7, None, ALU.arith_shift_right))
                    ch.last()
                    ch.step(dve.tensor_copy(tiles[:], cnt_i[:]))
                    ch.step(dve.memset(base[:], 1.0))
                    ch.last()
                    ch.step(dve.tensor_tensor_scan(incl[:], base[:], tiles[:], 0.0, ALU.mult, ALU.add))
                    ch.last()
                    ch.step(dve.tensor_tensor(base[:], incl[:], tiles[:], ALU.subtract))
                    ch.step(dve.tensor_copy(g["end_row"][:], incl[0:1, :]))
                    ch.step(dve.tensor_scalar(g["pairs"][:], incl[0:1, E - 1:E], 1.0, None, ALU.add))
                    ch.last()
                    ch.step(dve.tensor_scalar(g["pairs"][:], g["pairs"][:], 1, None, ALU.arith_shift_right))
                if m == 10:
                    ch.step(dve.tensor_scalar(cmp_e[:], incl[:], iota_p[:], None, ALU.is_le))
                    ch.last()
                    ch.step(dve.tensor_reduce(eid_f[:], cmp_e[:], AX.X, ALU.add))
                    ch.step(dve.tensor_scalar(base[:], base[:], float(P), None, ALU.mult))
                    ch.last()
                    dve.tensor_scalar(eid_i[:], eid_f[:], float(E - 1), None, ALU.min).then_inc(s_eid, 1)
                if m == 11:
                    dve.wait_ge(s_rank, 3)
                    for h in range(2):
                        t = slice(h * NT // 2, (h + 1) * NT // 2)
                        ins = dve.tensor_tensor(R[:, t, :], psR[h][:].rearrange("p (t e) -> p t e", e=E),
                                                base[:].unsqueeze(1).broadcast_to([P, NT // 2, E]), ALU.add)
                        if h == 0:
                            ch.step(ins)
                    ins.then_inc(s_seen, 1)
                    dve.wait_ge(s_seen, 2)
                if 12 <= m < 14:
                    ch.last()
                    for k in (2 * (m - 12), 2 * (m - 12) + 1):
                        ch.step(dve.tensor_tensor(PR[:, :, k, :], OH[:, :, k, :], R[:], ALU.mult))
                if m == 14:
                    ch.last()
                    ch.step(dve.tensor_reduce(posf[:], PR[:], AX.X, ALU.add))
                if m == 15:
                    ch.last()
                    ch.step(dve.tensor_copy(POSI[:], posf[:]))
                    ch.last()
                    ch.step(dve.tensor_scalar(slot_i[:, 0], POSI[:], 7, None, ALU.arith_shift_right))
                    ch.step(dve.tensor_scalar(slot_i[:, 1], POSI[:], P - 1, None, ALU.bitwise_and))
                    ch.last()
                    ch.step(dve.tensor_copy(slot_f[:], slot_i[:]))
                if m >= TABLE_AT:
                    t = m - TABLE_AT
                    ch.last()
                    if t >= 2:
                        dve.wait_ge(s_table, t - 1)
                    columns = iota_e[:].unsqueeze(1).broadcast_to([P, TOPK, P])
                    dve.tensor_tensor(place[:, t % 2], columns,
                                      slot_f[:, 1, t, :].unsqueeze(2).broadcast_to([P, TOPK, P]), ALU.is_equal)
                    ch.step(dve.tensor_tensor(where[:, t % 2], columns,
                                              slot_f[:, 0, t, :].unsqueeze(2).broadcast_to([P, TOPK, P]), ALU.is_equal))
                    ch.last()
                    ch.step(dve.tensor_scalar(token[:, t % 2, 0], where[:, t % 2], iota_p[:], None, ALU.mult))
                    dve.tensor_scalar(token[:, t % 2, 1], where[:, t % 2], float(t * P), None, ALU.mult).then_inc(s_place, 1)

            for n in range(NG):
                if n:
                    dve.wait_ge(s_down, GT * n)
                for c in range(NCH):
                    i = n * NCH + c
                    dve.wait_ge(s_silu, i + 1)
                    dve.wait_ge(s_up, i + 1)
                    dve.tensor_tensor(hid[:, c], sg[:, i % 2], psU[i % 2][:], ALU.mult).then_inc(s_hid, 1)
                    dispatch_step(i)
                if n == NG - 1:
                    dve.memset(g["TOKI"][:, MAXT:], 0).then_inc(s_toks, 1)
                    dve.wait_ge(s_table, NT)
                    dve.tensor_copy(g["TOKI"][:, 0:MAXT], psR[1][:, 0:P]).then_inc(s_toks, 1)
                for t in range(GT):
                    i = n * GT + t
                    dve.wait_ge(s_down, i + 1)
                    if i >= 2:
                        dve.wait_ge(s_t, i - 1)
                    dve.tensor_tensor(tmp[:, i % 2], psY[i % 2][:], g["gb_row"][:], ALU.mult).then_inc(s_add, 1)

        @block.gpsimd
        def _(pool):
            pool.iota(iota_i[:], pattern=[[1, P]], base=0, channel_multiplier=0).then_inc(s_iota, 1)
            pool.iota(iota_pi[:], pattern=[[0, 1]], base=0, channel_multiplier=1).then_inc(s_iota, 1)
            pool.memset(before[:], 1.0).then_inc(s_bef, 1)
            pool.wait_ge(s_bef, 1)
            pool.affine_select(out=before[:], in_=before[:], compare_op=ALU.is_ge, fill=0.0, base=-1,
                               pattern=[[1, P]], channel_multiplier=-1).then_inc(s_bef, 1)
            for i in range(NT):
                pool.wait_ge(s_add, i + 1)
                pool.tensor_tensor(X[:, i], X[:, i], tmp[:, i % 2], ALU.add).then_inc(s_t, 1)


def routed_experts(nc, ctx, sb, ps, sem, g):
    B = lambda name, shape, dt=F32: sb(name, shape, dt, ctx)
    RING = 8
    ident = g["ident"]
    W = B("W", [P, RING, 2, KC, F])
    WD = B("rWD", [P, RING, C])
    XT = B("rX", [P, 2, C])
    xT = B("rxT", [P, 2, KC, P])
    sg = B("rsg", [P, 2, F])
    hid = B("rhid", [P, 2, F])
    hT = B("rhT", [P, 2, P])
    Y = B("rY", [P, 2, C])
    nothing = B("nothing", [P, C])
    psX = [ps(f"rpX{i}", [P, KC * P], F32, ctx) for i in range(2)]
    psGU = [ps(f"rpG{i}", [P, 2, F], F32, ctx) for i in range(2)]
    psH = ps("rpH", [P, P], F32, ctx)
    psY = [ps(f"rpY{i}", [P, C], F32, ctx) for i in range(2)]
    s_w = [sem(f"r_w{i}") for i in range(RING)]
    s_x = [sem(f"r_x{i}") for i in range(2)]
    s_yo = [sem(f"r_yo{i}") for i in range(2)]
    ends = B("ends", [1, RING], I32)
    tok = B("tok", [P, 2], I32)
    s_nothing, s_ends, s_tok, s_empty = (sem("r_" + n) for n in ("nothing", "ends", "tok", "empty"))
    s_wready, s_tr, s_xt, s_gu, s_silu, s_h, s_ht, s_hc, s_down, s_y = (
        sem("r_" + n) for n in ("wready", "tr", "xt", "gu", "silu", "h", "ht", "hc", "down", "y"))
    wg_v = g["wg"].rearrange("e (p k) f -> e p (k f)", k=KC)
    wu_v = g["wu"].rearrange("e (p k) f -> e p (k f)", k=KC)
    MAXPAIRS, MINPAIRS = MAXT // 2, E // 2

    def sweep(eng, step, drain):
        pairs = eng.value_load(g["pairs"][0:1, 0:1], min_val=MINPAIRS, max_val=MAXPAIRS)
        for h in range(2):
            for b in range(2):
                step(h, b)
        with eng.Fori(2, MINPAIRS - 1) as h:
            for b in range(2):
                step(h, b)
        with eng.Fori(MINPAIRS - 1, MAXPAIRS) as h:
            with eng.If(h < pairs):
                for b in range(2):
                    step(h, b)
            with eng.If(h + 1 == pairs):
                drain(h + 1)
        return pairs

    with nc.Block() as block:
        @block.sync
        def _(sp):
            def load(i, b):
                e = i * RING + b
                if not (isinstance(i, int) and i == 0):
                    sp.wait_ge(s_down, sp.value_load(ends[0:1, b:b + 1], min_val=1, max_val=MAXT))
                one = bass.ds(e, 1)
                sp.dma_start(W[:, b, 0].rearrange("p k f -> p (k f)"), wg_v[one].rearrange("a p n -> (a p) n")).then_inc(s_w[b], 16)
                sp.dma_start(W[:, b, 1].rearrange("p k f -> p (k f)"), wu_v[one].rearrange("a p n -> (a p) n")).then_inc(s_w[b], 16)
                sp.dma_start(WD[:, b], g["wd"][one].rearrange("a p n -> (a p) n")).then_inc(s_w[b], 16)

            def landed(i, b):
                sp.wait_ge(s_w[b], 48 * (i + 1))
                sp.sem_inc(s_wready, 1)

            LAG = RING // 2
            for b in range(RING):
                load(0, b)
                if b >= LAG:
                    landed(0, b - LAG)
            with sp.Fori(1, E // RING) as i:
                sp.dma_start(ends[:], g["end_row"][0:1, bass.ds((i - 1) * RING, RING)]).then_inc(s_ends, 16)
                sp.wait_ge(s_ends, 16 * i)
                hold(sp, g)
                for b in range(RING):
                    load(i, b)
                    if b >= LAG:
                        landed(i, b - LAG)
                    else:
                        landed(i - 1, b + RING - LAG)
            for b in range(RING - LAG, RING):
                landed(E // RING - 1, b)
            pairs = sp.value_load(g["pairs"][0:1, 0:1], min_val=MINPAIRS, max_val=MAXPAIRS)
            sp.wait_ge(s_nothing, 1)
            with sp.Fori(MINPAIRS, MAXPAIRS) as h:
                with sp.If(h >= pairs):
                    for b in range(2):
                        sp.dma_start(g["slot_y"][bass.ds((h * 2 + b) * P, P), :], nothing[:]).then_inc(s_empty, 16)
                with sp.If(h < pairs):
                    sp.sem_inc(s_empty, 32)
            sp.wait_ge(s_empty, (MAXPAIRS - MINPAIRS) * 32)

        @block.gpsimd
        def _(pool):
            def gather(h, t, b):
                wait(pool, s_tr, t - 1)
                hold(pool, g)
                pool.tensor_copy(tok[:, b:b + 1], g["TOKI"][:, bass.ds(t, 1)]).then_inc(s_tok, 1)
                pool.wait_ge(s_tok, t + 1)
                hold(pool, g)
                pool.indirect_dma_start(out=XT[:, b], out_offset=None, in_=g["h2_rows"].rearrange("t p c -> (t p) c"),
                                        in_offset=bass.IndirectOffsetOnAxis(ap=tok[:, b:b + 1], axis=0)).then_inc(s_x[b], 16)

            def step(h, b):
                gather(h + 1, h * 2 + b + 2, b)

            def drain(pairs):
                for b in range(2):
                    pool.wait_ge(s_x[b], pairs * 16 + 16)
                    hold(pool, g)
            pool.memset(nothing[:], 0.0).then_inc(s_nothing, 1)
            for b in range(2):
                gather(0, b, b)
            sweep(pool, step, drain)

        @block.tensor
        def _(pe):
            def expert(t):
                return pe.value_load(g["eid_row"][0:1, bass.ds(t, 1)], min_val=0, max_val=E - 1)

            def rows(h, t, b):
                pe.wait_ge(s_x[b], 16 * (h + 1))
                wait(pe, s_xt, t - 1)
                for k in range(KC):
                    ins = pe.transpose(psX[b][:, k * P:(k + 1) * P], XT[:, b, k::KC], ident[:])
                ins.then_inc(s_tr, 1)

            def gate_up(t, b, e):
                pe.wait_ge(s_wready, e + 1)
                pe.wait_ge(s_xt, t + 1)
                wait(pe, s_h, t - 1)
                slot = bass.ds(e % RING, 1)
                for k in range(KC):
                    ins = pe.matmul(psGU[b][:], xT[:, b, k, :], W[:, slot, :, k, :].rearrange("p a s f -> p (a s) f"),
                                    start=(k == 0), stop=(k == KC - 1))
                ins.then_inc(s_gu, 1)

            def hidden(t, b):
                pe.wait_ge(s_h, t + 1)
                wait(pe, s_hc, t)
                pe.transpose(psH[:], hid[:, b], ident[:]).then_inc(s_ht, 1)

            def down(t, b, e):
                pe.wait_ge(s_hc, t + 1)
                wait(pe, s_y, t - 1)
                pe.matmul(psY[b][:], hT[:, b], WD[:, bass.ds(e % RING, 1)].rearrange("p a n -> p (a n)"),
                          start=True, stop=True).then_inc(s_down, 1)

            def step(h, b):
                t = h * 2 + b
                e1 = None if isinstance(h, int) and t == 0 else expert(t - 1)
                e2 = None if isinstance(h, int) and h == 0 else expert(t - 2)
                rows(h, t, b)
                if e2 is not None:
                    hidden(t - 2, b)
                if e1 is not None:
                    gate_up(t - 1, 1 - b, e1)
                if e2 is not None:
                    down(t - 2, b, e2)

            def drain(pairs):
                T2 = pairs * 2
                e1, e2 = expert(T2 - 1), expert(T2 - 2)
                hidden(T2 - 2, 0)
                gate_up(T2 - 1, 1, e1)
                down(T2 - 2, 0, e2)
                hidden(T2 - 1, 1)
                down(T2 - 1, 1, e1)
            sweep(pe, step, drain)

        @block.scalar
        def _(act):
            def rows(t, b):
                act.wait_ge(s_tr, t + 1)
                wait(act, s_gu, t - 1)
                act.activation(xT[:, b].rearrange("p k n -> p (k n)"), psX[b][:], ACT.Copy).then_inc(s_xt, 1)

            def silu(t, b):
                act.wait_ge(s_gu, t + 1)
                wait(act, s_h, t - 1)
                act.activation(sg[:, b], psGU[b][:, 0, :], ACT.Silu).then_inc(s_silu, 1)

            def store(t, b):
                act.wait_ge(s_y, t + 1)
                act.dma_start(g["slot_y"][bass.ds(t * P, P), :], Y[:, b]).then_inc(s_yo[b], 16)

            def step(h, b):
                t = h * 2 + b
                rows(t, b)
                if not (isinstance(h, int) and (h == 0 or t == 2)):
                    store(t - 3, 1 - b)
                if not (isinstance(h, int) and t == 0):
                    silu(t - 1, 1 - b)

            def drain(pairs):
                T2 = pairs * 2
                store(T2 - 3, 1)
                silu(T2 - 1, 1)
                for b in range(2):
                    store(T2 - 2 + b, b)
                for b in range(2):
                    act.wait_ge(s_yo[b], pairs * 16)
                    hold(act, g)
            sweep(act, step, drain)

        @block.vector
        def _(dve):
            def mult(t, b):
                dve.wait_ge(s_silu, t + 1)
                wait(dve, s_ht, t - 1)
                dve.tensor_tensor(hid[:, b], sg[:, b], psGU[b][:, 1, :], ALU.mult).then_inc(s_h, 1)

            def hidden(t, b):
                dve.wait_ge(s_ht, t + 1)
                wait(dve, s_down, t - 1)
                dve.tensor_copy(hT[:, b], psH[:]).then_inc(s_hc, 1)

            def output(h, t, b):
                dve.wait_ge(s_down, t + 1)
                wait(dve, s_yo[b], 16 * (h - 1))
                dve.tensor_tensor(Y[:, b], psY[b][:], g["gb_row"][:], ALU.mult).then_inc(s_y, 1)

            def step(h, b):
                t = h * 2 + b
                if not (isinstance(h, int) and h == 0):
                    hidden(t - 2, b)
                if not (isinstance(h, int) and t == 0):
                    mult(t - 1, 1 - b)
                if not (isinstance(h, int) and h == 0):
                    output(h, t - 2, b)

            def drain(pairs):
                T2 = pairs * 2
                hidden(T2 - 2, 0)
                mult(T2 - 1, 1)
                output(pairs, T2 - 2, 0)
                hidden(T2 - 1, 1)
                output(pairs, T2 - 1, 1)
            sweep(dve, step, drain)


def combine(nc, ctx, sb, ps, sem, g):
    X, GATE, POSI = (g[k] for k in ("X", "GATE", "POSI"))
    B = lambda name, shape, dt=F32: sb(name, shape, dt, ctx)
    NB = 4
    YR = B("YR", [P, NB, TOPK, C])
    s_rows = [sem(f"c_rows{i}") for i in range(NB)]
    s_c, s_sum, s_out = (sem("c_" + n) for n in ("c", "sum", "out"))
    with nc.Block() as block:
        @block.gpsimd
        def _(pool):
            for t in range(NT):
                b = t % NB
                wait(pool, s_sum, t - NB + 1)
                for k in range(TOPK):
                    pool.indirect_dma_start(out=YR[:, b, k, :], out_offset=None, in_=g["slot_y"],
                                            in_offset=bass.IndirectOffsetOnAxis(ap=POSI[:, t, k:k + 1], axis=0)).then_inc(s_rows[b], 16)

        @block.vector
        def _(dve):
            ch = Chain(dve, s_c)
            for t in range(NT):
                b = t % NB
                dve.wait_ge(s_rows[b], 16 * TOPK * (t // NB + 1))
                for k in range(TOPK):
                    if k:
                        ch.last()
                    ins = dve.scalar_tensor_tensor(out=X[:, t], in0=YR[:, b, k, :], scalar=GATE[:, t, k:k + 1],
                                                   in1=X[:, t], op0=ALU.mult, op1=ALU.add)
                    if k < TOPK - 1:
                        ch.step(ins)
                ins.then_inc(s_sum, 1)

        @block.sync
        def _(sp):
            for t in range(NT):
                sp.wait_ge(s_sum, t + 1)
                sp.dma_start(g["out_t"][:, t], X[:, t]).then_inc(s_out, 16)
            sp.wait_ge(s_out, 16 * NT)


_INS = ["L0_attn_x", "L0_attn_Wq", "L0_attn_Wk", "L0_attn_Wv", "L0_attn_Wo", "L0_ffn_router_w", "L0_ffn_router_bias",
        "L0_ffn_wg", "L0_ffn_wu", "L0_ffn_wd", "L0_ffn_swg", "L0_ffn_swu", "L0_ffn_swd", "L0_c", "L0_wmod"]
_OUTS = [((1, T, C), "float32")]


def kernel(**inputs):
    import numpy as _np
    import concourse.bacc as _bacc
    from concourse import mybir as _mybir
    from concourse.bass_utils import run_bass_kernel_spmd as _run

    nc = _bacc.Bacc("TRN2", target_bir_lowering=False, num_devices=1)
    arrays, args = {}, []
    for name in _INS:
        a = _np.ascontiguousarray(inputs[name])
        arrays[f"in_{name}_dram"] = a
        args.append(nc.dram_tensor(f"in_{name}_dram", a.shape, _mybir.dt.from_np(a.dtype), kind="ExternalInput").ap())
    for i, (shape, dtype) in enumerate(_OUTS):
        dt = _mybir.dt.from_np(_np.dtype(dtype))
        args.append(nc.dram_tensor(f"out_{i}_dram", shape, dt, kind="ExternalOutput").ap())
    build_kernel(nc, *args)
    r = _run(nc, [arrays], core_ids=[0])
    got = tuple(r.results[0][f"out_{i}_dram"] for i in range(len(_OUTS)))
    return got[0]
```

```python
from contextlib import ExitStack

import concourse.bass as bass
from concourse import mybir

F32 = mybir.dt.float32
BF16 = mybir.dt.bfloat16
F32R = mybir.dt.float32r
I32 = mybir.dt.int32
U32 = mybir.dt.uint32
ALU = mybir.AluOpType
ACT = mybir.ActivationFunctionType
AX = mybir.AxisListType

P = 128
T, C = 2048, 512
NT = T // P
KC = C // P
HS, NH, NKV = 32, 16, 4
HPG = NH // NKV
SINK = 4
WT = 3
E, F, TOPK = 64, 128, 4
SH, HC = 2, 4
MAXT = T * TOPK // P + E
AHEAD_TILES = 4
EPS = 1e-5
NEG = -1e30
GROUPS = 4
GROUP_TOKENS = T // GROUPS
SCALE = HS ** -0.5
KW = WT * P
SW = KW + SINK


class Chain:

    def __init__(self, eng, sem):
        self.eng, self.sem, self.n = eng, sem, 0

    def step(self, ins):
        ins.then_inc(self.sem, 1)
        self.n += 1

    def last(self):
        self.eng.wait_ge(self.sem, self.n)


def wait(eng, sem, value):
    if not (isinstance(value, int) and value <= 0):
        eng.wait_ge(sem, value)


def hold(eng, g):
    eng.sem_inc(g["s_held"][eng.engine.name], 1)


def rsqrt(dve, ch, out, var, tmp):
    v, t = tmp
    ch.step(dve.tensor_scalar(v, var, EPS, None, ALU.add))
    ch.last()
    ch.step(dve.tensor_scalar(t.bitcast(I32), v.bitcast(I32), 1, None, ALU.arith_shift_right))
    ch.last()
    ch.step(dve.tensor_scalar(out.bitcast(I32), t.bitcast(I32), -1.0, float(0x5F3759DF), ALU.mult, ALU.add))
    for _ in range(3):
        ch.last()
        ch.step(dve.tensor_tensor(t, out, out, ALU.mult))
        ch.last()
        ch.step(dve.tensor_tensor(t, t, v, ALU.mult))
        ch.last()
        ch.step(dve.tensor_scalar(t, t, -0.5, 1.5, ALU.mult, ALU.add))
        ch.last()
        ch.step(dve.tensor_tensor(out, out, t, ALU.mult))
    ch.last()


def build_kernel(nc, x, Wq, Wk, Wv, Wo, router_w, router_bias, wg, wu, wd, swg, swu, swd, cvec, wmod, out):
    stack = ExitStack()
    with stack:
        def sb(name, shape, dt=F32, ctx=stack):
            return ctx.enter_context(nc.sbuf_tensor(name, shape, dt))

        def ps(name, shape, dt=F32, ctx=stack):
            return ctx.enter_context(nc.psum_tensor(name, shape, dt))

        def sem(name):
            return stack.enter_context(nc.semaphore(name))

        x_t = x.rearrange("b (t p) c -> p (b t) c", p=P)
        out_t = out.rearrange("b (t p) c -> p (b t) c", p=P)
        h2_rows = nc.dram_tensor("h2_rows", [NT + 1, P, C + E], F32, kind="Internal").ap()
        h2t_cols = nc.dram_tensor("h2t_cols", [NT, P, KC, P], F32, kind="Internal").ap()
        total = [nc.dram_tensor(f"total{i}", [NT + 1, P, C], F32, kind="Internal").ap() for i in range(2)]

        X = sb("X", [P, NT, C])
        ident = sb("ident", [P, P])
        ones = sb("ones", [P, P])
        gb_row = sb("gb_row", [P, C])
        LG = sb("LG", [P, NT, E])
        EIDX = sb("EIDX", [P, NT, 8])
        TOKI = sb("TOKI", [P, MAXT + AHEAD_TILES], I32)

        tile_expert = nc.dram_tensor("tile_expert", [1, P], I32, kind="Internal").ap()
        eid_row = sb("eid_row", [1, P], I32)
        end_row = sb("end_row", [1, E], I32)
        pairs = sb("pairs", [1, 1], I32)
        s_tile_expert = sem("s_tile_expert")
        s_held = {name: sem("s_held_" + name) for name in ("DVE", "Pool", "SP", "Activation")}
        s_ident, s_mask = sem("s_ident"), sem("s_mask")
        s_in = [sem(f"s_in{i}") for i in range(10)]
        HTin = X[:, 0:4].rearrange("p t (k n) -> p t k n", k=KC)
        work = X[:, 4:8]
        room = X[:, 8:13].rearrange("p t c -> p (t c)")
        s_ht, s_w = sem("h_ht"), [sem(f"h_w{i}") for i in range(6)]
        s_stacked = [sem(f"s_stacked{i}") for i in range(GROUPS)]

        attn = ExitStack()
        with attn:
            A = lambda name, shape, dt=F32: sb(name, shape, dt, attn)
            ga_row = A("ga_row", [P, C])
            cb1_row = A("cb1_row", [P, C])
            sb_row = A("sb_row", [P, C])
            WoT = A("WoT", [P, KC, C])
            V = A("V", [P, NT, P])
            Q4 = A("Q4", [P, NH, T], BF16)
            K4 = A("K4", [P, NKV, T], BF16)
            rw = A("rw", [P, KC, E])
            rbias = A("rbias", [P, E])
            mask = A("mask", [P, 4, SW], BF16)

            QT = A("QT", [P, GROUPS, 2, NKV, GROUP_TOKENS], BF16)
            KT = A("KT", [P, GROUPS, 2, GROUP_TOKENS], BF16)
            with ExitStack() as pro:
                prologue(nc, pro, sb, ps, sem, locals())
            with ExitStack() as mid:
                attention(nc, mid, sb, ps, sem, locals())
        with ExitStack() as tail:
            shared_experts(nc, tail, sb, ps, sem, locals())
        with ExitStack() as tail:
            routed_experts(nc, tail, sb, ps, sem, locals())
        with ExitStack() as tail:
            finish(nc, tail, sb, sem, locals())


def prologue(nc, ctx, sb, ps, sem, g):
    X, V, Q4, K4, WoT = (g[k] for k in ("X", "V", "Q4", "K4", "WoT"))
    QT, KT = g["QT"], g["KT"]
    ident, ones = g["ident"], g["ones"]
    s_in = g["s_in"]
    B = lambda name, shape, dt=F32: sb(name, shape, dt, ctx)
    WqT = B("WqT", [P, KC, C])
    WkvT = B("WkvT", [P, 2, KC, P])
    xh = B("xh", [P, 2, C])
    hT = B("hT", [P, 2, KC, P])
    cT = B("cT", [P, KC])
    sc = B("sc", [P, KC])
    sa_col = B("sa_col", [P, KC])
    ca1_col = B("ca1_col", [P, KC])
    stats = B("stats", [P, NT // 4, 6])
    mv = B("mv", [P, NT, 2])
    rstd = B("rstd", [P, NT])
    rt = B("rt", [P, 2, NT])
    room = Q4[:].rearrange("p h t -> p (h t)").bitcast(F32)
    wm = room[:, 0:6 * KC * C].rearrange("p (r k s n) -> p r k s n", r=3, k=KC, s=2)
    Wqo = room[:, 6 * KC * C:8 * KC * C].rearrange("p (s o c) -> p s o c", s=2, o=KC)
    room = K4[:].rearrange("p h t -> p (h t)").bitcast(F32)
    Wkv = room[:, 0:2 * C].rearrange("p (s c) -> p s c", s=2)
    scb = room[:, 2 * C:3 * C].rearrange("p (k m) -> p k m", k=KC)
    gtmp = room[:, 3 * C:5 * C].rearrange("p (s c) -> p s c", s=2)
    s_c, s_sc, s_scb, s_mod, s_modc, s_wt, s_wtc, s_dve, s_xh, s_tr, s_hT, s_q, s_k, s_v, s_hi, s_lo, s_vc, s_ln = (
        sem("p_" + n) for n in ("c", "sc", "scb", "mod", "modc", "wt", "wtc", "dve", "xh", "tr", "hT", "q", "k", "v",
                                "hi", "lo", "vc", "ln"))
    s_wm = [sem(f"p_wm{i}") for i in range(3)]
    s_modr, s_col = sem("p_modr"), sem("p_col")
    psT = [ps(f"psT{i}", [P, KC, P], F32, ctx) for i in range(2)]
    psQ = [ps(f"psQ{i}", [P, KC, P], F32, ctx) for i in range(2)]
    psK = [ps(f"psK{i}", [P, C], F32, ctx) for i in range(2)]
    psV = [ps(f"psV{i}", [P, C], F32, ctx) for i in range(2)]
    psW = psT + psQ
    wmod_v = g["wmod"].rearrange("(p k) n -> p k n", k=KC)
    TURNS, MODS = 2 * KC + 2, 6
    XQ = NT // 4

    def parts(dst, h, b, part):
        tok = bass.ds(h % (XQ // 2) * (2 * P) + b * P, P)
        if dst is KT:
            return dst[:, bass.ds(h // (XQ // 2), 1), part, tok].rearrange("p a n -> p (a n)")
        return dst[:, bass.ds(h // (XQ // 2), 1), part, :, tok].rearrange("p a g n -> p (a g) n")

    def sweep(eng, tile, first=0):
        for i in range(first, 2):
            tile(0, i, i)
        with eng.Fori(1, NT // 2 - 1) as h:
            for b in range(2):
                tile(h, h * 2 + b, b)
        for i in range(NT - 2, NT):
            tile(NT // 2 - 1, i, i % 2)

    with nc.Block() as block:
        @block.sync
        def _(sp):
            def mod_sections(r):
                sp.dma_start(wm[:, r], wmod_v[:, :, 2 * r * C:(2 * r + 2) * C].rearrange("p k (s n) -> p k s n", s=2)).then_inc(s_wm[r], 16)

            sp.dma_start(cT[:], g["cvec"].rearrange("b (p k) -> (b p) k", k=KC)).then_inc(s_c, 16)
            mod_sections(0)
            sp.dma_start(Wqo[:, 0], g["Wq"].rearrange("(o p) c -> p o c", p=P)).then_inc(s_in[0], 16)
            sp.dma_start(Wkv[:, 0], g["Wk"]).then_inc(s_in[1], 16)
            sp.dma_start(Wkv[:, 1], g["Wv"]).then_inc(s_in[2], 16)
            for i in range(4):
                sp.dma_start(X[:, XQ * i:XQ * (i + 1)], g["x_t"][:, XQ * i:XQ * (i + 1)]).then_inc(s_in[3 + i], 16)
                if i == 0:
                    sp.dma_start(Wqo[:, 1], g["Wo"].rearrange("(o p) c -> p o c", p=P)).then_inc(s_in[7], 16)
            mod_sections(1)
            mod_sections(2)
            sp.dma_start(g["rw"][:], g["router_w"].rearrange("(p k) e -> p k e", k=KC)).then_inc(s_in[8], 16)
            sp.dma_start(g["rbias"][:], g["router_bias"].rearrange("(a e) -> a e", a=1).broadcast_to([P, E])).then_inc(s_in[9], 16)
            sp.wait_ge(s_wtc, TURNS)
            sp.wait_ge(s_modc, MODS)
            for q in range(GROUPS - 1):
                sp.wait_ge(s_lo, 2 * XQ * (q + 1))
                stack_group(sp, g, q)
            for q in range(GROUPS - 1):
                sp.wait_ge(g["s_stacked"][q], 16 * 2 * 4 * HPG)

        @block.gpsimd
        def _(pool):
            pool.memset(ident[:], 0.0).then_inc(g["s_ident"], 1)
            pool.memset(ones[:], 1.0).then_inc(g["s_ident"], 1)
            pool.wait_ge(g["s_ident"], 2)
            pool.affine_select(out=ident[:], in_=ident[:], compare_op=ALU.not_equal, fill=1.0, base=0,
                               pattern=[[-1, P]], channel_multiplier=1).then_inc(g["s_ident"], 1)
            pool.memset(g["mask"][:], 0.0).then_inc(g["s_mask"], 1)
            pool.wait_ge(g["s_mask"], 1)

            def keep(m, lo, n, base, step, mult):
                pool.affine_select(out=g["mask"][:, m, lo:lo + n], in_=g["mask"][:, m, lo:lo + n], compare_op=ALU.is_ge,
                                   fill=-NEG, base=base, pattern=[[step, n]], channel_multiplier=mult).then_inc(g["s_mask"], 1)
            keep(0, 0, P, 0, -1, 1)
            keep(1, P, P, 0, -1, 1)
            keep(2, 2 * P, P, 0, -1, 1)
            keep(3, 2 * P, P, 0, -1, 1)
            keep(2, 0, P, -1, 1, -1)
            keep(3, 0, P, -1, 1, -1)
            pool.wait_ge(g["s_mask"], 7)
            keep(2, 0, P, -SINK, 1, 0)

        @block.scalar
        def _(act):
            act.wait_ge(s_c, 16)
            act.activation(sc[:], cT[:], ACT.Silu).then_inc(s_sc, 1)
            for n in range(TURNS):
                act.wait_ge(s_wt, n + 1)
                if n < KC:
                    dst = WqT[:, n]
                elif n < KC + 2:
                    dst = WkvT[:, n - KC].rearrange("p k o -> p (k o)")
                else:
                    dst = WoT[:, n - KC - 2]
                act.activation(dst, psW[n % 4][:].rearrange("p k n -> p (k n)"), ACT.Copy).then_inc(s_wtc, 1)

            def modulated(i, b):
                act.wait_ge(s_tr, i + 1)
                wait(act, s_v, i - 1)
                if isinstance(i, int) and i == 0:
                    act.wait_ge(s_modc, 2)
                for k in range(KC):
                    ins = act.activation(hT[:, b, k, :], psT[b][:, k, :], ACT.Identity,
                                         bias=sa_col[:, k:k + 1], scale=ca1_col[:, k:k + 1])
                ins.then_inc(s_hT, 1)

            def tile(h, i, b):
                q_hi, k_hi = parts(QT, h, b, 0), parts(KT, h, b, 0)
                if not isinstance(i, int) or i + 1 < NT:
                    modulated(i + 1, 1 - b)
                act.wait_ge(s_q, i + 1)
                act.activation(q_hi, psQ[b][:], ACT.Copy, scale=-SCALE).then_inc(s_hi, 1)
                act.wait_ge(s_k, i + 1)
                act.activation(k_hi, psK[b][:, 0:P], ACT.Copy).then_inc(s_hi, 1)
                act.wait_ge(s_v, i + 1)
                act.activation(V[:, bass.ds(i, 1)].rearrange("p a c -> p (a c)"), psV[b][:, 0:P],
                               ACT.Copy).then_inc(s_vc, 1)
            modulated(0, 0)
            sweep(act, tile)

        @block.vector
        def _(dve):
            ch = Chain(dve, s_dve)
            dve.wait_ge(s_sc, 1)
            for k in range(KC):
                dve.tensor_copy(scb[:, k, :], sc[:, k:k + 1].broadcast_to([P, P])).then_inc(s_scb, 1)
            for s in range(2):
                dve.wait_ge(s_mod, s + 1)
                dve.tensor_copy(gtmp[:, s], psK[s][:]).then_inc(s_modr, 1)
            ln = Chain(dve, s_ln)

            def statistics(q):
                dve.wait_ge(s_in[3 + q], 16)
                t = range(q * XQ, (q + 1) * XQ)
                for i in t:
                    ln.step(dve.bn_stats(stats[:, i % XQ], X[:, i]))
                ln.last()
                for i in t:
                    ln.step(dve.bn_aggr(mv[:, i], stats[:, i % XQ]))
                ln.last()
                t = slice(q * XQ, (q + 1) * XQ)
                rsqrt(dve, ln, rstd[:, t], mv[:, t, 1:2].rearrange("p t a -> p (t a)"), (rt[:, 0, t], rt[:, 1, t]))

            def norm(i, b):
                wait(dve, s_tr, i - 1)
                dve.tensor_scalar(xh[:, b], X[:, bass.ds(i, 1)].rearrange("p a c -> p (a c)"),
                                  mv[:, bass.ds(i, 1), 0:1].rearrange("p a b -> p (a b)"), rstd[:, bass.ds(i, 1)],
                                  ALU.subtract, ALU.mult).then_inc(s_xh, 1)

            def tile(h, i, b):
                if not isinstance(i, int) or i + 2 < NT:
                    norm(i + 2, b)
                dve.wait_ge(s_hi, 2 * i + 1)
                dve.scalar_tensor_tensor(out=parts(QT, h, b, 1), in0=psQ[b][:], scalar=-SCALE, in1=parts(QT, h, b, 0),
                                         op0=ALU.mult, op1=ALU.subtract).then_inc(s_lo, 1)
                dve.wait_ge(s_hi, 2 * i + 2)
                dve.scalar_tensor_tensor(out=parts(KT, h, b, 1), in0=psK[b][:, 0:P], scalar=1.0, in1=parts(KT, h, b, 0),
                                         op0=ALU.mult, op1=ALU.subtract).then_inc(s_lo, 1)

            def floored(dst, src, sem_value):
                dve.wait_ge(s_mod, sem_value)
                ch.step(dve.tensor_scalar(gtmp[:, 0], src, -1.0, 0.25, ALU.mult, ALU.max))
                ch.last()
                ch.step(dve.scalar_tensor_tensor(out=gtmp[:, 0], in0=src, scalar=0.25, in1=gtmp[:, 0],
                                                 op0=ALU.max, op1=ALU.max))
                ch.step(dve.tensor_scalar(gtmp[:, 1], src, 0.0, 2.0, ALU.is_ge, ALU.mult))
                ch.last()
                dve.scalar_tensor_tensor(out=dst, in0=gtmp[:, 1], scalar=-1.0, in1=gtmp[:, 0],
                                         op0=ALU.add, op1=ALU.mult).then_inc(s_modc, 1)
            def modulation_rows():
                floored(g["ga_row"][:], psV[1][:], 3)
                dve.wait_ge(s_mod, 4)
                dve.tensor_copy(g["sb_row"][:], psV[0][:]).then_inc(s_modc, 1)
                dve.wait_ge(s_mod, 5)
                dve.tensor_scalar(g["cb1_row"][:], psK[1][:], 1.0, None, ALU.add).then_inc(s_modc, 1)
                dve.wait_ge(s_modc, 3)
                floored(g["gb_row"][:], psK[0][:], 6)

            statistics(0)
            norm(0, 0)
            norm(1, 1)
            dve.wait_ge(s_col, 1)
            dve.tensor_copy(sa_col[:], psV[0][:, 0:C:P]).then_inc(s_modc, 1)
            dve.wait_ge(s_col, 2)
            dve.tensor_scalar(ca1_col[:], psV[1][:, 0:C:P], 1.0, None, ALU.add).then_inc(s_modc, 1)
            statistics(1)
            tile(0, 0, 0)
            modulation_rows()
            statistics(2)
            tile(0, 1, 1)
            statistics(3)
            sweep(dve, tile, 2)

        @block.tensor
        def _(pe):
            def rows(r, s, bank):
                for k in range(KC):
                    ins = pe.matmul(bank[:], scb[:, k, :], wm[:, r, k, s, :], start=(k == 0), stop=(k == KC - 1))
                ins.then_inc(s_mod, 1)

            def turn(n, blocks):
                if n >= 4:
                    pe.wait_ge(s_wtc, n - 3)
                for j, b in enumerate(blocks):
                    ins = pe.transpose(psW[n % 4][:, j, :], b, ident[:])
                ins.then_inc(s_wt, 1)

            pe.wait_ge(s_scb, KC)
            pe.wait_ge(s_wm[0], 16)
            rows(0, 0, psK[0])
            rows(0, 1, psK[1])
            pe.wait_ge(g["s_ident"], 3)
            pe.wait_ge(s_in[0], 16)
            for k in range(KC):
                turn(k, [Wqo[:, 0, o, k::KC] for o in range(KC)])
            pe.wait_ge(s_in[1], 16)
            turn(KC, [Wkv[:, 0, k::KC] for k in range(KC)])
            pe.wait_ge(s_in[2], 16)
            turn(KC + 1, [Wkv[:, 1, k::KC] for k in range(KC)])
            pe.wait_ge(s_in[7], 16)
            for k in range(KC):
                turn(KC + 2 + k, [Wqo[:, 1, o, k * P:(k + 1) * P] for o in range(KC)])

            for s, bank in enumerate(psV):
                pe.wait_ge(s_modr, s + 1)
                for k in range(KC):
                    ins = pe.transpose(bank[:, k * P:(k + 1) * P], gtmp[:, s, k::KC], ident[:])
                ins.then_inc(s_col, 1)

            def modulation_rows():
                pe.wait_ge(s_scb, KC)
                pe.wait_ge(s_wm[1], 16)
                rows(1, 0, psV[1])
                pe.wait_ge(s_vc, 1)
                rows(1, 1, psV[0])
                pe.wait_ge(s_wm[2], 16)
                rows(2, 0, psK[1])
                pe.wait_ge(s_lo, 2)
                rows(2, 1, psK[0])

            def turned(i, b):
                pe.wait_ge(s_xh, i + 1)
                wait(pe, s_hT, i - 1)
                for k in range(KC):
                    ins = pe.transpose(psT[b][:, k, :], xh[:, b, k::KC], ident[:])
                ins.then_inc(s_tr, 1)

            def tile(h, i, b):
                if not isinstance(i, int) or i + 1 < NT:
                    turned(i + 1, 1 - b)
                pe.wait_ge(s_hT, i + 1)
                wait(pe, s_lo, (i - 1) * 2)
                for o in range(KC):
                    for k in range(KC):
                        ins = pe.matmul(psQ[b][:, o, :], WqT[:, k, o * P:(o + 1) * P], hT[:, b, k, :],
                                        start=(k == 0), stop=(k == KC - 1))
                ins.then_inc(s_q, 1)
                if isinstance(i, int) and i == 0:
                    pe.wait_ge(s_modc, 2)
                if isinstance(i, int) and i == 1:
                    pe.wait_ge(s_modc, MODS)
                for k in range(KC):
                    ins = pe.matmul(psK[b][:, 0:P], WkvT[:, 0, k, :], hT[:, b, k, :],
                                    start=(k == 0), stop=(k == KC - 1))
                ins.then_inc(s_k, 1)
                wait(pe, s_vc, i - 1)
                for k in range(KC):
                    ins = pe.matmul(psV[b][:, 0:P], hT[:, b, k, :], WkvT[:, 1, k, :],
                                    start=(k == 0), stop=(k == KC - 1))
                ins.then_inc(s_v, 1)

            pe.wait_ge(s_wtc, TURNS)
            turned(0, 0)
            tile(0, 0, 0)
            modulation_rows()
            tile(0, 1, 1)
            sweep(pe, tile, 2)


def stack_group(sp, g, q):
    tok = slice(q * T // GROUPS, (q + 1) * T // GROUPS)
    for j in range(HPG):
        for r in range(4):
            rows, dst = slice(j * HS, (j + 1) * HS), slice(r * HS, (r + 1) * HS)
            sp.dma_start(g["Q4"][dst, j::HPG, tok], g["QT"][rows, q, r // 2]).then_inc(g["s_stacked"][q], 16)
            sp.dma_start(g["K4"][dst, j, tok], g["KT"][rows, q, r % 2]).then_inc(g["s_stacked"][q], 16)


def attention(nc, ctx, sb, ps, sem, g):
    X, V, Q4, K4, WoT = (g[k] for k in ("X", "V", "Q4", "K4", "WoT"))
    ident, LG = g["ident"], g["LG"]
    B = lambda name, shape, dt=F32: sb(name, shape, dt, ctx)
    S_AHEAD, M_AHEAD, E_AHEAD = 3, 2, 1
    U = NKV
    GROUP_DMAS = 2 * 4 * HPG
    mask = g["mask"]
    room = g["QT"][:].rearrange("p q r h n -> p (q r h n)").bitcast(F32)
    S = B("S", [P, 8, SW])
    den = B("den", [P, 8])
    nm = B("nm", [P, 8])
    PT = room[:, 0:2 * HPG * KW].rearrange("p (s j n) -> p s j n", s=2, j=HPG)
    yT, t1, xh, h2, h2t = (room[:, 2 * HPG * KW + i * C:2 * HPG * KW + (i + 1) * C] for i in range(5))
    yT, h2t = yT.rearrange("p (u n) -> p u n", u=NKV), h2t.rearrange("p (k n) -> p k n", k=KC)
    skP = B("skP", [P, 2, HPG * SINK])
    skT = B("skT", [HPG * SINK, P])
    Vs = B("Vs", [HPG * SINK, NKV, P])
    Vc = B("Vc", [P, WT, P])
    RB = B("RB", [P, 2, HPG, HS])
    rden = B("rden", [P, 2, HPG])
    s_rden, s_xw = sem("a_rden"), sem("a_xw")
    yU = B("yU", [P, 2, P])
    stats = B("stats2", [P, 6])
    mv = B("mv2", [P, 2])
    rstd = B("rstd2", [P, 1])
    rt = B("rt2", [P, 2])
    v8 = B("v8", [P, 8])
    i8 = B("i8", [P, 8], U32)
    lgb = B("lgb", [P, E])
    psS = [ps(f"psS{i}", [P, C], F32, ctx) for i in range(2)]
    psT = [ps(f"psTa{i}", [P, C], F32, ctx) for i in range(2)]
    psO = ps("psO", [P, C], F32, ctx)
    psA = ps("psA", [P, C], F32, ctx)
    psX = ps("psX", [P, C], F32, ctx)
    psL = ps("psL", [P, E], F32, ctx)
    (s_vs, s_vcur, s_scores, s_masked, s_exp, s_turned, s_copied_a, s_copied_d, s_sinkw, s_sinkt, s_sinkc,
     s_rb, s_pv, s_yu, s_y, s_part, s_res, s_x1, s_st, s_xh, s_scaled, s_h2, s_h2w, s_h2t, s_h2c, s_h2tw,
     s_logit, s_lgread, s_top) = (sem("a_" + n) for n in (
         "vs", "vcur", "scores", "masked", "exp", "turned", "copied_a", "copied_d", "sinkw", "sinkt",
         "sinkc", "rb", "pv", "yu", "y", "part", "res", "x1", "st", "xh", "scaled", "h2", "h2w", "h2t",
         "h2c", "h2tw", "logit", "lgread", "top"))
    SINK_FROM = WT - 1

    DVE_HEAD = 1

    def act_copies(j):
        return j + 1 - (j > DVE_HEAD)

    def shape_of(qt):
        if isinstance(qt, int) and qt < WT:
            return (qt + 1) * P, 0, qt, qt >= SINK_FROM
        return KW, (qt - (WT - 1)) * P, WT, True

    def ahead(qt, n, by):
        qt, n = qt + (n + by) // NH, (n + by) % NH
        return None if isinstance(qt, int) and qt >= NT else (qt, n)

    def sweep(eng, slot):
        for qt in range(WT):
            for n in range(NH):
                slot(qt, n)
        with eng.Fori(WT, NT - 1) as qt:
            for n in range(NH):
                slot(qt, n)
        for qt in range(NT - 1, NT + 2):
            for n in range(NH):
                slot(qt, n)

    def tile_in(qt, back):
        return not isinstance(qt, int) or 0 <= qt - back < NT

    with nc.Block() as block:
        @block.sync
        def _(sp):
            stack_group(sp, g, GROUPS - 1)
            sp.wait_ge(s_vs, 1)
            for j in range(HPG):
                sp.dma_start(Vs[j * SINK:(j + 1) * SINK, :, j * HS:(j + 1) * HS],
                             V[0:SINK, 0, :].rearrange("p (g d) -> p g d", g=NKV)).then_inc(s_vs, 16)
            def store(i):
                sp.wait_ge(s_h2, i + 1)
                sp.dma_start(g["h2_rows"][bass.ds(i, 1), :, 0:C].rearrange("a p c -> (a p) c"), h2[:]).then_inc(s_h2w, 16)
                sp.dma_start(g["total"][0][bass.ds(i, 1)].rearrange("a p c -> (a p) c"),
                             X[:, bass.ds(i, 1)].rearrange("p a c -> p (a c)")).then_inc(s_xw, 16)
                sp.wait_ge(s_h2c, i + 1)
                sp.dma_start(g["h2t_cols"][bass.ds(i, 1)].rearrange("a p k n -> p (a k) n"), h2t[:]).then_inc(s_h2tw, 16)

            DONE = 13
            with sp.Fori(0, DONE) as i:
                store(i)
            for done in (s_h2w, s_xw, s_h2tw):
                sp.wait_ge(done, 16 * DONE)
            sp.dma_start(g["HTin"], g["h2t_cols"][0:4].rearrange("t p k n -> p t k n")).then_inc(g["s_ht"], 16)
            for i, (w, dst) in enumerate(((g["swg"], g["room"][:, 0:HC * C]), (g["swu"], g["work"].rearrange("p s n -> p (s n)")))):
                sp.dma_start(dst.rearrange("p (k n) -> p k n", k=KC),
                             w[0].rearrange("(p k) h -> p k h", k=KC)).then_inc(g["s_w"][i], 16)
            with sp.Fori(DONE, NT) as i:
                store(i)
            sp.wait_ge(s_h2w, 16 * NT)
            sp.wait_ge(s_xw, 16 * NT)
            sp.wait_ge(s_h2tw, 16 * NT)

        @block.gpsimd
        def _(pool):
            pool.memset(Vs[:], 0.0).then_inc(s_vs, 1)
            def slot(qt, n):
                j, u = n % HPG, n // HPG
                if n == 2 and tile_in(qt, 0):
                    w = shape_of(qt)[0] // P
                    wait(pool, s_pv, U * qt)
                    hold(pool, g)
                    pool.tensor_copy(Vc[:, 0:w], V[:, bass.ds(qt - (w - 1), w)]).then_inc(s_vcur, 1)
                if j == 3 and tile_in(qt, 0) and shape_of(qt)[3]:
                    G, i = qt * U + u, (qt - SINK_FROM) * U + u
                    wait(pool, s_exp, (G + 1) * HPG)
                    wait(pool, s_sinkt, i - 1)
                    b = (u % 2) * HPG
                    hold(pool, g)
                    pool.tensor_copy(skP[:, u % 2].rearrange("p (j s) -> p j s", j=HPG),
                                     S[:, b:b + HPG, KW:SW]).then_inc(s_sinkw, 1)
                if n == 8 and tile_in(qt, 1):
                    Xr = X[:, bass.ds(qt - 1, 1)].rearrange("p a c -> p (a c)")
                    wait(pool, s_res, qt)
                    pool.tensor_tensor(Xr, Xr, t1[:], ALU.add).then_inc(s_x1, 1)
                if n == 15 and tile_in(qt, 1):
                    wait(pool, s_xh, qt)
                    pool.tensor_tensor(xh[:], xh[:], g["cb1_row"][:], ALU.mult).then_inc(s_scaled, 1)
                    wait(pool, s_scaled, qt)
                    wait(pool, s_h2w, 16 * (qt - 1))
                    wait(pool, s_h2t, qt - 1)
                    pool.tensor_tensor(h2[:], xh[:], g["sb_row"][:], ALU.add).then_inc(s_h2, 1)
            sweep(pool, slot)

        @block.tensor
        def _(pe):
            def scores(qt, n):
                W, k0, m, sinks = shape_of(qt)
                u = n // HPG
                wait(pe, s_masked, qt * NH + n - 1)
                q = Q4[:, n, bass.ds(qt * P, P)]
                ins = pe.matmul(psS[n % 2][:, 0:W], q, K4[:, u, bass.ds(k0, W)], start=True, stop=True)
                if sinks:
                    ins = pe.matmul(psS[n % 2][:, KW:SW], q, K4[:, u, 0:SINK], start=True, stop=True)
                ins.then_inc(s_scores, 1)

            def turn(qt, n):
                wait(pe, s_exp, qt * NH + n + 1)
                G, j = qt * U + (n - 2) // HPG, (n - 2) % HPG
                if j == DVE_HEAD:
                    wait(pe, s_copied_d, G + 1)
                else:
                    wait(pe, s_copied_a, G * (HPG - 1) + act_copies(j))
                for k in range(shape_of(qt)[0] // P):
                    ins = pe.transpose(psT[n % 2][:, k * P:(k + 1) * P], S[:, n % 8, k * P:(k + 1) * P], ident[:])
                ins.then_inc(s_turned, 1)

            def sinks_turn(qt, u):
                if shape_of(qt)[3]:
                    wait(pe, s_sinkw, (qt - SINK_FROM) * U + u + 1)
                    wait(pe, s_y, qt * U + u)
                    pe.transpose(psO[0:HPG * SINK, 2 * P:3 * P], skP[:, u % 2], ident[:]).then_inc(s_sinkt, 1)

            def products(qt, u):
                W, k0, m, sinks = shape_of(qt)
                G = qt * U + u
                wait(pe, s_y, G)
                wait(pe, s_rb, G + 1)
                if sinks:
                    wait(pe, s_sinkc, (qt - SINK_FROM) * U + u + 1)
                pe.matmul(psO[:, P:2 * P], RB[:, u % 2].rearrange("p j d -> p (j d)"), ident[:], start=True, stop=True)
                wait(pe, s_copied_a, (HPG - 1) * (G + 1))
                wait(pe, s_copied_d, G + 1)
                if u == 0:
                    wait(pe, s_vcur, qt + 1)
                if sinks:
                    if isinstance(qt, int) and qt == SINK_FROM and u == 0:
                        wait(pe, s_vs, 1 + 16 * HPG)
                    pe.matmul(psO[:, 0:P], Vs[:, u, :], skT[:], start=True, stop=False, skip_group_check=True)
                for k in range(W // P):
                    for j in range(HPG):
                        ins = pe.matmul(psO[j * HS:(j + 1) * HS, 0:P], Vc[:, k, u * HS:(u + 1) * HS],
                                        PT[:, u % 2, j, k * P:(k + 1) * P], start=(k == 0 and not sinks),
                                        stop=(k == W // P - 1), skip_group_check=True)
                ins.then_inc(s_pv, 1)

            def project(qt, u):
                wait(pe, s_y, qt * U + u + 1)
                if u == 0:
                    wait(pe, s_res, qt)
                ins = pe.matmul(psA[:], yT[:, u, :], WoT[:, u, :], start=(u == 0), stop=(u == U - 1))
                ins.then_inc(s_part, 1)

            def slot(qt, n):
                j, u = n % HPG, n // HPG
                if tile_in(qt, 0):
                    turn(qt, n)
                if isinstance(qt, int) and (qt, n) == (WT - 1, NH - S_AHEAD):
                    for q in range(1, GROUPS):
                        pe.wait_ge(g["s_stacked"][q], GROUP_DMAS * 16)
                if h := ahead(qt, n, S_AHEAD):
                    scores(*h)
                back, v = (0, u - 1) if u else (1, U - 1)
                if j == 0 and tile_in(qt, back):
                    sinks_turn(qt - back, v)
                if j == 1 and tile_in(qt, back):
                    products(qt - back, v)
                back, v = (0, u - 2) if u >= 2 else (1, u + U - 2)
                if j == 0 and tile_in(qt, back):
                    project(qt - back, v)
                if n == 2 and tile_in(qt, 2):
                    wait(pe, s_h2, qt - 1)
                    wait(pe, s_h2c, qt - 2)
                    for k in range(KC):
                        ins = pe.transpose(psX[:, k * P:(k + 1) * P], h2[:, k::KC], ident[:])
                    ins.then_inc(s_h2t, 1)
                if n == 7 and tile_in(qt, 2):
                    wait(pe, s_h2c, qt - 1)
                    wait(pe, s_lgread, qt - 2)
                    for k in range(KC):
                        ins = pe.matmul(psL[:], h2t[:, k, :], g["rw"][:, k, :], start=(k == 0), stop=(k == KC - 1))
                    ins.then_inc(s_logit, 1)

            pe.wait_ge(g["s_stacked"][0], GROUP_DMAS * 16)
            pe.wait_ge(g["s_in"][8], 16)
            for n in range(S_AHEAD):
                scores(0, n)
            sweep(pe, slot)

        @block.scalar
        def _(act):
            def exps(qt, n):
                W, k0, m, sinks = shape_of(qt)
                wait(act, s_masked, qt * NH + n + 1)
                wait(act, s_rb, qt * U + n // HPG - 1)
                w = SW if sinks else W
                act.activation(S[:, n % 8, 0:w], S[:, n % 8, 0:w], ACT.Exp, bias=nm[:, n % 8:n % 8 + 1], scale=-1.0,
                               accum_out=den[:, n % 8:n % 8 + 1]).then_inc(s_exp, 1)

            def copy(qt, n):
                W = shape_of(qt)[0]
                wait(act, s_turned, qt * NH + n + 1)
                wait(act, s_pv, qt * U + n // HPG - 1)
                act.activation(PT[:, (n // HPG) % 2, n % HPG, 0:W], psT[n % 2][:, 0:W], ACT.Copy).then_inc(s_copied_a, 1)

            def slot(qt, n):
                j, u = n % HPG, n // HPG
                if h := ahead(qt, n, E_AHEAD):
                    exps(*h)
                if n and (n - 1) % HPG != DVE_HEAD and tile_in(qt, 0):
                    copy(qt, n - 1)
                if n == 0 and tile_in(qt, 1):
                    copy(qt - 1, NH - 1)
                back, v = (0, u - 1) if u else (1, U - 1)
                if j == 2 and tile_in(qt, back):
                    G = (qt - back) * U + v
                    wait(act, s_pv, G + 1)
                    wait(act, s_y, G - 1)
                    act.activation(yU[:, v % 2, :], psO[:, 0:P], ACT.Copy).then_inc(s_yu, 1)
                if n == 4 and tile_in(qt, 2):
                    wait(act, s_h2t, qt - 1)
                    wait(act, s_logit, qt - 2)
                    wait(act, s_h2tw, 16 * (qt - 2))
                    act.activation(h2t[:].rearrange("p k n -> p (k n)"), psX[:], ACT.Copy).then_inc(s_h2c, 1)

            for n in range(E_AHEAD):
                exps(0, n)
            sweep(act, slot)

        @block.vector
        def _(dve):
            def masked(qt, n):
                W, k0, m, sinks = shape_of(qt)
                w = SW if sinks else W
                N = qt * NH + n
                wait(dve, s_scores, N + 1)
                wait(dve, s_turned, N - 7)
                if n % HPG == 0 and not (isinstance(qt, int) and qt <= SINK_FROM and n < 8):
                    wait(dve, s_sinkw, (qt - SINK_FROM) * U + n // HPG - 1)
                hold(dve, g)
                dve.tensor_tensor_reduce(S[:, n % 8, 0:w], psS[n % 2][:, 0:w], mask[:, m, 0:w], 1.0, 3e38,
                                         ALU.add, ALU.min, nm[:, n % 8:n % 8 + 1]).then_inc(s_masked, 1)

            def copy(qt, n):
                W = shape_of(qt)[0]
                wait(dve, s_turned, qt * NH + n + 1)
                wait(dve, s_pv, qt * U + n // HPG - 1)
                dve.tensor_copy(PT[:, (n // HPG) % 2, n % HPG, 0:W], psT[1][:, 0:W]).then_inc(s_copied_d, 1)

            STEPS = 14

            def step(ins):
                ins.then_inc(s_st, 1)

            def since(qt, k):
                wait(dve, s_st, (qt - 1) * STEPS + k)

            def norm_steps(qt, n):
                v, t, y = rt[:, 0:1], rt[:, 1:2], rstd[:]
                if n == 9:
                    wait(dve, s_x1, qt)
                    hold(dve, g)
                    step(dve.bn_stats(stats[:], X[:, bass.ds(qt - 1, 1)].rearrange("p a c -> p (a c)")))
                    since(qt, 1)
                    hold(dve, g)
                    step(dve.bn_aggr(mv[:], stats[:]))
                    since(qt, 2)
                    step(dve.tensor_scalar(v, mv[:, 1:2], EPS, None, ALU.add))
                if n == 10:
                    since(qt, 3)
                    step(dve.tensor_scalar(t.bitcast(I32), v.bitcast(I32), 1, None, ALU.arith_shift_right))
                    since(qt, 4)
                    step(dve.tensor_scalar(y.bitcast(I32), t.bitcast(I32), -1.0, float(0x5F3759DF), ALU.mult, ALU.add))
                if 11 <= n <= 13:
                    k = 5 + 3 * (n - 11)
                    since(qt, k)
                    step(dve.scalar_tensor_tensor(out=t, in0=y, scalar=v, in1=y, op0=ALU.mult, op1=ALU.mult))
                    since(qt, k + 1)
                    step(dve.tensor_scalar(t, t, -0.5, 1.5, ALU.mult, ALU.add))
                    since(qt, k + 2)
                    step(dve.tensor_tensor(y, y, t, ALU.mult))
                if n == 14:
                    since(qt, 14)
                    wait(dve, s_h2, qt - 1)
                    dve.tensor_scalar(xh[:], X[:, bass.ds(qt - 1, 1)].rearrange("p a c -> p (a c)"), mv[:, 0:1], y,
                                      ALU.subtract, ALU.mult).then_inc(s_xh, 1)

            def top_steps(qt, n):
                lg = LG[:, bass.ds(qt - 2, 1)].rearrange("p a c -> p (a c)")

                def since_top(k):
                    wait(dve, s_top, (qt - 2) * 3 + k)
                if n == 9:
                    wait(dve, s_logit, qt - 1)
                    dve.tensor_copy(lg, psL[:]).then_inc(s_lgread, 1)
                if n == 10:
                    wait(dve, s_lgread, qt - 1)
                    dve.tensor_tensor(lgb[:], lg, g["rbias"][:], ALU.add).then_inc(s_top, 1)
                if n == 11:
                    since_top(1)
                    hold(dve, g)
                    dve.max(v8[:], lgb[:]).then_inc(s_top, 1)
                if n == 12:
                    since_top(2)
                    hold(dve, g)
                    dve.max_index(i8[:], v8[:], lgb[:]).then_inc(s_top, 1)
                if n == 13:
                    since_top(3)
                    dve.tensor_copy(g["EIDX"][:, bass.ds(qt - 2, 1)].rearrange("p a c -> p (a c)"), i8[:])

            def slot(qt, n):
                j, u = n % HPG, n // HPG
                if h := ahead(qt, n, M_AHEAD):
                    masked(*h)
                back, v = (0, u - 1) if u else (1, U - 1)
                if j == 0 and tile_in(qt, back):
                    G = (qt - back) * U + v
                    wait(dve, s_exp, (G + 1) * HPG)
                    wait(dve, s_pv, G - 1)
                    b = (v % 2) * HPG
                    dve.reciprocal(rden[:, v % 2], den[:, b:b + HPG]).then_inc(s_rden, 1)
                if n and (n - 1) % HPG == DVE_HEAD and tile_in(qt, 0):
                    copy(qt, n - 1)
                if j == 0 and tile_in(qt, back):
                    wait(dve, s_rden, G + 1)
                    dve.tensor_copy(RB[:, v % 2], rden[:, v % 2].unsqueeze(2).broadcast_to([P, HPG, HS])).then_inc(s_rb, 1)
                if j == 0 and tile_in(qt, back) and shape_of(qt - back)[3]:
                    G, i = (qt - back) * U + v, (qt - back - SINK_FROM) * U + v
                    wait(dve, s_sinkt, i + 1)
                    wait(dve, s_pv, G)
                    dve.tensor_copy(skT[:], psO[0:HPG * SINK, 2 * P:3 * P]).then_inc(s_sinkc, 1)
                if j == 3 and tile_in(qt, back):
                    G = (qt - back) * U + v
                    wait(dve, s_yu, G + 1)
                    wait(dve, s_part, G - 3)
                    dve.tensor_tensor(yT[:, v, :], yU[:, v % 2, :], psO[:, P:2 * P], ALU.mult).then_inc(s_y, 1)
                if n == 6 and tile_in(qt, 1):
                    wait(dve, s_part, qt * U)
                    wait(dve, s_x1, qt - 1)
                    dve.tensor_tensor(t1[:], psA[:], g["ga_row"][:], ALU.mult).then_inc(s_res, 1)
                if tile_in(qt, 1):
                    norm_steps(qt, n)
                if tile_in(qt, 2):
                    top_steps(qt, n)

            dve.wait_ge(g["s_mask"], 8)
            dve.wait_ge(g["s_in"][9], 16)
            for n in range(M_AHEAD):
                masked(0, n)
            sweep(dve, slot)


def shared_experts(nc, ctx, sb, ps, sem, g):
    LG, EIDX = g["LG"], g["EIDX"]
    B = lambda name, shape, dt=F32: sb(name, shape, dt, ctx)
    GT = 4
    NG = NT // GT
    NCH = SH * HC
    STEPS = NG * NCH
    WG = B("WG", [P, 2, SH, KC, HC * P], F32R)
    WU = B("WU", [P, 2, SH, KC, HC * P], F32R)
    WD = B("WD", [P, 2, SH, HC, C], F32R)
    HT = B("HT", [P, 2, GT, KC, P], F32R)
    hid = B("hid", [P, 2, NCH, C], F32R)
    HTin, work, room = g["HTin"], g["work"], g["room"]
    sg = work[:, 0:2]
    tmp = work[:, 2:4]
    PARTS = ((0, 0), (0, 1), (1, 0))
    whole = lambda w, part, s: w[:, part, s].rearrange("p k n -> p (k n)")
    rows_at, room_at = HTin.rearrange("p t k n -> p (t k n)"), room[:, 0:HC * C]
    pieces = [(WG, 0, room_at), (WU, 0, work.rearrange("p s n -> p (s n)")), (WG, 1, rows_at),
              (WU, 1, room_at), (WD, 0, rows_at), (WD, 1, room_at)]
    psG = [ps(f"psG{i}", [P, C], F32, ctx) for i in range(2)]
    psU = [ps(f"psU{i}", [P, C], F32, ctx) for i in range(2)]
    psY = [ps(f"psY{i}", [P, C], F32, ctx) for i in range(2)]
    s_ht, s_w = g["s_ht"], g["s_w"]
    s_whi, s_wlo_d, s_wlo_p, s_hthi, s_htlo, s_hhi, s_hlo = (
        sem("h_" + n) for n in ("whi", "wlo_d", "wlo_p", "hthi", "htlo", "hhi", "hlo"))
    s_stored = [sem(f"h_stored{i}") for i in range(2)]
    s_gate, s_up, s_silu, s_hid, s_down, s_add = (sem("h_" + n) for n in ("gate", "up", "silu", "hid", "down", "add"))

    PR = B("PR", [P, NT, E])
    iota_i = PR[:, 0:P // E].rearrange("p t e -> p (t e)").bitcast(I32)
    iota_e = g["X"][:, 15, 0:P]
    iota_pi = B("iota_pi", [P, 1], I32)
    iota_p = B("iota_p", [P, 1])
    before = g["X"][:, 15, P:2 * P]
    OH = B("OH", [P, NT, TOPK, E], BF16)
    M = B("M", [P, NT, E])
    MP = B("MP", [P, NT + 1, E])
    X = g["X"]
    R = X[:, 13:15].rearrange("p t c -> p (t c)").rearrange("p (t e) -> p t e", e=E)
    cnt_i = B("cnt_i", [P, E], I32)
    tiles = B("tiles", [P, E])
    incl = B("incl", [P, E])
    base = B("base", [P, E])
    GATE = B("GATE", [P, NT, TOPK])
    DG = R
    POSI = B("POSI", [P, NT, TOPK], I32)
    empty = PR[:, 0:P // E].rearrange("p t e -> p (t e)")
    zeros = M[:].rearrange("p t e -> p (t e)")[:, 0:C + E]
    lk = B("lk", [P, NT, TOPK])
    mxk = B("mxk", [P, NT])
    sumk = B("sumk", [P, NT])
    posf = B("posf", [P, NT, TOPK])
    eid_f = B("eid_f", [P, 1])
    eid_i = B("eid_i", [P, 1], I32)
    cmp_e = B("cmp_e", [P, E])
    slot_i, slot_f = (g["X"][:, 15, i * P:(i + 1) * P].rearrange("p (s t k) -> p s t k", s=2, k=TOPK) for i in (2, 3))
    slot_i = slot_i.bitcast(I32)
    place = room[:, 0:512].bitcast(BF16).rearrange("p (b k n) -> p b k n", b=2, k=TOPK)
    where = room[:, 512:1536].rearrange("p (b k n) -> p b k n", b=2, k=TOPK)
    token = room[:, 1536:2560].bitcast(BF16).rearrange("p (b s k n) -> p b s k n", b=2, s=2, k=TOPK)
    psR = [ps(f"psR{i}", [P, C], F32, ctx) for i in range(2)]
    s_zero, s_pad, s_dense, s_dstored = (sem("d_" + n) for n in ("zero", "pad", "dense", "dstored"))
    s_iota, s_bef, s_cnt, s_rank, s_d, s_lk, s_ek, s_eid, s_seen, s_place, s_table, s_toks = (
        sem("d_" + n) for n in ("iota", "bef", "cnt", "rank", "d", "lk", "ek", "eid", "seen", "place", "table", "toks"))
    COUNT_AT, RANK_AT, TABLE_AT = 5, 8, 16

    with nc.Block() as block:
        @block.sync
        def _(sp):
            def rows_in(n):
                sp.wait_ge(s_hthi, n)
                sp.wait_ge(s_htlo, n)
                sp.dma_start(HTin, g["h2t_cols"][n * GT:(n + 1) * GT].rearrange("t p k n -> p t k n")).then_inc(s_ht, 16)

            def weights_in(i, src, *split):
                for sem_, value in split:
                    sp.wait_ge(sem_, value)
                sp.dma_start(pieces[i][2].rearrange("p (k n) -> p k n", k=KC), src).then_inc(s_w[i], 16)

            wg_v = g["swg"].rearrange("s (p k) h -> s p k h", k=KC)
            wu_v = g["swu"].rearrange("s (p k) h -> s p k h", k=KC)
            wd_v = g["swd"].rearrange("s (c p) n -> s p c n", p=P)
            weights_in(2, wg_v[1], (s_hthi, 1), (s_htlo, 1))
            weights_in(3, wu_v[1], (s_whi, 1), (s_wlo_d, 1))
            weights_in(4, wd_v[0], (s_whi, 3), (s_wlo_d, 2))
            weights_in(5, wd_v[1], (s_whi, 4), (s_wlo_p, 2))
            sp.wait_ge(s_whi, 5)
            sp.wait_ge(s_wlo_p, 3)
            rows_in(1)
            sp.wait_ge(s_eid, 1)
            sp.dma_start(g["tile_expert"].rearrange("a p -> p a"), eid_i[:]).then_inc(g["s_tile_expert"], 16)
            sp.wait_ge(g["s_tile_expert"], 16)
            sp.dma_start(g["eid_row"][:], g["tile_expert"]).then_inc(g["s_tile_expert"], 16)
            sp.wait_ge(g["s_tile_expert"], 32)
            rows_in(2)
            sp.wait_ge(s_dense, 1)
            sp.dma_start(g["h2_rows"][0:NT, :, C:].rearrange("t p e -> p t e"), DG).then_inc(s_dstored, 16)
            sp.wait_ge(s_zero, 1)
            sp.dma_start(g["h2_rows"][NT], zeros).then_inc(s_pad, 16)
            sp.dma_start(g["total"][0][NT], zeros[:, 0:C]).then_inc(s_pad, 16)
            sp.dma_start(g["total"][1][NT], zeros[:, 0:C]).then_inc(s_pad, 16)
            sp.wait_ge(s_pad, 16 * 3)
            sp.wait_ge(s_dstored, 16)
            for n in range(3, NG):
                rows_in(n)

        @block.tensor
        def _(pe):
            def up(n, c):
                i = n * NCH + c
                s = c // HC
                for w, bank, done, split in ((WG, psG, s_gate, s_wlo_d), (WU, psU, s_up, s_wlo_p)):
                    if i >= 2:
                        pe.wait_ge(s_hid, i - 1)
                    if n == 0 and c % HC == 0:
                        pe.wait_ge(s_whi, 2 * s + (1 if w is WG else 2))
                        pe.wait_ge(split, s + 1)
                    for k in range(KC):
                        for a, b in PARTS:
                            ins = pe.matmul(bank[i % 2][:].rearrange("p (t n) -> p t n", t=GT),
                                            w[:, a, s, k, (c % HC) * P:(c % HC + 1) * P],
                                            HT[:, b, :, k, :], start=(k == 0 and a + b == 0),
                                            stop=(k == KC - 1 and a == 1))
                    ins.then_inc(done, 1)

            def dispatch_step(m):
                if m == COUNT_AT:
                    pe.wait_ge(s_cnt, 1)
                    pe.wait_ge(s_bef, 2)
                    pe.matmul(psR[0][:, 0:E], g["ones"][:], MP[:, NT, :], start=True, stop=True).then_inc(s_rank, 1)
                if m == RANK_AT:
                    for h in (1, 0):
                        if h == 0:
                            pe.wait_ge(s_seen, 1)
                        t = slice(h * NT // 2, (h + 1) * NT // 2)
                        bank = psR[h][:].rearrange("p (t e) -> p t e", e=E)
                        pe.matmul(bank, before, M[:, t, :], start=True, stop=False)
                        pe.matmul(bank, g["ones"][:], MP[:, t, :], start=False, stop=True).then_inc(s_rank, 1)
                if m > TABLE_AT + 1:
                    t = m - TABLE_AT - 2
                    if t == 0:
                        pe.wait_ge(s_seen, 2)
                    pe.wait_ge(s_place, t + 1)
                    for k in range(TOPK):
                        for half in range(2):
                            ins = pe.matmul(psR[1][:, 0:P], place[:, t % 2, k], token[:, t % 2, half, k],
                                            start=(t + k + half == 0), stop=(t == NT - 1 and k == TOPK - 1 and half == 1))
                    ins.then_inc(s_table, 1)

            for n in range(NG):
                pe.wait_ge(s_hthi, n + 1)
                pe.wait_ge(s_htlo, n + 1)
                for c in range(NCH):
                    up(n, c)
                    dispatch_step(n * NCH + c)
                if n == NG - 1:
                    dispatch_step(STEPS)
                if n == 0:
                    pe.wait_ge(s_whi, 6)
                    pe.wait_ge(s_wlo_p, 4)
                pe.wait_ge(s_hlo, NCH * (n + 1) - 1)
                for t in range(GT):
                    i = n * GT + t
                    if i >= 2:
                        pe.wait_ge(s_add, i - 1)
                    for c in range(NCH):
                        if t == 0 and c == NCH - 1:
                            pe.wait_ge(s_hlo, NCH * (n + 1))
                        for a, b in PARTS:
                            ins = pe.matmul(psY[i % 2][:], hid[:, a, c, t * P:(t + 1) * P], WD[:, b, c // HC, c % HC, :],
                                            start=(c + a + b == 0), stop=(c == NCH - 1 and a == 1))
                    ins.then_inc(s_down, 1)
                    if i == NT - GT:
                        dispatch_step(STEPS + 1)

        @block.scalar
        def _(act):
            def high_rows(n):
                act.wait_ge(s_ht, 16 * (n + 1))
                if n:
                    act.wait_ge(s_up, NCH * n)
                act.activation(HT[:, 0].rearrange("p t k n -> p (t k n)"), HTin.rearrange("p t k n -> p (t k n)"),
                               ACT.Copy).then_inc(s_hthi, 1)

            def high_weights(i):
                w, s, src = pieces[i]
                act.wait_ge(s_w[i], 16)
                act.activation(whole(w, 0, s), src, ACT.Copy).then_inc(s_whi, 1)

            def store(t):
                act.wait_ge(s_add, t + 1)
                act.dma_start(g["total"][1][t], tmp[:, t % 2]).then_inc(s_stored[t % 2], 16)

            high_rows(0)
            for i in range(2):
                high_weights(i)
            for n in range(NG):
                for c in range(NCH):
                    i = n * NCH + c
                    act.wait_ge(s_gate, i + 1)
                    if i >= 2:
                        act.wait_ge(s_hlo, i - 1)
                    if i == 0:
                        act.wait_ge(s_wlo_p, 1)
                    act.activation(sg[:, i % 2], psG[i % 2][:], ACT.Silu).then_inc(s_silu, 1)
                    act.wait_ge(s_hid, i + 1)
                    if n and c == 0:
                        act.wait_ge(s_down, GT * n)
                    act.activation(hid[:, 0, c], sg[:, i % 2], ACT.Copy).then_inc(s_hhi, 1)
                    if n == 0 and c < 4:
                        high_weights(2 + c)
                    if i == RANK_AT:
                        act.wait_ge(s_lk, 1)
                        act.activation(lk[:], lk[:], ACT.Exp).then_inc(s_ek, 1)
                if n < NG - 1:
                    high_rows(n + 1)
                for t in range(n * GT, (n + 1) * GT):
                    store(t)
            for b in range(2):
                act.wait_ge(s_stored[b], 16 * NT // 2)

        @block.vector
        def _(dve):
            ch = Chain(dve, s_d)

            def chosen(dst, k, src):
                ch.last()
                ch.step(dve.tensor_tensor(PR[:], OH[:, :, k, :], src, ALU.mult))
                ch.last()
                ch.step(dve.tensor_reduce(dst[:, :, k:k + 1].rearrange("p t a -> p (t a)"), PR[:], AX.X, ALU.add))

            def dispatch_step(m):
                if m == 0:
                    dve.wait_ge(s_iota, 2)
                    ch.step(dve.tensor_copy(iota_e, iota_i))
                    ch.step(dve.tensor_copy(iota_p[:], iota_pi[:]))
                    ch.step(dve.memset(MP[:, 0, :], 0.0))
                    ch.last()
                if m < 2:
                    for k in (2 * m, 2 * m + 1):
                        ch.step(dve.tensor_tensor(OH[:, :, k, :], iota_e[:, 0:E].unsqueeze(1).broadcast_to([P, NT, E]),
                                                  EIDX[:, :, k:k + 1].broadcast_to([P, NT, E]), ALU.is_equal))
                if m == 2:
                    ch.last()
                    ch.step(dve.tensor_tensor(M[:], OH[:, :, 0, :], OH[:, :, 1, :], ALU.add))
                    for k in range(2, TOPK):
                        ch.last()
                        ch.step(dve.tensor_tensor(M[:], M[:], OH[:, :, k, :], ALU.add))
                if m == 3:
                    for t in range(NT):
                        ch.last()
                        ins = dve.tensor_tensor(MP[:, t + 1, :], MP[:, t, :], M[:, t, :], ALU.add)
                        if t < NT - 1:
                            ch.step(ins)
                    ins.then_inc(s_cnt, 1)
                if 4 <= m < 7:
                    for k in {4: (0,), 5: (1,), 6: (2, 3)}[m]:
                        chosen(lk, k, LG[:])
                if m == 7:
                    ch.last()
                    ch.step(dve.tensor_reduce(mxk[:], lk[:], AX.X, ALU.max))
                    ch.last()
                    dve.tensor_tensor(lk[:], lk[:], mxk[:].unsqueeze(2).broadcast_to([P, NT, TOPK]), ALU.subtract).then_inc(s_lk, 1)
                if m == 9:
                    dve.wait_ge(s_ek, 1)
                    ch.step(dve.tensor_reduce(sumk[:], lk[:], AX.X, ALU.add))
                    ch.last()
                    ch.step(dve.reciprocal(sumk[:], sumk[:]))
                    ch.last()
                    ch.step(dve.tensor_tensor(GATE[:], lk[:], sumk[:].unsqueeze(2).broadcast_to([P, NT, TOPK]), ALU.mult))
                if m == 8:
                    dve.wait_ge(s_rank, 1)
                    dve.tensor_scalar(cnt_i[:], psR[0][:, 0:E], 1.0, float(P - 1), ALU.max, ALU.add).then_inc(s_seen, 1)
                    dve.wait_ge(s_seen, 1)
                    ch.step(dve.tensor_scalar(cnt_i[:], cnt_i[:], 7, None, ALU.arith_shift_right))
                    ch.last()
                    ch.step(dve.tensor_copy(tiles[:], cnt_i[:]))
                    ch.step(dve.memset(base[:], 1.0))
                    ch.last()
                    ch.step(dve.tensor_tensor_scan(incl[:], base[:], tiles[:], 0.0, ALU.mult, ALU.add))
                    ch.last()
                    ch.step(dve.tensor_tensor(base[:], incl[:], tiles[:], ALU.subtract))
                    ch.step(dve.tensor_copy(g["end_row"][:], incl[0:1, :]))
                    ch.step(dve.tensor_scalar(g["pairs"][:], incl[0:1, E - 1:E], 1.0, None, ALU.add))
                    ch.last()
                    ch.step(dve.tensor_scalar(g["pairs"][:], g["pairs"][:], 1, None, ALU.arith_shift_right))
                if m == 10:
                    ch.step(dve.tensor_scalar(cmp_e[:], incl[:], iota_p[:], None, ALU.is_le))
                    ch.last()
                    ch.step(dve.tensor_reduce(eid_f[:], cmp_e[:], AX.X, ALU.add))
                    ch.step(dve.tensor_scalar(base[:], base[:], float(P), None, ALU.mult))
                    ch.last()
                    dve.tensor_scalar(eid_i[:], eid_f[:], float(E - 1), None, ALU.min).then_inc(s_eid, 1)
                if m == 11:
                    dve.wait_ge(s_rank, 3)
                    for h in range(2):
                        t = slice(h * NT // 2, (h + 1) * NT // 2)
                        ins = dve.tensor_tensor(R[:, t, :], psR[h][:].rearrange("p (t e) -> p t e", e=E),
                                                base[:].unsqueeze(1).broadcast_to([P, NT // 2, E]), ALU.add)
                        if h == 0:
                            ch.step(ins)
                    ins.then_inc(s_seen, 1)
                    dve.wait_ge(s_seen, 2)
                if 12 <= m < 15:
                    for k in {12: (0,), 13: (1,), 14: (2, 3)}[m]:
                        chosen(posf, k, R)
                if m == 15:
                    ch.last()
                    ch.step(dve.tensor_copy(POSI[:], posf[:]))
                    ch.last()
                    ch.step(dve.tensor_scalar(slot_i[:, 0], POSI[:], 7, None, ALU.arith_shift_right))
                    ch.step(dve.tensor_scalar(slot_i[:, 1], POSI[:], P - 1, None, ALU.bitwise_and))
                    ch.last()
                    ch.step(dve.tensor_copy(slot_f, slot_i))
                if m in (TABLE_AT, TABLE_AT + 1):
                    for k in range(2 * (m - TABLE_AT), 2 * (m - TABLE_AT) + 2):
                        ch.last()
                        ins = dve.tensor_tensor(DG if k == 0 else PR[:], OH[:, :, k, :],
                                                GATE[:, :, k:k + 1].broadcast_to([P, NT, E]), ALU.mult)
                        ch.step(ins)
                        if k:
                            ch.last()
                            ins = dve.tensor_tensor(DG, DG, PR[:], ALU.add)
                            if k < TOPK - 1:
                                ch.step(ins)
                            else:
                                ins.then_inc(s_dense, 1)
                if m >= TABLE_AT:
                    t = m - TABLE_AT
                    ch.last()
                    if t >= 2:
                        dve.wait_ge(s_table, t - 1)
                    columns = iota_e.unsqueeze(1).broadcast_to([P, TOPK, P])
                    dve.tensor_tensor(place[:, t % 2], columns,
                                      slot_f[:, 1, t, :].unsqueeze(2).broadcast_to([P, TOPK, P]), ALU.is_equal)
                    ch.step(dve.tensor_tensor(where[:, t % 2], columns,
                                              slot_f[:, 0, t, :].unsqueeze(2).broadcast_to([P, TOPK, P]), ALU.is_equal))
                    ch.last()
                    ch.step(dve.tensor_scalar(token[:, t % 2, 0], where[:, t % 2], iota_p[:], None, ALU.mult))
                    dve.tensor_scalar(token[:, t % 2, 1], where[:, t % 2], float(t * P - T), None, ALU.mult).then_inc(s_place, 1)

            def token_table():
                dve.memset(g["TOKI"][:, MAXT:], 0).then_inc(s_toks, 1)
                dve.wait_ge(s_table, NT)
                ch.step(dve.tensor_scalar(empty, psR[1][:, 0:P], 0.0, iota_p[:], ALU.is_equal, ALU.mult))
                ch.last()
                dve.scalar_tensor_tensor(out=g["TOKI"][:, 0:MAXT], in0=psR[1][:, 0:P], scalar=float(T), in1=empty,
                                         op0=ALU.add, op1=ALU.add).then_inc(s_toks, 1)

            def low_rows(n):
                dve.wait_ge(s_hthi, n + 1)
                dve.tensor_tensor(HT[:, 1], HTin, HT[:, 0].bitcast(F32), ALU.subtract).then_inc(s_htlo, 1)

            def low_hidden(c, i):
                dve.wait_ge(s_hhi, i + 1)
                dve.tensor_tensor(hid[:, 1, c], sg[:, i % 2], hid[:, 0, c].bitcast(F32), ALU.subtract).then_inc(s_hlo, 1)

            def low_weights(i):
                w, s, src = pieces[i]
                dve.wait_ge(s_whi, i + 1)
                dve.tensor_tensor(whole(w, 1, s), src, whole(w, 0, s).bitcast(F32), ALU.subtract).then_inc(s_wlo_d, 1)

            low_rows(0)
            low_weights(0)
            for n in range(NG):
                for c in range(NCH):
                    i = n * NCH + c
                    dve.wait_ge(s_silu, i + 1)
                    dve.wait_ge(s_up, i + 1)
                    dve.tensor_tensor(sg[:, i % 2], sg[:, i % 2], psU[i % 2][:], ALU.mult).then_inc(s_hid, 1)
                    if c == NCH - 1:
                        low_hidden(c, i)
                        if n < NG - 1:
                            low_rows(n + 1)
                        dispatch_step(i)
                    else:
                        dispatch_step(i)
                        low_hidden(c, i)
                    if i == 0:
                        low_weights(2)
                for t in range(GT):
                    i = n * GT + t
                    if i == NT - GT + 1:
                        token_table()
                    dve.wait_ge(s_down, i + 1)
                    if i >= 2:
                        dve.wait_ge(s_stored[i % 2], 16 * (i // 2))
                    dve.tensor_tensor(tmp[:, i % 2], psY[i % 2][:], g["gb_row"][:], ALU.mult).then_inc(s_add, 1)

        @block.gpsimd
        def _(pool):
            pool.iota(iota_i, pattern=[[1, P]], base=0, channel_multiplier=0).then_inc(s_iota, 1)
            pool.iota(iota_pi[:], pattern=[[0, 1]], base=0, channel_multiplier=1).then_inc(s_iota, 1)
            pool.memset(before, 1.0).then_inc(s_bef, 1)
            pool.wait_ge(s_bef, 1)
            pool.affine_select(out=before, in_=before, compare_op=ALU.is_ge, fill=0.0, base=-1,
                               pattern=[[1, P]], channel_multiplier=-1).then_inc(s_bef, 1)
            for i in (1, 3, 4, 5):
                w, s, src = pieces[i]
                pool.wait_ge(s_whi, i + 1)
                pool.tensor_tensor(whole(w, 1, s), src, whole(w, 0, s).bitcast(F32), ALU.subtract).then_inc(s_wlo_p, 1)
            pool.wait_ge(s_rank, 3)
            pool.memset(zeros, 0.0).then_inc(s_zero, 1)


def routed_experts(nc, ctx, sb, ps, sem, g):
    B = lambda name, shape, dt=F32: sb(name, shape, dt, ctx)
    RING = 8
    DEEP = 4
    ident = g["ident"]
    W = B("W", [P, RING, 2, KC, F])
    WD = B("rWD", [P, RING, C])
    XT = B("rX", [P, DEEP, C + E])
    weight = B("weight", [P, 2])
    xT = B("rxT", [P, 2, KC, P])
    sg = B("rsg", [P, 2, F])
    hid = B("rhid", [P, 2, F])
    hT = B("rhT", [P, 2, P])
    Y = B("rY", [P, DEEP, C])
    psX = [ps(f"rpX{i}", [P, KC * P], F32, ctx) for i in range(2)]
    psGU = [ps(f"rpG{i}", [P, 2, F], F32, ctx) for i in range(2)]
    psH = ps("rpH", [P, P], F32, ctx)
    psY = [ps(f"rpY{i}", [P, C], F32, ctx) for i in range(2)]
    s_w = [sem(f"r_w{i}") for i in range(RING)]
    s_x = [sem(f"r_x{i}") for i in range(DEEP)]
    ends = B("ends", [1, RING], I32)
    tok = B("tok", [P, DEEP], I32)
    to = B("to", [P, 2], I32)
    s_added = [sem(f"r_added{i}") for i in range(2)]
    s_ends, s_tok, s_to, s_weight = (sem("r_" + n) for n in ("ends", "tok", "to", "weight"))
    s_wready, s_tr, s_xt, s_gu, s_silu, s_h, s_ht, s_hc, s_down, s_y = (
        sem("r_" + n) for n in ("wready", "tr", "xt", "gu", "silu", "h", "ht", "hc", "down", "y"))
    wg_v = g["wg"].rearrange("e (p k) f -> e p (k f)", k=KC)
    wu_v = g["wu"].rearrange("e (p k) f -> e p (k f)", k=KC)
    MAXPAIRS, MINPAIRS = MAXT // 2, E // 2

    def sweep(eng, step, drain, begin=None):
        pairs = eng.value_load(g["pairs"][0:1, 0:1], min_val=MINPAIRS, max_val=MAXPAIRS)

        def run(h, n):
            if begin:
                begin(2 * n)
            for i in range(n):
                for b in range(2):
                    step(h + i, (2 * i + b) % DEEP)
        run(0, 4)
        with eng.Fori(1, MINPAIRS // 4) as o:
            run(o * 4, 4)
        with eng.If(pairs == MINPAIRS):
            drain(MINPAIRS, 0)
        with eng.Fori(MINPAIRS // 2, MAXPAIRS // 2) as q:
            with eng.If(q * 2 + 1 < pairs):
                run(q * 2, 2)
                with eng.If(q * 2 + 2 == pairs):
                    drain(q * 2 + 2, 0)
            with eng.If(q * 2 + 1 == pairs):
                run(q * 2, 1)
                drain(q * 2 + 1, 2)

    with nc.Block() as block:
        @block.sync
        def _(sp):
            def load(i, b):
                e = i * RING + b
                if not (isinstance(i, int) and i == 0):
                    sp.wait_ge(s_down, sp.value_load(ends[0:1, b:b + 1], min_val=1, max_val=MAXT))
                one = bass.ds(e, 1)
                sp.dma_start(W[:, b, 0].rearrange("p k f -> p (k f)"), wg_v[one].rearrange("a p n -> (a p) n")).then_inc(s_w[b], 16)
                sp.dma_start(W[:, b, 1].rearrange("p k f -> p (k f)"), wu_v[one].rearrange("a p n -> (a p) n")).then_inc(s_w[b], 16)
                sp.dma_start(WD[:, b], g["wd"][one].rearrange("a p n -> (a p) n")).then_inc(s_w[b], 16)

            def landed(i, b):
                sp.wait_ge(s_w[b], 48 * (i + 1))
                sp.sem_inc(s_wready, 1)

            LAG = RING // 2
            for b in range(RING):
                load(0, b)
                if b >= LAG:
                    landed(0, b - LAG)
            with sp.Fori(1, E // RING) as i:
                sp.dma_start(ends[:], g["end_row"][0:1, bass.ds((i - 1) * RING, RING)]).then_inc(s_ends, 16)
                sp.wait_ge(s_ends, 16 * i)
                hold(sp, g)
                for b in range(RING):
                    load(i, b)
                    if b >= LAG:
                        landed(i, b - LAG)
                    else:
                        landed(i - 1, b + RING - LAG)
            for b in range(RING - LAG, RING):
                landed(E // RING - 1, b)

        @block.gpsimd
        def _(pool):
            def gather(t, r):
                wait(pool, s_tr, t - DEEP + 1)
                wait(pool, s_weight, t - DEEP + 1)
                hold(pool, g)
                pool.tensor_copy(tok[:, r:r + 1], g["TOKI"][:, bass.ds(t, 1)]).then_inc(s_tok, 1)
                pool.wait_ge(s_tok, t + 1)
                hold(pool, g)
                pool.indirect_dma_start(out=XT[:, r], out_offset=None, in_=g["h2_rows"].rearrange("t p c -> (t p) c"),
                                        in_offset=bass.IndirectOffsetOnAxis(ap=tok[:, r:r + 1], axis=0)).then_inc(s_x[r], 16)

            def scatter(h, r):
                b = r % 2
                t = h * 2 + b
                wait(pool, s_added[b], 16 * h)
                hold(pool, g)
                pool.tensor_copy(to[:, b:b + 1], g["TOKI"][:, bass.ds(t, 1)]).then_inc(s_to, 1)
                pool.wait_ge(s_to, t + 1)
                pool.wait_ge(s_y, t + 1)
                hold(pool, g)
                pool.indirect_dma_start(out=g["total"][b].rearrange("t p c -> (t p) c"),
                                        out_offset=bass.IndirectOffsetOnAxis(ap=to[:, b:b + 1], axis=0),
                                        in_=Y[:, r], in_offset=None, compute_op=ALU.add).then_inc(s_added[b], 16)

            def step(h, r):
                t = h * 2 + r % 2
                if not (isinstance(h, int) and t < 3):
                    scatter(h - 2 + r % 2, (r + 1) % DEEP)
                gather(t + DEEP, r)

            def drain(pairs, r):
                scatter(pairs - 2, (r + 1) % DEEP)
                scatter(pairs - 1, (r + 2) % DEEP)
                scatter(pairs - 1, (r + 3) % DEEP)
                for b in range(2):
                    pool.wait_ge(s_added[b], pairs * 16)
                for i in range(DEEP):
                    pool.wait_ge(s_x[i], (pairs // 2 + 1 + (r == 2 and i < 2)) * 16)
                hold(pool, g)
            for r in range(DEEP):
                gather(r, r)
            sweep(pool, step, drain)

        @block.tensor
        def _(pe):
            experts = {}

            def begin(n):
                experts.clear()
                experts["steps"] = n

            def expert(t):
                return pe.value_load(g["eid_row"][0:1, bass.ds(t, 1)], min_val=0, max_val=E - 1)

            def rows(t, r):
                b = r % 2
                pe.wait_ge(s_x[r], 16 * (t // DEEP + 1))
                wait(pe, s_xt, t - 1)
                for k in range(KC):
                    ins = pe.transpose(psX[b][:, k * P:(k + 1) * P], XT[:, r, k:C:KC], ident[:])
                ins.then_inc(s_tr, 1)

            def gate_up(t, b, e):
                pe.wait_ge(s_xt, t + 1)
                wait(pe, s_h, t - 1)
                slot = bass.ds(e % RING, 1)
                for k in range(KC):
                    ins = pe.matmul(psGU[b][:], xT[:, b, k, :], W[:, slot, :, k, :].rearrange("p a s f -> p (a s) f"),
                                    start=(k == 0), stop=(k == KC - 1))
                ins.then_inc(s_gu, 1)

            def hidden(t, b):
                pe.wait_ge(s_h, t + 1)
                wait(pe, s_hc, t)
                pe.transpose(psH[:], hid[:, b], ident[:]).then_inc(s_ht, 1)

            def down(t, b, e):
                pe.wait_ge(s_hc, t + 1)
                wait(pe, s_y, t - 1)
                pe.matmul(psY[b][:], hT[:, b], WD[:, bass.ds(e % RING, 1)].rearrange("p a n -> p (a n)"),
                          start=True, stop=True).then_inc(s_down, 1)

            def step(h, r):
                b = r % 2
                t = h * 2 + b
                if "next" in experts:
                    e1, e2 = experts["next"], experts["last"]
                else:
                    e1 = None if isinstance(h, int) and t == 0 else expert(t - 1)
                    e2 = None if isinstance(h, int) and t == 0 else expert(t - 2)
                if e1 is not None:
                    pe.wait_ge(s_wready, e1 + 1)
                rows(t, r)
                if e2 is not None:
                    hidden(t - 2, b)
                if e1 is not None:
                    gate_up(t - 1, 1 - b, e1)
                experts["steps"] -= 1
                if experts["steps"]:
                    experts["next"], experts["last"] = expert(t), e1
                if e2 is not None:
                    down(t - 2, b, e2)

            def drain(pairs, r):
                T2 = pairs * 2
                e1, e2 = expert(T2 - 1), expert(T2 - 2)
                pe.wait_ge(s_wready, e1 + 1)
                hidden(T2 - 2, 0)
                gate_up(T2 - 1, 1, e1)
                down(T2 - 2, 0, e2)
                hidden(T2 - 1, 1)
                down(T2 - 1, 1, e1)
            sweep(pe, step, drain, begin)

        @block.scalar
        def _(act):
            def rows(t, b):
                act.wait_ge(s_tr, t + 1)
                wait(act, s_gu, t - 1)
                act.activation(xT[:, b].rearrange("p k n -> p (k n)"), psX[b][:], ACT.Copy).then_inc(s_xt, 1)

            def silu(t, b):
                act.wait_ge(s_gu, t + 1)
                wait(act, s_h, t - 1)
                act.activation(sg[:, b], psGU[b][:, 0, :], ACT.Silu).then_inc(s_silu, 1)

            def step(h, r):
                b = r % 2
                t = h * 2 + b
                rows(t, b)
                if not (isinstance(h, int) and t == 0):
                    silu(t - 1, 1 - b)

            def drain(pairs, r):
                silu(pairs * 2 - 1, 1)
            sweep(act, step, drain)

        @block.vector
        def _(dve):
            def weights(t, r):
                e = dve.value_load(g["eid_row"][0:1, bass.ds(t, 1)], min_val=0, max_val=E - 1)
                b = r % 2
                dve.wait_ge(s_x[r], 16 * (t // DEEP + 1))
                wait(dve, s_h, t - 1)
                dve.tensor_copy(weight[:, b:b + 1], XT[:, r, bass.ds(C + e, 1)]).then_inc(s_weight, 1)

            def mult(t, b):
                dve.wait_ge(s_silu, t + 1)
                wait(dve, s_ht, t - 1)
                dve.wait_ge(s_weight, t + 1)
                dve.scalar_tensor_tensor(out=hid[:, b], in0=sg[:, b], scalar=weight[:, b:b + 1], in1=psGU[b][:, 1, :],
                                         op0=ALU.mult, op1=ALU.mult).then_inc(s_h, 1)

            def hidden(t, b):
                dve.wait_ge(s_ht, t + 1)
                wait(dve, s_down, t - 1)
                dve.tensor_copy(hT[:, b], psH[:]).then_inc(s_hc, 1)

            def output(h, r):
                b = r % 2
                dve.wait_ge(s_down, h * 2 + b + 1)
                wait(dve, s_added[b], 16 * (h - 1))
                dve.tensor_tensor(Y[:, r], psY[b][:], g["gb_row"][:], ALU.mult).then_inc(s_y, 1)

            def step(h, r):
                b = r % 2
                t = h * 2 + b
                weights(t, r)
                if not (isinstance(h, int) and h == 0):
                    hidden(t - 2, b)
                if not (isinstance(h, int) and t == 0):
                    mult(t - 1, 1 - b)
                if not (isinstance(h, int) and h == 0):
                    output(h - 1, (r + 2) % DEEP)

            def drain(pairs, r):
                T2 = pairs * 2
                hidden(T2 - 2, 0)
                mult(T2 - 1, 1)
                output(pairs - 1, (r + 2) % DEEP)
                hidden(T2 - 1, 1)
                output(pairs - 1, (r + 3) % DEEP)
            sweep(dve, step, drain)


def finish(nc, ctx, sb, sem, g):
    PARTS = 8
    n = NT // PARTS
    X = g["X"]
    T1 = sb("T1", [P, NT, C], F32, ctx)
    s_totals = [sem(f"f_totals{i}") for i in range(PARTS)]
    s_sum, s_out = sem("f_sum"), sem("f_out")
    with nc.Block() as block:
        def totals(eng, parts):
            for i in parts:
                t = slice(i * n, (i + 1) * n)
                for dst, src in ((X, g["total"][0]), (T1, g["total"][1])):
                    eng.dma_start(dst[:, t], src[t].rearrange("t p c -> p t c")).then_inc(s_totals[i], 16)

        @block.sync
        def _(sp):
            totals(sp, range(PARTS))

        @block.vector
        def _(dve):
            for i in range(PARTS):
                t = slice(i * n, (i + 1) * n)
                dve.wait_ge(s_totals[i], 32)
                dve.tensor_tensor(X[:, t], X[:, t], T1[:, t], ALU.add).then_inc(s_sum, 1)

        @block.scalar
        def _(act):
            for i in range(PARTS):
                t = slice(i * n, (i + 1) * n)
                act.wait_ge(s_sum, i + 1)
                act.dma_start(g["out_t"][:, t], X[:, t]).then_inc(s_out, 16)
            act.wait_ge(s_out, 16 * PARTS)


_INS = ["L0_attn_x", "L0_attn_Wq", "L0_attn_Wk", "L0_attn_Wv", "L0_attn_Wo", "L0_ffn_router_w", "L0_ffn_router_bias",
        "L0_ffn_wg", "L0_ffn_wu", "L0_ffn_wd", "L0_ffn_swg", "L0_ffn_swu", "L0_ffn_swd", "L0_c", "L0_wmod"]
_OUTS = [((1, T, C), "float32")]


def kernel(**inputs):
    import numpy as _np
    import concourse.bacc as _bacc
    from concourse import mybir as _mybir
    from concourse.bass_utils import run_bass_kernel_spmd as _run

    nc = _bacc.Bacc("TRN2", target_bir_lowering=False, num_devices=1)
    arrays, args = {}, []
    for name in _INS:
        a = _np.ascontiguousarray(inputs[name])
        arrays[f"in_{name}_dram"] = a
        args.append(nc.dram_tensor(f"in_{name}_dram", a.shape, _mybir.dt.from_np(a.dtype), kind="ExternalInput").ap())
    for i, (shape, dtype) in enumerate(_OUTS):
        dt = _mybir.dt.from_np(_np.dtype(dtype))
        args.append(nc.dram_tensor(f"out_{i}_dram", shape, dt, kind="ExternalOutput").ap())
    build_kernel(nc, *args)
    r = _run(nc, [arrays], core_ids=[0])
    got = tuple(r.results[0][f"out_{i}_dram"] for i in range(len(_OUTS)))
    return got[0]
```
